# Optimizing a Trainium2 kernel written in Bass

```python
import numpy as np
import jax
import jax.numpy as jnp

def _softmax(x, axis=-1):
    return jax.nn.softmax(x, axis=axis)

def _gelu(x):
    return jax.nn.gelu(x, approximate=True)

def _silu(x):
    return jax.nn.silu(x)

def _sigmoid(x):
    return jax.nn.sigmoid(x)

def _layernorm(x, axis=-1, eps=1e-05):
    m = jnp.mean(x, axis=axis, keepdims=True)
    v = jnp.var(x, axis=axis, keepdims=True)
    return (x - m) / jnp.sqrt(v + eps)

def _scatter_add(tgt, idx, src, axis=0):
    return tgt.at[idx].add(src)

def _segment_sum(src, seg, n):
    return jax.ops.segment_sum(src, seg, n)
kernel_name = 'mk_vit_tower_d1_tok_img256_r4_5ad12a'

def setup_inputs(seed: int=0):
    np.random.seed(seed)
    _w = jnp.asarray

    def _rec_inputs():
        import jax
        import jax.numpy as jnp
        _rk = jax.random.key(seed)
        x = 7.22013e-05 + 1.00017 * jax.random.normal(jax.random.fold_in(_rk, 1), (2, 64, 64, 64), jnp.float32)
        return x
    x = _rec_inputs()

    def _L0_tok_setup():
        import jax, jax.numpy as jnp
        import numpy as np
        B, C, H, W = (8, 64, 64, 64)
        NB = 3
        E = 64
        key = jax.random.key(seed)
        ks = jax.random.split(key, 6)
        x = jax.random.normal(ks[0], (B, C, H, W), dtype=jnp.float32)
        bases = jax.random.normal(ks[1], (C, NB), dtype=jnp.float32)
        W_spline = jax.random.normal(ks[2], (E, C * NB), dtype=jnp.float32) * (1.0 / np.sqrt(C * NB))
        b_spline = jax.random.normal(ks[3], (E,), dtype=jnp.float32) * 0.01
        W_base = jax.random.normal(ks[4], (E, C), dtype=jnp.float32) * (1.0 / np.sqrt(C))
        b_base = jax.random.normal(ks[5], (E,), dtype=jnp.float32) * 0.01
        return {'x': x, 'bases': bases, 'W_spline': W_spline, 'b_spline': b_spline, 'W_base': W_base, 'b_base': b_base}
    _L0_tok_all = _L0_tok_setup()
    _L0_tok_in = {k: v for k, v in _L0_tok_all.items() if k in ('bases', 'W_spline', 'b_spline', 'W_base', 'b_base')}
    del _L0_tok_all

    def _L0_attn_setup():
        import jax, jax.numpy as jnp
        import numpy as np
        B, N, D = (8, 512, 64)
        S = 128
        H = int(2.0 * D)
        EPS = 1e-05
        key = jax.random.key(seed)
        ks = jax.random.split(key, 4)
        x = jax.random.normal(ks[0], (B, N, D), dtype=jnp.float32)
        g = jnp.ones((), jnp.float32)
        W_uv = jax.random.normal(ks[1], (D, 2 * H + S), jnp.float32) * 0.02
        b_uv = jnp.zeros((2 * H + S,), jnp.float32)
        gamma = jnp.ones((2, S), jnp.float32)
        beta = jnp.zeros((2, S), jnp.float32)
        W_o = jax.random.normal(ks[2], (H, D), jnp.float32) * 0.02
        b_o = jnp.zeros((D,), jnp.float32)
        return {'x': x, 'g': g, 'W_uv': W_uv, 'b_uv': b_uv, 'gamma': gamma, 'beta': beta, 'W_o': W_o, 'b_o': b_o}
    _L0_attn_all = _L0_attn_setup()
    _L0_attn_in = {k: v for k, v in _L0_attn_all.items() if k in ('g', 'W_uv', 'b_uv', 'gamma', 'beta', 'W_o', 'b_o')}
    del _L0_attn_all

    def _L0_ffn_setup():
        import jax, jax.numpy as jnp
        import numpy as np
        B, T, C = (64, 96, 64)
        NH, NKV = (4, 2)
        HD = C // NH
        NREP = NH // NKV
        NE, TOPK = (8, 2)
        HID = int(8 / 3 * C)
        EPS_RMS = 1e-06

        def _rope_tables(t_len):
            inv_freq = 1.0 / 10000.0 ** (np.arange(0, HD, 2, dtype=np.float32) / HD)
            t = np.arange(t_len, dtype=np.float32)
            freqs = np.outer(t, inv_freq)
            emb = np.concatenate([freqs, freqs], axis=-1)
            return (jnp.asarray(np.cos(emb)), jnp.asarray(np.sin(emb)))

        def _rotate_half(x):
            h = x.shape[-1] // 2
            return jnp.concatenate([-x[..., h:], x[..., :h]], axis=-1)

        def _rmsnorm(v, w):
            return v * jax.lax.rsqrt(jnp.mean(v * v, axis=-1, keepdims=True) + EPS_RMS) * w
        key = jax.random.key(seed)
        ks = jax.random.split(key, 10)
        s = lambda k, shape: jax.random.normal(k, shape, jnp.float32) * 0.02
        return {'x': jax.random.normal(ks[0], (B, T, C), jnp.float32), 'ln1_w': jnp.ones((C,), jnp.float32), 'ln2_w': jnp.ones((C,), jnp.float32), 'wq': s(ks[1], (NH * HD, C)), 'wk': s(ks[2], (NKV * HD, C)), 'wv': s(ks[3], (NKV * HD, C)), 'wo': s(ks[4], (C, C)), 'router_w': s(ks[5], (NE, C)), 'w1': s(ks[6], (NE, HID, C)), 'w2': s(ks[7], (NE, C, HID)), 'w3': s(ks[8], (NE, HID, C))}
    _L0_ffn_all = _L0_ffn_setup()
    _L0_ffn_in = {k: v for k, v in _L0_ffn_all.items() if k in ('ln1_w', 'ln2_w', 'wq', 'wk', 'wv', 'wo', 'router_w', 'w1', 'w2', 'w3')}
    del _L0_ffn_all
    return {'x': x, 'L0_tok_bases': _L0_tok_in['bases'], 'L0_tok_W_spline': _L0_tok_in['W_spline'], 'L0_tok_b_spline': _L0_tok_in['b_spline'], 'L0_tok_W_base': _L0_tok_in['W_base'], 'L0_tok_b_base': _L0_tok_in['b_base'], 'L0_attn_g': _L0_attn_in['g'], 'L0_attn_W_uv': _L0_attn_in['W_uv'], 'L0_attn_b_uv': _L0_attn_in['b_uv'], 'L0_attn_gamma': _L0_attn_in['gamma'], 'L0_attn_beta': _L0_attn_in['beta'], 'L0_attn_W_o': _L0_attn_in['W_o'], 'L0_attn_b_o': _L0_attn_in['b_o'], 'L0_ffn_ln1_w': _L0_ffn_in['ln1_w'], 'L0_ffn_ln2_w': _L0_ffn_in['ln2_w'], 'L0_ffn_wq': _L0_ffn_in['wq'], 'L0_ffn_wk': _L0_ffn_in['wk'], 'L0_ffn_wv': _L0_ffn_in['wv'], 'L0_ffn_wo': _L0_ffn_in['wo'], 'L0_ffn_router_w': _L0_ffn_in['router_w'], 'L0_ffn_w1': _L0_ffn_in['w1'], 'L0_ffn_w2': _L0_ffn_in['w2'], 'L0_ffn_w3': _L0_ffn_in['w3']}

def reference(x, L0_tok_bases, L0_tok_W_spline, L0_tok_b_spline, L0_tok_W_base, L0_tok_b_base, L0_attn_g, L0_attn_W_uv, L0_attn_b_uv, L0_attn_gamma, L0_attn_beta, L0_attn_W_o, L0_attn_b_o, L0_ffn_ln1_w, L0_ffn_ln2_w, L0_ffn_wq, L0_ffn_wk, L0_ffn_wv, L0_ffn_wo, L0_ffn_router_w, L0_ffn_w1, L0_ffn_w2, L0_ffn_w3):
    import jax
    import jax.numpy as jnp

    def _L0_tok_ref(x, bases, W_spline, b_spline, W_base, b_base):
        import jax, jax.numpy as jnp
        import numpy as np
        B, C, H, W = (8, 64, 64, 64)
        NB = 3
        E = 64
        b, c, h, w = x.shape
        x_flat = jnp.transpose(x.reshape(b, c, h * w), (0, 2, 1))
        base_out = jnp.einsum('blc,ec->ble', jax.nn.silu(x_flat), W_base) + b_base
        spline = jax.nn.sigmoid(x_flat[..., None] * bases[None, None, :, :])
        spline_flat = spline.reshape(b, h * w, c * bases.shape[1])
        spline_proj = jnp.einsum('blk,ek->ble', spline_flat, W_spline) + b_spline
        return base_out + spline_proj

    def _L0_attn_ref(x, g, W_uv, b_uv, gamma, beta, W_o, b_o):
        import jax, jax.numpy as jnp
        import numpy as np
        B, N, D = (8, 512, 64)
        S = 128
        H = int(2.0 * D)
        EPS = 1e-05
        d = x.shape[-1]
        norm = jnp.linalg.norm(x, axis=-1, keepdims=True) * jax.lax.rsqrt(jnp.float32(d))
        xn = x / jnp.maximum(norm, EPS) * g
        uv = jax.nn.silu(jnp.einsum('bnd,de->bne', xn, W_uv) + b_uv)
        u = uv[..., :H]
        v = uv[..., H:2 * H]
        base = uv[..., 2 * H:]
        q = base * gamma[0] + beta[0]
        k = base * gamma[1] + beta[1]
        qk = jnp.einsum('bns,bms->bnm', q, k) * jax.lax.rsqrt(jnp.float32(S))
        attn = jnp.square(jax.nn.relu(qk))
        gated = u * jnp.einsum('bnm,bmh->bnh', attn, v)
        return jnp.einsum('bnh,hd->bnd', gated, W_o) + b_o

    def _L0_ffn_ref(x, ln1_w, ln2_w, wq, wk, wv, wo, router_w, w1, w2, w3):
        import jax, jax.numpy as jnp
        import numpy as np
        B, T, C = (64, 96, 64)
        NH, NKV = (4, 2)
        HD = C // NH
        NREP = NH // NKV
        NE, TOPK = (8, 2)
        HID = int(8 / 3 * C)
        EPS_RMS = 1e-06

        def _rope_tables(t_len):
            inv_freq = 1.0 / 10000.0 ** (np.arange(0, HD, 2, dtype=np.float32) / HD)
            t = np.arange(t_len, dtype=np.float32)
            freqs = np.outer(t, inv_freq)
            emb = np.concatenate([freqs, freqs], axis=-1)
            return (jnp.asarray(np.cos(emb)), jnp.asarray(np.sin(emb)))

        def _rotate_half(x):
            h = x.shape[-1] // 2
            return jnp.concatenate([-x[..., h:], x[..., :h]], axis=-1)

        def _rmsnorm(v, w):
            return v * jax.lax.rsqrt(jnp.mean(v * v, axis=-1, keepdims=True) + EPS_RMS) * w
        Bx, Tx, Cx = x.shape
        h = _rmsnorm(x, ln1_w)
        q = (h @ wq.T).reshape(Bx, Tx, NH, HD).transpose(0, 2, 1, 3)
        k = (h @ wk.T).reshape(Bx, Tx, NKV, HD).transpose(0, 2, 1, 3)
        v = (h @ wv.T).reshape(Bx, Tx, NKV, HD).transpose(0, 2, 1, 3)
        cos, sin = _rope_tables(Tx)
        cos, sin = (cos[None, None], sin[None, None])
        q = q * cos + _rotate_half(q) * sin
        k = k * cos + _rotate_half(k) * sin
        k = jnp.repeat(k, NREP, axis=1)
        v = jnp.repeat(v, NREP, axis=1)
        scores = jnp.einsum('bhtd,bhsd->bhts', q, k) / jnp.sqrt(jnp.float32(HD))
        causal = jnp.tril(jnp.ones((Tx, Tx), dtype=bool))
        scores = jnp.where(causal[None, None], scores, jnp.float32(-1e+30))
        att = jax.nn.softmax(scores, axis=-1)
        y = jnp.einsum('bhts,bhsd->bhtd', att, v).transpose(0, 2, 1, 3).reshape(Bx, Tx, Cx)
        x = x + y @ wo.T
        flat = _rmsnorm(x, ln2_w).reshape(-1, Cx)
        probs = jax.nn.softmax(flat @ router_w.T, axis=-1)
        tp, ti = jax.lax.top_k(probs, TOPK)
        tp = tp / (jnp.sum(tp, axis=-1, keepdims=True) + 1e-09)
        weights = jnp.sum(tp[..., None] * jax.nn.one_hot(ti, NE, dtype=flat.dtype), axis=1)
        out = jnp.zeros_like(flat)
        for e in range(NE):
            hh = jax.nn.silu(flat @ w1[e].T) * (flat @ w3[e].T)
            out = out + weights[:, e:e + 1] * (hh @ w2[e].T)
        return x + out.reshape(Bx, Tx, Cx)
    h = _L0_tok_ref(x, L0_tok_bases, L0_tok_W_spline, L0_tok_b_spline, L0_tok_W_base, L0_tok_b_base)
    h = h + _L0_attn_ref(_layernorm(h, axis=-1), L0_attn_g, L0_attn_W_uv, L0_attn_b_uv, L0_attn_gamma, L0_attn_beta, L0_attn_W_o, L0_attn_b_o)
    h = h + _L0_ffn_ref(_layernorm(h, axis=-1), L0_ffn_ln1_w, L0_ffn_ln2_w, L0_ffn_wq, L0_ffn_wk, L0_ffn_wv, L0_ffn_wo, L0_ffn_router_w, L0_ffn_w1, L0_ffn_w2, L0_ffn_w3)
    return h

_drawn_inputs = setup_inputs


def setup_inputs(seed=0):
    import zlib

    import numpy as np

    out = dict(_drawn_inputs(seed))
    spreads = {'L0_attn_b_uv': (0.0, 0.1),
     'L0_attn_gamma': (1.0, 0.6),
     'L0_attn_beta': (0.0, 0.696),
     'L0_attn_b_o': (0.0, 0.1),
     'L0_ffn_ln1_w': (1.0, 0.6),
     'L0_ffn_ln2_w': (1.0, 0.6)}
    factors = {'L0_tok_b_spline': 3.64,
     'L0_tok_b_base': 3.925,
     'L0_ffn_wq': 8.0,
     'L0_ffn_wk': 8.0,
     'L0_ffn_wv': 4.207,
     'L0_ffn_wo': 4.464,
     'L0_ffn_router_w': 8.0,
     'L0_ffn_w1': 8.0,
     'L0_ffn_w2': 8.0,
     'L0_ffn_w3': 8.0}
    for name, (base, spread) in spreads.items():
        noise = np.random.default_rng([zlib.crc32(name.encode()), seed]).standard_normal(out[name].shape)
        drawn = base * np.exp(spread * noise) if base else spread * noise
        out[name] = jnp.asarray(drawn.astype(out[name].dtype))
    for name, factor in factors.items():
        out[name] = (out[name] * factor).astype(out[name].dtype)
    return out
```

```python
from contextlib import ExitStack

import numpy as np

import concourse.bass as bass
from concourse import mybir

F32 = mybir.dt.float32
F32R = mybir.dt.float32r
BF16 = mybir.dt.bfloat16
ALU = mybir.AluOpType
ACT = mybir.ActivationFunctionType
AX = mybir.AxisListType

P = 128
BATCH, SEQ, C = 2, 4096, 64
TILES = BATCH * SEQ // P
BT = SEQ // P
CH = 512
CT = CH // P
CHUNKS = SEQ // CH
GH = 128
NH, NKV, HD = 4, 2, 16
QKV = (NH + 2 * NKV) * HD
ROPED = (NH + NKV) * HD
Q_PARTS = (0, 0, 1, 0, 2, 1)
K_PARTS = (0, 1, 0, 2, 0, 1)
STACK = len(Q_PARTS) * HD
SHIFT = 3
VW = 32
NE, TOPK, EHID = 8, 2, 170
HIDDEN = NE * EHID
HM = -(-HIDDEN // P)
LN_EPS, RMS_EPS, NORM_EPS = 1e-5, 1e-6, 1e-5


def bcast(ap, axis, n):
    a = ap.unsqueeze(axis)
    shape = list(a.shape)
    shape[axis] = n
    return a.broadcast_to(shape)


class Chain:

    def __init__(self, eng, sem):
        self.eng, self.sem, self.n, self.base = eng, sem, 0, None

    def then(self, ins):
        ins.then_inc(self.sem, 1)
        self.n += 1

    def ready(self):
        self.eng.wait_ge(self.sem, self.n if self.base is None else self.base + self.n)

    def enter(self, base):
        self.outer, self.base, self.n = self.n, base, 0

    def leave(self, per, times):
        assert self.n == per, self.n
        self.base, self.n = None, self.outer + per * times


class Scope:

    def __init__(self, nc, ctx, tag):
        self.nc, self.ctx, self.tag = nc, ctx, tag

    def sb(self, name, shape, dt=F32):
        return self.ctx.enter_context(self.nc.sbuf_tensor(f"{self.tag}.{name}", shape, dt))

    def ps(self, name, shape, dt=F32):
        return self.ctx.enter_context(self.nc.psum_tensor(f"{self.tag}.{name}", shape, dt))

    def sem(self, name):
        return self.ctx.enter_context(self.nc.semaphore(f"{self.tag}.{name}"))


def token_embedding(nc, d, H, XC, scale):
    W = 1024
    WT = W // P
    STEPS = SEQ // W
    with ExitStack() as ctx:
        m = Scope(nc, ctx, "tok")
        x2 = m.sb("x2", [P, BATCH, SEQ])
        wtok = m.sb("wtok", [P, 2, C])
        factor = m.sb("factor", [P, 2])
        biases = m.sb("biases", [P, 2, C])
        bias = m.sb("bias", [P, C])
        g = m.sb("g", [P, 1])
        feat = m.sb("feat", [P, 2, 2, W])
        square = m.sb("square", [P, TILES, C])
        sums = m.sb("sums", [P, TILES])
        mean = m.sb("mean", [P, TILES])
        var = m.sb("var", [P, TILES])
        shifted = m.sb("shifted", [P, TILES])
        root = m.sb("root", [P, 2, TILES])
        inv = m.sb("inv", [P, TILES])
        norm = m.sb("norm", [P, TILES])
        pH = m.ps("pH", [P, 2, 512])

        weights_in = m.sem("weights_in")
        x_in = [m.sem("x_in0"), m.sem("x_in1")]
        sigmoids_made = m.sem("sigmoids_made")
        silu_made = m.sem("silu_made")
        feat_free = m.sem("feat_free")
        h_ready = m.sem("h_ready")
        h_free = m.sem("h_free")
        var_made = m.sem("var_made")
        roots_made = m.sem("roots_made")
        dve_chain = m.sem("dve_chain")
        block = ctx.enter_context(nc.Block())

        @block.sync
        def _(sp):
            for b in range(BATCH):
                for half in (0, C):
                    sp.dma_start(x2[half:half + C, b, :], d["x"][b]).then_inc(x_in[b], 16)

        @block.scalar
        def _(act):
            act.dma_start(wtok[:], d["wtok"]).then_inc(weights_in, 16)
            act.dma_start(factor[:], d["tok_factor"]).then_inc(weights_in, 16)
            act.dma_start(biases[:, 0, :], d["b_base"].partition_broadcast(P)).then_inc(weights_in, 16)
            act.dma_start(biases[:, 1, :], d["b_spline"].partition_broadcast(P)).then_inc(weights_in, 16)
            act.dma_start(g[:], d["g"].partition_broadcast(P)).then_inc(weights_in, 16)
            act.wait_ge(weights_in, 80)
            for b in range(BATCH):
                act.wait_ge(x_in[b], 32)
                with act.Fori(0, STEPS // 2) as i:
                    for j in range(2):
                        act.wait_ge(feat_free, 2 * i + (STEPS * b + j + 1))
                        for f in range(2):
                            act.activation(feat[:, j, f, :], x2[:, b, bass.ds(i * (2 * W) + j * W, W)],
                                           ACT.Sigmoid, scale=factor[:, f:f + 1]).then_inc(sigmoids_made, 1)
            act.wait_ge(var_made, 1)
            act.activation(root[:, 0, :], shifted[:], ACT.Sqrt).then_inc(roots_made, 1)
            act.activation(root[:, 1, :], var[:], ACT.Sqrt).then_inc(roots_made, 1)

        @block.tensor
        def _(pe):
            pe.sem_inc(feat_free, 2)
            pe.wait_ge(weights_in, 80)
            with pe.Fori(0, BATCH * STEPS // 2) as i:
                for j in range(2):
                    pe.wait_ge(silu_made, 2 * i + (j + 1))
                    pe.wait_ge(sigmoids_made, 4 * i + (2 * j + 2))
                    pe.wait_ge(h_free, 2 * i + (j + 1))
                    for t in range(WT):
                        for f in range(2):
                            last = pe.matmul(pH[:, j, t * C:(t + 1) * C], feat[:, j, f, t * P:(t + 1) * P],
                                             wtok[:, f, :], start=f == 0, stop=f == 1)
                    last.then_inc(h_ready, 1)
                    pe.wait_ge(h_ready, 2 * i + (j + 1))
                    pe.sem_inc(feat_free, 1)

        @block.gpsimd
        def _(pool):
            for b in range(BATCH):
                with pool.Fori(0, STEPS // 2) as i:
                    for j in range(2):
                        pool.wait_ge(sigmoids_made, 4 * i + (2 * STEPS * b + 2 * j + 1))
                        pool.tensor_tensor(feat[0:C, j, 0, :], feat[0:C, j, 0, :],
                                           x2[0:C, b, bass.ds(i * (2 * W) + j * W, W)],
                                           ALU.mult).then_inc(silu_made, 1)

        @block.vector
        def _(dve):
            chain = Chain(dve, dve_chain)
            dve.sem_inc(h_free, 2)
            dve.wait_ge(weights_in, 80)
            chain.then(dve.tensor_tensor(bias[:], biases[:, 0, :], biases[:, 1, :], ALU.add))
            chain.ready()
            with dve.Fori(0, BATCH * STEPS // 2) as i:
                for j in range(2):
                    dve.wait_ge(h_ready, 2 * i + (j + 1))
                    dve.tensor_tensor(H[:, bass.ds(i * (2 * WT) + j * WT, WT), :],
                                      pH[:, j, :].rearrange("p (t c) -> p t c", c=C),
                                      bcast(bias[:], 1, WT), ALU.add).then_inc(h_free, 1)
            dve.wait_ge(h_free, BATCH * STEPS + 2)
            centre(dve, chain, H, XC, square, sums, mean, var)
            chain.ready()
            dve.tensor_scalar(shifted[:], var[:], LN_EPS, None, ALU.add).then_inc(var_made, 1)
            dve.wait_ge(roots_made, 2)
            chain.then(dve.reciprocal(inv[:], root[:, 0, :]))
            chain.ready()
            chain.then(dve.tensor_tensor(norm[:], root[:, 1, :], inv[:], ALU.mult))
            chain.ready()
            chain.then(dve.tensor_scalar(norm[:], norm[:], NORM_EPS, None, ALU.max))
            chain.ready()
            chain.then(dve.reciprocal(norm[:], norm[:]))
            chain.ready()
            chain.then(dve.scalar_tensor_tensor(out=scale[:], in0=norm[:], scalar=g[:, 0:1], in1=inv[:],
                                                op0=ALU.mult, op1=ALU.mult))
            chain.ready()


def centre(dve, chain, H, XC, square, sums, mean, var):
    chain.then(dve.tensor_reduce(sums[:], H[:], AX.X, ALU.add))
    chain.ready()
    chain.then(dve.tensor_scalar(mean[:], sums[:], 1.0 / C, None, ALU.mult))
    chain.ready()
    chain.then(dve.tensor_tensor(XC[:], H[:], bcast(mean[:], 2, C), ALU.subtract))
    chain.ready()
    chain.then(dve.tensor_tensor(square[:], XC[:], XC[:], ALU.mult))
    chain.ready()
    chain.then(dve.tensor_reduce(sums[:], square[:], AX.X, ALU.add))
    chain.ready()
    chain.then(dve.tensor_scalar(var[:], sums[:], 1.0 / C, None, ALU.mult))


def split_weights(dve, chain, raw, hi, lo):
    chain.then(dve.tensor_copy(hi, raw))
    chain.ready()
    chain.then(dve.tensor_tensor(lo, raw, hi.bitcast(F32), ALU.subtract))


def split_rows(dve, chain, src, pair):
    chain.then(dve.tensor_copy(pair[:, :, 0:C].bitcast(F32R), src))
    chain.ready()
    chain.then(dve.tensor_tensor(pair[:, :, C:2 * C], src, pair[:, :, 0:C], ALU.subtract))


def gated_attention(nc, d, H, XC, scale, ident):
    PAIRS = BT // 2
    with ExitStack() as ctx:
        m = Scope(nc, ctx, "ga")
        wraw = m.sb("wraw", [P, 3 * GH])
        whi = m.sb("whi", [P, 3 * GH], F32R)
        wlo = m.sb("wlo", [P, 3 * GH], F32R)
        wo = m.sb("wo", [GH, C])
        cols = m.sb("cols", [P, 7])
        bcol, gb = cols[:, 0:3], cols[:, 3:7]
        bv = m.sb("bv", [P, GH])
        bo = m.sb("bo", [P, C])
        xn = m.sb("xn", [P, CT, C])
        pair = m.sb("pair", [P, CT, 2 * C])
        xT = m.sb("xT", [P, CH], F32R)
        base = m.sb("base", [P, CH])
        vb = m.sb("vb", [P, CT, GH])
        q = m.sb("q", [P, CH])
        k = m.sb("k", [P, CH])
        qhi = m.sb("qhi", [P, SEQ], F32R)
        qlo = m.sb("qlo", [P, SEQ], F32R)
        khi = m.sb("khi", [P, SEQ], F32R)
        klo = m.sb("klo", [P, SEQ], F32R)
        V = m.sb("V", [P, BT, GH])
        uT = m.sb("uT", [P, SEQ])
        relu = m.sb("relu", [P, 2, 2 * CH])
        attn = m.sb("attn", [P, 2, 2, CH])
        gated = m.sb("gated", [P, CH])
        pS = m.ps("pS", [P, 4, 512])
        pO = m.ps("pO", [P, 512])
        pY = m.ps("pY", [P, 512])
        pBase, pU, pV, pT = pS[:, 0, :], pS[:, 1, :], pS[:, 2, :], pS[:, 3, :]

        weights_in = m.sem("weights_in")
        split_done = m.sem("split_done")
        pair_made = m.sem("pair_made")
        xT_ready = m.sem("xT_ready")
        xT_made = m.sem("xT_made")
        proj_ready = m.sem("proj_ready")
        vb_made = m.sem("vb_made")
        base_made = m.sem("base_made")
        uv_made = m.sem("uv_made")
        q_made = m.sem("q_made")
        k_made = m.sem("k_made")
        scores_ready = m.sem("scores_ready")
        relu_made = m.sem("relu_made")
        attn_made = m.sem("attn_made")
        pairs_summed = m.sem("pairs_summed")
        gated_made = m.sem("gated_made")
        y_ready = m.sem("y_ready")
        h_made = m.sem("h_made")
        bo_added = m.sem("bo_added")
        dve_chain = m.sem("dve_chain")
        pool_chain = m.sem("pool_chain")
        pe_gate = m.sem("pe_gate")
        pool_gate = m.sem("pool_gate")
        block = ctx.enter_context(nc.Block())

        @block.sync
        def _(sp):
            for half in (0, C):
                sp.dma_start(wraw[half:half + C, :], d["W_uv"]).then_inc(weights_in, 16)
            sp.dma_start(wo[:], d["W_o"]).then_inc(weights_in, 16)
            sp.dma_start(cols[:], d["ga_cols"]).then_inc(weights_in, 16)
            sp.dma_start(bv[:], d["b_uv"][GH:2 * GH].partition_broadcast(P)).then_inc(weights_in, 16)
            sp.dma_start(bo[:], d["b_o"].partition_broadcast(P)).then_inc(weights_in, 16)

        @block.tensor
        def _(pe):
            pe.wait_ge(weights_in, 96)
            pe.wait_ge(split_done, 1)
            with pe.Fori(0, BATCH) as b:
                with pe.Fori(0, CHUNKS) as c:
                    n = b * CHUNKS + c
                    pe.wait_ge(pair_made, n + 1)
                    for t in range(CT):
                        last = pe.transpose(pT[:, t * P:(t + 1) * P], pair[:, t, :], ident[:])
                    last.then_inc(xT_ready, 1)
                    pe.wait_ge(xT_made, n + 1)
                    pe.wait_ge(vb_made, n + 1)
                    pe.wait_ge(uv_made, 2 * n + 1)
                    for out, col in ((pBase, 2 * GH), (pU, 0)):
                        for w in (whi, wlo):
                            last = pe.matmul(out, w[:, col:col + GH], xT[:], start=w is whi, stop=w is wlo)
                        last.then_inc(proj_ready, 1)
                    for t in range(CT):
                        for w in (whi, wlo):
                            last = pe.matmul(pV[:, t * P:(t + 1) * P], xT[:, t * P:(t + 1) * P],
                                             w[:, GH:2 * GH], start=w is whi, stop=w is wlo)
                    last.then_inc(proj_ready, 1)
                pe.wait_ge(q_made, (b + 1) * CHUNKS + 1)
                pe.wait_ge(k_made, (b + 1) * CHUNKS + 1)
                pe.wait_ge(vb_made, (b + 1) * CHUNKS + 1)
                pe.wait_ge(uv_made, (b + 1) * (2 * CHUNKS) + 1)
                pe.sem_inc(pe_gate, 1)
                with pe.Fori(0, CHUNKS) as qb:
                    g0 = (b * CHUNKS + qb) * PAIRS

                    def weigh_values(p):
                        pe.wait_ge(attn_made, g0 + (p + 3))
                        if p == 0:
                            pe.wait_ge(gated_made, b * CHUNKS + qb + 1)
                        for j in range(2):
                            last = pe.matmul(pO[:], V[:, 2 * p + j, :], attn[:, p % 2, j, :],
                                             start=p == 0 and j == 0, stop=p == PAIRS - 1 and j == 1)
                        last.then_inc(pairs_summed, 1)

                    for p in range(PAIRS):
                        pe.wait_ge(relu_made, g0 + (p + 1))
                        pe.sem_inc(pe_gate, 1)
                        for j in range(2):
                            kt = slice((2 * p + j) * P, (2 * p + j + 1) * P)
                            qs = bass.ds(qb * CH, CH)
                            out = pS[:, 2 * (p % 2) + j, :]
                            pe.matmul(out, khi[:, kt], qhi[:, qs], start=True, stop=False)
                            pe.matmul(out, khi[:, kt], qlo[:, qs], start=False, stop=False)
                            last = pe.matmul(out, klo[:, kt], qhi[:, qs], start=False, stop=True)
                        last.then_inc(scores_ready, 1)
                        if p:
                            weigh_values(p - 1)
                    weigh_values(PAIRS - 1)
                    pe.wait_ge(gated_made, b * CHUNKS + qb + 2)
                    pe.wait_ge(h_made, b * CHUNKS + qb + 1)
                    for t in range(CT):
                        last = pe.matmul(pY[:, t * C:(t + 1) * C], gated[:, t * P:(t + 1) * P], wo[:],
                                         start=True, stop=True)
                    last.then_inc(y_ready, 1)

        @block.scalar
        def _(act):
            act.sem_inc(uv_made, 1)
            act.sem_inc(attn_made, 2)
            act.wait_ge(weights_in, 96)
            with act.Fori(0, BATCH) as b:
                with act.Fori(0, CHUNKS) as c:
                    n = b * CHUNKS + c
                    act.wait_ge(proj_ready, 3 * n + 1)
                    act.wait_ge(q_made, n + 1)
                    act.wait_ge(k_made, n + 1)
                    act.activation(base[:], pBase, ACT.Silu, bias=bcol[:, 2:3]).then_inc(base_made, 1)
                    act.wait_ge(proj_ready, 3 * n + 2)
                    act.activation(uT[:, bass.ds(c * CH, CH)], pU, ACT.Silu, bias=bcol[:, 0:1]).then_inc(uv_made, 1)
                    act.wait_ge(vb_made, n + 2)
                    act.activation(V[:, bass.ds(c * CT, CT), :], vb[:], ACT.Silu).then_inc(uv_made, 1)
                with act.Fori(0, CHUNKS) as qb:
                    g0 = (b * CHUNKS + qb) * PAIRS
                    for p in range(PAIRS):
                        act.wait_ge(relu_made, g0 + (p + 3))
                        act.wait_ge(pairs_summed, g0 + (p + 1))
                        act.activation(attn[:, p % 2, :, :].rearrange("p j q -> p (j q)"), relu[:, p % 2, :],
                                       ACT.Square).then_inc(attn_made, 1)

        @block.gpsimd
        def _(pool):
            chain = Chain(pool, pool_chain)
            pool.sem_inc(k_made, 1)
            pool.sem_inc(pairs_summed, 2)
            pool.wait_ge(weights_in, 96)
            pool.tensor_tensor(H[:], H[:], bcast(bo[:], 1, TILES), ALU.add).then_inc(bo_added, 1)
            with pool.Fori(0, BATCH) as b:
                with pool.Fori(0, CHUNKS) as c:
                    chain.enter((b * CHUNKS + c) * 2)
                    pool.wait_ge(base_made, b * CHUNKS + c + 1)
                    pool.sem_inc(pool_gate, 1)
                    chain.then(pool.tensor_scalar(k[:], base[:], gb[:, 1:2], gb[:, 3:4], ALU.mult, ALU.add))
                    chain.ready()
                    hi = khi[:, bass.ds(c * CH, CH)]
                    chain.then(pool.tensor_copy(hi, k[:]))
                    chain.ready()
                    pool.tensor_tensor(klo[:, bass.ds(c * CH, CH)], k[:], hi.bitcast(F32),
                                       ALU.subtract).then_inc(k_made, 1)
                    chain.leave(2, 0)

        @block.vector
        def _(dve):
            chain = Chain(dve, dve_chain)
            for credit, many in ((vb_made, 1), (q_made, 1), (relu_made, 2), (gated_made, 1), (h_made, 1)):
                dve.sem_inc(credit, many)
            dve.wait_ge(weights_in, 96)
            split_weights(dve, chain, wraw[:], whi[:], wlo[:])
            chain.ready()
            dve.sem_inc(split_done, 1)
            dve.wait_ge(bo_added, 1)
            with dve.Fori(0, BATCH) as b:
                with dve.Fori(0, CHUNKS) as c:
                    n = b * CHUNKS + c
                    chain.enter(n * 4 + 2)
                    tiles = bass.ds(b * BT + c * CT, CT)
                    chain.then(dve.tensor_tensor(xn[:], XC[:, tiles, :], bcast(scale[:, tiles], 2, C), ALU.mult))
                    chain.ready()
                    chain.then(dve.tensor_copy(pair[:, :, 0:C].bitcast(F32R), xn[:]))
                    chain.ready()
                    dve.tensor_tensor(pair[:, :, C:2 * C], xn[:], pair[:, :, 0:C],
                                      ALU.subtract).then_inc(pair_made, 1)
                    dve.wait_ge(xT_ready, n + 1)
                    dve.tensor_copy(xT[:], pT).then_inc(xT_made, 1)
                    dve.wait_ge(proj_ready, 3 * n + 3)
                    dve.wait_ge(uv_made, 2 * n + 1)
                    dve.tensor_tensor(vb[:], pV.rearrange("p (t c) -> p t c", c=GH), bcast(bv[:], 1, CT),
                                      ALU.add).then_inc(vb_made, 1)
                    dve.wait_ge(base_made, n + 1)
                    chain.then(dve.tensor_scalar(q[:], base[:], gb[:, 0:1], gb[:, 2:3], ALU.mult, ALU.add))
                    chain.ready()
                    hi = qhi[:, bass.ds(c * CH, CH)]
                    chain.then(dve.tensor_copy(hi, q[:]))
                    chain.ready()
                    dve.tensor_tensor(qlo[:, bass.ds(c * CH, CH)], q[:], hi.bitcast(F32),
                                      ALU.subtract).then_inc(q_made, 1)
                    chain.leave(4, 0)
                with dve.Fori(0, CHUNKS) as qb:
                    n = b * CHUNKS + qb
                    g0 = n * PAIRS
                    for p in range(PAIRS):
                        dve.wait_ge(scores_ready, g0 + (p + 1))
                        dve.wait_ge(attn_made, g0 + (p + 1))
                        dve.tensor_scalar(relu[:, p % 2, :],
                                          pS[:, 2 * (p % 2):2 * (p % 2) + 2, :].rearrange("p j q -> p (j q)"),
                                          0.0, None, ALU.max).then_inc(relu_made, 1)
                    dve.wait_ge(pairs_summed, g0 + (PAIRS + 2))
                    dve.scalar_tensor_tensor(out=gated[:], in0=pO[:], scalar=1.0 / GH,
                                             in1=uT[:, bass.ds(qb * CH, CH)], op0=ALU.mult,
                                             op1=ALU.mult).then_inc(gated_made, 1)
                    dve.wait_ge(y_ready, n + 1)
                    tiles = bass.ds(b * BT + qb * CT, CT)
                    dve.tensor_tensor(H[:, tiles, :], pY[:, 0:CT * C].rearrange("p (t c) -> p t c", c=C),
                                      H[:, tiles, :], ALU.add).then_inc(h_made, 1)


def normed_input(nc, H, XC, X2, inv_rms):
    with ExitStack() as ctx:
        m = Scope(nc, ctx, "ln")
        square = m.sb("square", [P, TILES, C])
        sums = m.sb("sums", [P, TILES])
        mean = m.sb("mean", [P, TILES])
        var = m.sb("var", [P, TILES])
        shifted = m.sb("shifted", [P, TILES])
        root = m.sb("root", [P, TILES])
        inv = m.sb("inv", [P, TILES])
        ms = m.sb("ms", [P, TILES])
        shifted_made = m.sem("shifted_made")
        root_made = m.sem("root_made")
        dve_chain = m.sem("dve_chain")
        block = ctx.enter_context(nc.Block())

        @block.scalar
        def _(act):
            for n in range(2):
                act.wait_ge(shifted_made, n + 1)
                act.activation(root[:], shifted[:], ACT.Sqrt).then_inc(root_made, 1)

        @block.vector
        def _(dve):
            chain = Chain(dve, dve_chain)
            centre(dve, chain, H, XC, square, sums, mean, var)
            chain.ready()
            dve.tensor_scalar(shifted[:], var[:], LN_EPS, None, ALU.add).then_inc(shifted_made, 1)
            dve.wait_ge(root_made, 1)
            chain.then(dve.reciprocal(inv[:], root[:]))
            chain.ready()
            chain.then(dve.tensor_tensor(X2[:], XC[:], bcast(inv[:], 2, C), ALU.mult))
            chain.then(dve.tensor_tensor(ms[:], var[:], inv[:], ALU.mult))
            chain.ready()
            chain.then(dve.tensor_tensor(ms[:], ms[:], inv[:], ALU.mult))
            chain.ready()
            dve.tensor_scalar(shifted[:], ms[:], RMS_EPS, None, ALU.add).then_inc(shifted_made, 1)
            dve.wait_ge(root_made, 2)
            chain.then(dve.reciprocal(inv_rms[:], root[:]))
            chain.ready()


def causal_attention(nc, d, X2, inv_rms, ident, identb, masks):
    FULL = CHUNKS * (CHUNKS + 1) // 2 * CT

    def before(qb):
        return 2 * qb * (qb + 1)

    with ExitStack() as ctx:
        m = Scope(nc, ctx, "ca")
        wraw = m.sb("wraw", [P, QKV])
        whi = m.sb("whi", [P, QKV], F32R)
        wlo = m.sb("wlo", [P, QKV], F32R)
        woraw = m.sb("woraw", [P, C])
        wohi = m.sb("wohi", [P, C], F32R)
        wolo = m.sb("wolo", [P, C], F32R)
        ln1 = m.sb("ln1", [P, 1])
        cos = m.sb("cos", [P, BT, HD])
        sin = m.sb("sin", [P, BT, HD])
        hx = m.sb("hx", [P, CT, C])
        pair = m.sb("pair", [P, CT, 2 * C])
        xT = m.sb("xT", [P, CH], F32R)
        direct = m.sb("direct", [P, CT, NH + NKV, HD])
        turned = m.sb("turned", [P, CT, NH + NKV, HD])
        QK = m.sb("QK", [P, BT, ROPED])
        KS = m.sb("KS", [P, CT, NKV, STACK], BF16)
        QS = m.sb("QS", [P, 2, CT, NH, STACK], BF16)
        rest = m.sb("rest", [P, CT, NH, HD])
        KT = m.sb("KT", [STACK + SHIFT, NKV, SEQ], BF16)
        QT = m.sb("QT", [STACK + SHIFT, 2, NH, CH], BF16)
        VA = m.sb("VA", [P, BT, NKV, VW])
        VS = m.sb("VS", [P, CT, NKV, VW])
        zeros = m.sb("zeros", [P, CH], BF16)
        probs = m.sb("probs", [P, 2, NH, CH])
        peaks = m.sb("peaks", [P, CT, NH, CHUNKS])
        peak = m.sb("peak", [P, CT, NH])
        left = m.sb("left", [P, CT, NH])
        shift = m.sb("shift", [P, CT, NH, SHIFT + 1], BF16)
        oT = m.sb("oT", [P, CH])
        inv = m.sb("inv", [P, CT, NH])
        y = m.sb("y", [P, CT, C])
        ypair = m.sb("ypair", [P, CT, 2 * C])
        yT = m.sb("yT", [P, CH], F32R)
        pS = m.ps("pS", [P, 2, 512])
        pM = m.ps("pM", [P, 4, 512])
        pO = m.ps("pO", [P, 512])
        pX = m.ps("pX", [P, 512])
        pK, pT, pQ = pM[:, 0, :].bitcast(BF16), pM[:, 2, :], pM[:, 3, :]

        weights_in = m.sem("weights_in")
        split_done = m.sem("split_done")
        fills_done = m.sem("fills_done")
        pair_made = m.sem("pair_made")
        xT_ready = m.sem("xT_ready")
        xT_made = m.sem("xT_made")
        qkv_ready = m.sem("qkv_ready")
        roped = m.sem("roped")
        v_made = m.sem("v_made")
        ks_made = m.sem("ks_made")
        kT_ready = m.sem("kT_ready")
        kT_made = m.sem("kT_made")
        qs_made = m.sem("qs_made")
        qT_ready = m.sem("qT_ready")
        qT_made = m.sem("qT_made")
        raw_ready = m.sem("raw_ready")
        raw_free = m.sem("raw_free")
        shift_made = m.sem("shift_made")
        shiftT_ready = m.sem("shiftT_ready")
        shiftT_made = m.sem("shiftT_made")
        vs_made = m.sem("vs_made")
        scores_ready = m.sem("scores_ready")
        probs_made = m.sem("probs_made")
        weighed = m.sem("weighed")
        o_copied = m.sem("o_copied")
        oT_ready = m.sem("oT_ready")
        y_made = m.sem("y_made")
        yT_ready = m.sem("yT_ready")
        yT_made = m.sem("yT_made")
        wo_ready = m.sem("wo_ready")
        x3_made = m.sem("x3_made")
        dve_chain = m.sem("dve_chain")
        pool_chain = m.sem("pool_chain")
        pe_gate, act_gate, dve_gate, pool_gate = (m.sem(f"{e}_gate") for e in ("pe", "act", "dve", "pool"))
        block = ctx.enter_context(nc.Block())

        @block.sync
        def _(sp):
            for half in (0, C):
                sp.dma_start(wraw[half:half + C, :], d["wqkv"]).then_inc(weights_in, 16)
                sp.dma_start(woraw[half:half + C, :], d["wo"]).then_inc(weights_in, 16)
                sp.dma_start(ln1[half:half + C, :], d["ln1_w"]).then_inc(weights_in, 16)
            sp.dma_start(cos[:], d["cos"]).then_inc(weights_in, 16)
            sp.dma_start(sin[:], d["sin"]).then_inc(weights_in, 16)

        @block.tensor
        def _(pe):
            def gated_wait(sem, value):
                pe.wait_ge(sem, value)
                pe.sem_inc(pe_gate, 1)

            pe.sem_inc(qT_ready, 2)
            pe.sem_inc(weighed, CT)
            pe.wait_ge(weights_in, 128)
            pe.wait_ge(split_done, 1)
            pe.wait_ge(fills_done, 3)
            with pe.Fori(0, BATCH) as b:
                s0 = b * FULL

                with pe.Fori(0, CHUNKS) as c:
                    n = b * CHUNKS + c
                    pe.wait_ge(pair_made, n + 1)
                    for t in range(CT):
                        last = pe.transpose(pT[:, t * P:(t + 1) * P], pair[:, t, :], ident[:])
                    last.then_inc(xT_ready, 1)
                    pe.wait_ge(xT_made, n + 1)
                    pe.wait_ge(v_made, n + 1)
                    for t in range(CT):
                        for w in (whi, wlo):
                            last = pe.matmul(pQ[:, t * QKV:(t + 1) * QKV], xT[:, t * P:(t + 1) * P], w[:],
                                             start=w is whi, stop=w is wlo)
                    last.then_inc(qkv_ready, 1)
                    pe.wait_ge(ks_made, n + 1)
                    pe.wait_ge(kT_made, n + 1)
                    for kv in range(NKV):
                        for t in range(CT):
                            col = (kv * CT + t) * P
                            last = pe.transpose(pK[0:STACK, col:col + P], KS[:, t, kv, :], identb[:])
                    last.then_inc(kT_ready, 1)
                gated_wait(kT_made, (b + 1) * CHUNKS + 1)
                gated_wait(v_made, (b + 1) * CHUNKS + 1)

                def turn_queries(qb):
                    n = b * CHUNKS + qb
                    gated_wait(qs_made, n + 1)
                    gated_wait(raw_free, 2 * (s0 + before(qb)) + 2)
                    bank = pM[:].bitcast(BF16)
                    for h in range(NH):
                        for t in range(CT):
                            col = ((h % 2) * CT + t) * P
                            last = pe.transpose(bank[0:STACK, h // 2, col:col + P], QS[:, qb % 2, t, h, :], identb[:])
                    last.then_inc(qT_ready, 1)
                    gated_wait(qT_made, n + 1)

                def raw_scores(qb, c, t, diag=False):
                    unit = s0 + before(qb) + 4 * c + t
                    keys = (t + 1) * P if diag else CH
                    at = c * CH if diag or isinstance(c, int) else None
                    for k in range(2):
                        gated_wait(raw_free, 2 * unit + (k + 1))
                        for h in (2 * k, 2 * k + 1):
                            rhs = KT[0:STACK, h // 2, at:at + keys] if at is not None else \
                                KT[0:STACK, h // 2, bass.ds(c * CH, CH)]
                            last = pe.matmul(pM[:, h, 0:keys], QT[0:STACK, qb % 2, h, t * P:(t + 1) * P], rhs,
                                             start=True, stop=not diag)
                            if diag:
                                last = pe.matmul(pM[:, h, t * P:keys], identb[:], masks[:, 1, :],
                                                 start=False, stop=True)
                        last.then_inc(raw_ready, 1)

                def scores(qb, c, t, heads, diag=False):
                    step = s0 + before(qb) + 4 * c + t
                    q0 = t * P if diag else 0
                    static = diag or isinstance(c, int)
                    for h in heads:
                        gated_wait(probs_made, 4 * step + (h + 1))
                        lhsT = KT[:, h // 2, (4 * c + t) * P:(4 * c + t + 1) * P] if static else \
                            KT[:, h // 2, bass.ds(c * CH + t * P, P)]
                        last = pe.matmul(pS[:, h % 2, q0:CH], lhsT, QT[:, qb % 2, h, q0:CH],
                                         start=True, stop=not diag)
                        if diag:
                            last = pe.matmul(pS[:, h % 2, q0:q0 + P], identb[:], masks[:, 0, :],
                                             start=False, stop=True)
                        last.then_inc(scores_ready, 1)

                def weigh(qb, c, t, diag=False):
                    step = s0 + before(qb) + 4 * c + t
                    q0 = t * P if diag else 0
                    gated_wait(vs_made, step + 1)
                    gated_wait(probs_made, 4 * step + 6)
                    for h in range(NH):
                        last = pe.matmul(pO[VW * h:VW * h + VW, q0:CH], VS[:, t, h // 2, :],
                                         probs[:, t % 2, h, q0:CH], start=False, stop=False,
                                         skip_group_check=True)
                    last.then_inc(weighed, 1)

                turn_queries(0)
                for t in range(CT):
                    raw_scores(0, 0, t, diag=True)
                for qb in range(CHUNKS):
                    n = b * CHUNKS + qb
                    ahead = qb + 1 < CHUNKS
                    if qb == 0:
                        turn_shift(pe, gated_wait, pM, shift, identb, shift_made, shiftT_ready, n)
                    gated_wait(shiftT_made, n + 1)
                    if ahead:
                        turn_queries(qb + 1)
                    gated_wait(o_copied, n + 1)
                    pe.matmul(pO[:], zeros[:, 0:P], zeros[:], start=True, stop=False, skip_group_check=True)
                    if qb:
                        with pe.Fori(0, qb) as c:
                            for t in range(CT):
                                scores(qb, c, t, (0, 1))
                                if t:
                                    weigh(qb, c, t - 1)
                                scores(qb, c, t, (2, 3))
                                if ahead:
                                    raw_scores(qb + 1, c, t)
                            weigh(qb, c, CT - 1)
                    for t in range(CT):
                        scores(qb, qb, t, (0, 1), diag=True)
                        if t:
                            weigh(qb, qb, t - 1, diag=True)
                        scores(qb, qb, t, (2, 3), diag=True)
                        if ahead:
                            raw_scores(qb + 1, qb, t)
                    weigh(qb, qb, CT - 1, diag=True)
                    if ahead:
                        for t in range(CT):
                            raw_scores(qb + 1, qb + 1, t, diag=True)
                    gated_wait(o_copied, n + 2)
                    gated_wait(x3_made, n + 1)
                    for t in range(CT):
                        last = pe.transpose(pX[:, t * P:(t + 1) * P], oT[:, t * P:(t + 1) * P], ident[:])
                    last.then_inc(oT_ready, 1)
                    if ahead:
                        turn_shift(pe, gated_wait, pM, shift, identb, shift_made, shiftT_ready, n + 1)
                    gated_wait(y_made, n + 1)
                    for t in range(CT):
                        last = pe.transpose(pX[:, t * P:(t + 1) * P], ypair[:, t, :], ident[:])
                    last.then_inc(yT_ready, 1)
                    gated_wait(yT_made, n + 1)
                    for t in range(CT):
                        for w in (wohi, wolo):
                            last = pe.matmul(pX[:, t * C:(t + 1) * C], yT[:, t * P:(t + 1) * P], w[:],
                                             start=w is wohi, stop=w is wolo)
                    last.then_inc(wo_ready, 1)

        @block.scalar
        def _(act):
            def gated_wait(sem, value):
                act.wait_ge(sem, value)
                act.sem_inc(act_gate, 1)

            for credit, many in ((v_made, 1), (kT_made, 1), (probs_made, 2), (o_copied, 1)):
                act.sem_inc(credit, many)
            act.wait_ge(fills_done, 3)
            with act.Fori(0, BATCH) as b:
                s0 = b * FULL
                with act.Fori(0, CHUNKS) as c:
                    n = b * CHUNKS + c
                    gated_wait(roped, n + 1)
                    act.activation(VA[:, bass.ds(c * CT, CT), :, 0:HD],
                                   pQ.rearrange("p (t n) -> p t n", n=QKV)[:, :, ROPED:QKV]
                                   .rearrange("p t (k e) -> p t k e", e=HD), ACT.Copy).then_inc(v_made, 1)
                    gated_wait(kT_ready, n + 1)
                    act.activation(KT[0:STACK, :, bass.ds(c * CH, CH)],
                                   pK[0:STACK, :].rearrange("p (k n) -> p k n", n=CH),
                                   ACT.Copy).then_inc(kT_made, 1)

                def take_queries(qb):
                    gated_wait(qT_ready, b * CHUNKS + qb + 3)
                    act.activation(QT[0:STACK, qb % 2, :, :].rearrange("p h n -> p (h n)"),
                                   pM[0:STACK, 0:2, :].bitcast(BF16).rearrange("p a n -> p (a n)"),
                                   ACT.Copy).then_inc(qT_made, 1)

                def take_shift(qb):
                    gated_wait(shiftT_ready, b * CHUNKS + qb + 1)
                    act.activation(QT[STACK:STACK + SHIFT, qb % 2, :, :].rearrange("p h n -> p (h n)"),
                                   pM[STACK:STACK + SHIFT, 0:2, :].bitcast(BF16).rearrange("p a n -> p (a n)"),
                                   ACT.Copy).then_inc(shiftT_made, 1)

                def exps(qb, c, t, diag=False):
                    step = s0 + before(qb) + 4 * c + t
                    q0 = t * P if diag else 0
                    gated_wait(weighed, step + (CT - 1))
                    for h in range(NH):
                        act.wait_ge(scores_ready, 4 * step + (h + 1))
                        act.activation(probs[:, t % 2, h, q0:CH], pS[:, h % 2, q0:CH], ACT.Exp,
                                       scale=float(HD) ** -0.5).then_inc(probs_made, 1)

                take_queries(0)
                for qb in range(CHUNKS):
                    if qb == 0:
                        take_shift(0)
                    if qb + 1 < CHUNKS:
                        take_queries(qb + 1)
                    if qb:
                        with act.Fori(0, qb) as c:
                            for t in range(CT):
                                exps(qb, c, t)
                    for t in range(CT):
                        exps(qb, qb, t, diag=True)
                    gated_wait(weighed, s0 + before(qb + 1) + CT)
                    gated_wait(oT_ready, b * CHUNKS + qb + 1)
                    act.activation(oT[:], pO[:], ACT.Copy).then_inc(o_copied, 1)
                    if qb + 1 < CHUNKS:
                        take_shift(qb + 1)

        @block.gpsimd
        def _(pool):
            chain = Chain(pool, pool_chain)

            def gated_wait(sem, value):
                pool.wait_ge(sem, value)
                pool.sem_inc(pool_gate, 1)

            def chained():
                chain.ready()
                if chain.base is not None:
                    pool.sem_inc(pool_gate, 1)

            def stack(src, out, res, parts, signal):
                def block_of(i):
                    return out[:, :, :, i * HD:(i + 1) * HD]

                first = [parts.index(k) for k in range(3)]
                chain.then(pool.tensor_copy(block_of(first[0]), src))
                chained()
                chain.then(pool.tensor_tensor(res, src, block_of(first[0]), ALU.subtract))
                chained()
                chain.then(pool.tensor_copy(block_of(first[1]), res))
                chained()
                chain.then(pool.tensor_tensor(res, res, block_of(first[1]), ALU.subtract))
                chained()
                chain.then(pool.tensor_copy(block_of(first[2]), res))
                for i, k in enumerate(parts):
                    if i not in first:
                        chain.then(pool.tensor_copy(block_of(i), block_of(first[k])))
                chained()
                pool.sem_inc(signal, 1)

            pool.memset(VA[:], 0.0).then_inc(fills_done, 1)
            pool.wait_ge(fills_done, 1)
            pool.memset(KT[STACK:STACK + SHIFT, :, :], 1.0).then_inc(fills_done, 1)
            pool.wait_ge(fills_done, 2)
            pool.memset(VA[:, :, :, HD:HD + 1], 1.0).then_inc(fills_done, 1)
            pool.sem_inc(oT_ready, 1)
            PER = 8
            with pool.Fori(0, BATCH) as b:
                s0 = b * FULL
                with pool.Fori(0, CHUNKS) as c:
                    chain.enter(b * (2 * CHUNKS * PER) + c * PER)
                    n = b * CHUNKS + c
                    gated_wait(roped, n + 1)
                    stack(QK[:, bass.ds(c * CT, CT), NH * HD:ROPED].rearrange("p t (h e) -> p t h e", e=HD),
                          KS[:], rest[:, :, 0:NKV, :], K_PARTS, ks_made)
                    chain.leave(PER, 0)

                def stack_queries(qb):
                    chain.enter(b * (2 * CHUNKS * PER) + (CHUNKS + qb) * PER)
                    gated_wait(qT_ready, b * CHUNKS + qb + 1)
                    stack(QK[:, qb * CT:(qb + 1) * CT, 0:NH * HD].rearrange("p t (h e) -> p t h e", e=HD),
                          QS[:, qb % 2, :, :, :], rest[:], Q_PARTS, qs_made)
                    chain.leave(PER, 0)

                def stage_values(qb, c, t):
                    gated_wait(weighed, s0 + before(qb) + 4 * c + t + 1)
                    tile = 4 * c + t if isinstance(c, int) else None
                    src = VA[:, tile, :, :] if tile is not None else VA[:, bass.ds(c * CT + t, 1), :, :]
                    dst = VS[:, t, :, :] if tile is not None else VS[:, t:t + 1, :, :]
                    pool.tensor_copy(dst, src).then_inc(vs_made, 1)

                stack_queries(0)
                stack_queries(1)
                for qb in range(CHUNKS):
                    if qb:
                        with pool.Fori(0, qb) as c:
                            for t in range(CT):
                                stage_values(qb, c, t)
                    if qb + 2 < CHUNKS:
                        stack_queries(qb + 2)
                    for t in range(CT):
                        stage_values(qb, qb, t)

        @block.vector
        def _(dve):
            chain = Chain(dve, dve_chain)
            for credit, many in ((raw_free, 2), (x3_made, 1)):
                dve.sem_inc(credit, many)
            dve.memset(zeros[:], 0.0)
            dve.wait_ge(weights_in, 128)
            chain.then(dve.tensor_scalar(wraw[:], wraw[:], ln1[:, 0:1], None, ALU.mult))
            chain.ready()
            split_weights(dve, chain, wraw[:], whi[:], wlo[:])
            split_weights(dve, chain, woraw[:], wohi[:], wolo[:])
            chain.ready()
            dve.sem_inc(split_done, 1)
            SPLITS = chain.n
            PREP = 6
            TAIL = 11

            def gated_wait(sem, value):
                dve.wait_ge(sem, value)
                dve.sem_inc(dve_gate, 1)

            def chained():
                chain.ready()
                dve.sem_inc(dve_gate, 1)

            with dve.Fori(0, BATCH) as b:
                s0 = b * FULL
                c0 = b * (CHUNKS * (PREP + TAIL)) + SPLITS
                with dve.Fori(0, CHUNKS) as c:
                    n = b * CHUNKS + c
                    chain.enter(c0 + c * PREP)
                    tiles = bass.ds(b * BT + c * CT, CT)
                    own = bass.ds(c * CT, CT)
                    chain.then(dve.tensor_tensor(hx[:], X2[:, tiles, :], bcast(inv_rms[:, tiles], 2, C), ALU.mult))
                    chained()
                    chain.then(dve.tensor_copy(pair[:, :, 0:C].bitcast(F32R), hx[:]))
                    chained()
                    dve.tensor_tensor(pair[:, :, C:2 * C], hx[:], pair[:, :, 0:C],
                                      ALU.subtract).then_inc(pair_made, 1)
                    gated_wait(xT_ready, n + 1)
                    dve.tensor_copy(xT[:], pT).then_inc(xT_made, 1)
                    gated_wait(qkv_ready, n + 1)
                    qk = pQ.rearrange("p (t n) -> p t n", n=QKV)[:, :, 0:ROPED].rearrange(
                        "p t (h e) -> p t h e", e=HD)
                    chain.then(dve.tensor_tensor(direct[:], qk, bcast(cos[:, own, :], 2, NH + NKV), ALU.mult))
                    half = HD // 2
                    for lo, hi in ((0, half), (half, 0)):
                        chain.then(dve.tensor_tensor(turned[:, :, :, lo:lo + half], qk[:, :, :, hi:hi + half],
                                                     bcast(sin[:, own, lo:lo + half], 2, NH + NKV), ALU.mult))
                    chained()
                    chain.then(dve.tensor_tensor(QK[:, own, :].rearrange("p t (h e) -> p t h e", e=HD),
                                                 direct[:], turned[:], ALU.add))
                    chained()
                    dve.sem_inc(roped, 1)
                    chain.leave(PREP, 0)

                def maxima(qb, c, t, diag=False):
                    unit = s0 + before(qb) + 4 * c + t
                    keys = (t + 1) * P if diag else CH
                    at = slice(c, c + 1) if isinstance(c, int) else bass.ds(c, 1)
                    for k in range(2):
                        gated_wait(raw_ready, 2 * unit + (k + 1))
                        dve.tensor_reduce(peaks[:, t, 2 * k:2 * k + 2, at].rearrange("p h c -> p (h c)"),
                                          pM[:, 2 * k:2 * k + 2, 0:keys], AX.X, ALU.max).then_inc(raw_free, 1)

                def make_shift(qb):
                    gated_wait(raw_free, 2 * (s0 + before(qb + 1)) + 2)
                    chain.then(dve.tensor_reduce(peak[:], peaks[:, :, :, 0:qb + 1], AX.X, ALU.max, negate=True))
                    chained()
                    chain.then(dve.tensor_copy(shift[:, :, :, 0], peak[:]))
                    chained()
                    chain.then(dve.tensor_tensor(left[:], peak[:], shift[:, :, :, 0], ALU.subtract))
                    chained()
                    chain.then(dve.tensor_copy(shift[:, :, :, 1], left[:]))
                    chained()
                    chain.then(dve.tensor_tensor(left[:], left[:], shift[:, :, :, 1], ALU.subtract))
                    chained()
                    chain.then(dve.tensor_copy(shift[:, :, :, 2], left[:]))
                    chained()
                    dve.sem_inc(shift_made, 1)

                chain.enter(c0 + CHUNKS * PREP)
                for t in range(CT):
                    maxima(0, 0, t, diag=True)
                make_shift(0)
                for qb in range(CHUNKS):
                    n = b * CHUNKS + qb
                    if qb + 1 < CHUNKS:
                        if qb:
                            with dve.Fori(0, qb) as c:
                                for t in range(CT):
                                    maxima(qb + 1, c, t)
                        for t in range(CT):
                            maxima(qb + 1, qb, t)
                        for t in range(CT):
                            maxima(qb + 1, qb + 1, t, diag=True)
                        make_shift(qb + 1)
                    gated_wait(oT_ready, n + 2)
                    o = pX[:].rearrange("p (t h e) -> p t h e", h=NH, e=VW)
                    chain.then(dve.reciprocal(inv[:], o[:, :, :, HD]))
                    chained()
                    chain.then(dve.tensor_tensor(y[:].rearrange("p t (h e) -> p t h e", e=HD), o[:, :, :, 0:HD],
                                                 bcast(inv[:], 3, HD), ALU.mult))
                    chained()
                    chain.then(dve.tensor_copy(ypair[:, :, 0:C].bitcast(F32R), y[:]))
                    chained()
                    chain.then(dve.tensor_tensor(ypair[:, :, C:2 * C], y[:], ypair[:, :, 0:C], ALU.subtract))
                    chained()
                    dve.sem_inc(y_made, 1)
                    gated_wait(yT_ready, n + 1)
                    dve.tensor_copy(yT[:], pX[:]).then_inc(yT_made, 1)
                    gated_wait(wo_ready, n + 1)
                    tiles = bass.ds(b * BT + qb * CT, CT)
                    chain.then(dve.tensor_tensor(X2[:, tiles, :], pX[:, 0:CT * C].rearrange("p (t c) -> p t c", c=C),
                                                 X2[:, tiles, :], ALU.add))
                    chained()
                    dve.sem_inc(x3_made, 1)
                chain.leave(CHUNKS * TAIL, 0)


def turn_shift(pe, gated_wait, pM, shift, identb, shift_made, shiftT_ready, n):
    gated_wait(shift_made, n + 1)
    bank = pM[:].bitcast(BF16)
    for h in range(NH):
        for t in range(CT):
            col = ((h % 2) * CT + t) * P
            last = pe.transpose(bank[STACK:STACK + SHIFT, h // 2, col:col + P], shift[:, t, h, 0:SHIFT], identb[:])
    last.then_inc(shiftT_ready, 1)


def routing(nc, d, X3, ident, fT, weight):
    with ExitStack() as ctx:
        m = Scope(nc, ctx, "ro")
        square = m.sb("square", [P, TILES, C])
        ms = m.sb("ms", [P, TILES])
        root = m.sb("root", [P, TILES])
        inv = m.sb("inv", [P, TILES])
        rraw = m.sb("rraw", [P, NE])
        rhi = m.sb("rhi", [P, NE], F32R)
        rlo = m.sb("rlo", [P, NE], F32R)
        ln2 = m.sb("ln2", [P, 1])
        flat = m.sb("flat", [P, CT, C])
        pair = m.sb("pair", [P, CT, 2 * C])
        xT = m.sb("xT", [P, CH], F32R)
        logits = m.sb("logits", [P, TILES, NE])
        top = m.sb("top", [P, TILES])
        prob = m.sb("prob", [P, TILES, NE])
        total = m.sb("total", [P, TILES])
        above = m.sb("above", [P, TILES, NE, NE])
        level = m.sb("level", [P, TILES, NE, NE])
        earlier = m.sb("earlier", [P, NE, NE])
        rank = m.sb("rank", [P, TILES, NE])
        pT = m.ps("pT", [P, 512])
        pL = m.ps("pL", [P, 512])

        weights_in = m.sem("weights_in")
        ms_made = m.sem("ms_made")
        root_made = m.sem("root_made")
        split_done = m.sem("split_done")
        pair_made = m.sem("pair_made")
        xT_ready = m.sem("xT_ready")
        xT_made = m.sem("xT_made")
        fT_made = m.sem("fT_made")
        logits_ready = m.sem("logits_ready")
        logits_made = m.sem("logits_made")
        margin_made = m.sem("margin_made")
        exp_made = m.sem("exp_made")
        dve_chain = m.sem("dve_chain")
        pe_gate, dve_gate, pool_gate = (m.sem(f"{e}_gate") for e in ("pe", "dve", "pool"))
        block = ctx.enter_context(nc.Block())
        N = BATCH * CHUNKS

        @block.sync
        def _(sp):
            for half in (0, C):
                sp.dma_start(rraw[half:half + C, :], d["router"]).then_inc(weights_in, 16)
                sp.dma_start(ln2[half:half + C, :], d["ln2_w"]).then_inc(weights_in, 16)
            sp.dma_start(earlier[:], d["earlier"]).then_inc(weights_in, 16)

        @block.scalar
        def _(act):
            act.wait_ge(ms_made, 1)
            act.activation(root[:], ms[:], ACT.Sqrt).then_inc(root_made, 1)
            act.wait_ge(margin_made, 1)
            act.activation(prob[:], prob[:], ACT.Exp).then_inc(exp_made, 1)

        @block.tensor
        def _(pe):
            pe.wait_ge(split_done, 1)
            with pe.Fori(0, N) as n:
                pe.wait_ge(pair_made, n + 1)
                for t in range(CT):
                    last = pe.transpose(pT[:, t * P:(t + 1) * P], pair[:, t, :], ident[:])
                last.then_inc(xT_ready, 1)
                pe.wait_ge(xT_made, n + 1)
                pe.wait_ge(logits_made, n + 1)
                for t in range(CT):
                    for w in (rhi, rlo):
                        last = pe.matmul(pL[:, t * NE:(t + 1) * NE], xT[:, t * P:(t + 1) * P], w[:],
                                         start=w is rhi, stop=w is rlo)
                last.then_inc(logits_ready, 1)

        @block.gpsimd
        def _(pool):
            pool.sem_inc(fT_made, 1)
            with pool.Fori(0, N) as n:
                pool.wait_ge(xT_made, n + 1)
                pool.sem_inc(pool_gate, 1)
                pool.tensor_copy(fT[:, bass.ds(n * CH, CH)], xT[:].bitcast(F32)).then_inc(fT_made, 1)

        @block.vector
        def _(dve):
            chain = Chain(dve, dve_chain)
            dve.sem_inc(logits_made, 1)
            dve.wait_ge(weights_in, 80)
            chain.then(dve.tensor_scalar(rraw[:], rraw[:], ln2[:, 0:1], None, ALU.mult))
            chain.ready()
            split_weights(dve, chain, rraw[:], rhi[:], rlo[:])
            chain.ready()
            dve.sem_inc(split_done, 1)
            chain.then(dve.tensor_tensor(square[:], X3[:], X3[:], ALU.mult))
            chain.ready()
            chain.then(dve.tensor_reduce(ms[:], square[:], AX.X, ALU.add))
            chain.ready()
            dve.tensor_scalar(ms[:], ms[:], 1.0 / C, RMS_EPS, ALU.mult, ALU.add).then_inc(ms_made, 1)
            dve.wait_ge(root_made, 1)
            chain.then(dve.reciprocal(inv[:], root[:]))
            chain.ready()
            before = chain.n
            with dve.Fori(0, N) as n:
                chain.enter(n * 2 + before)
                tiles = bass.ds(n * CT, CT)
                chain.then(dve.tensor_tensor(flat[:], X3[:, tiles, :], bcast(inv[:, tiles], 2, C), ALU.mult))
                chain.ready()
                chain.then(dve.tensor_copy(pair[:, :, 0:C].bitcast(F32R), flat[:]))
                chain.ready()
                dve.tensor_tensor(pair[:, :, C:2 * C], flat[:], pair[:, :, 0:C], ALU.subtract).then_inc(pair_made, 1)
                dve.wait_ge(xT_ready, n + 1)
                dve.wait_ge(fT_made, n + 1)
                dve.sem_inc(dve_gate, 1)
                dve.tensor_copy(xT[:], pT[:]).then_inc(xT_made, 1)
                dve.wait_ge(logits_ready, n + 1)
                dve.sem_inc(dve_gate, 1)
                dve.tensor_copy(logits[:, tiles, :], pL[:, 0:CT * NE].rearrange("p (t e) -> p t e", e=NE)) \
                    .then_inc(logits_made, 1)
                chain.leave(2, N)
            dve.wait_ge(logits_made, N + 1)
            chain.then(dve.tensor_reduce(top[:], logits[:], AX.X, ALU.max))
            chain.ready()
            dve.tensor_tensor(prob[:], logits[:], bcast(top[:], 2, NE), ALU.subtract).then_inc(margin_made, 1)
            dve.wait_ge(exp_made, 1)
            chain.then(dve.tensor_reduce(total[:], prob[:], AX.X, ALU.add))
            chain.ready()
            chain.then(dve.reciprocal(total[:], total[:]))
            chain.ready()
            chain.then(dve.tensor_tensor(prob[:], prob[:], bcast(total[:], 2, NE), ALU.mult))
            chain.ready()
            chain.then(dve.tensor_tensor(above[:], bcast(prob[:], 2, NE), bcast(prob[:], 3, NE), ALU.is_gt))
            chain.then(dve.tensor_tensor(level[:], bcast(prob[:], 2, NE), bcast(prob[:], 3, NE), ALU.is_ge))
            chain.ready()
            chain.then(dve.tensor_tensor(level[:].rearrange("p t a b -> p t (a b)"),
                                         level[:].rearrange("p t a b -> p t (a b)"),
                                         bcast(earlier[:].rearrange("p a b -> p (a b)"), 1, TILES), ALU.mult))
            chain.ready()
            chain.then(dve.tensor_tensor(above[:], above[:], level[:], ALU.max))
            chain.ready()
            chain.then(dve.tensor_reduce(rank[:], above[:], AX.X, ALU.add))
            chain.ready()
            chain.then(dve.tensor_scalar(rank[:], rank[:], TOPK - 0.5, None, ALU.is_lt))
            chain.ready()
            chain.then(dve.tensor_tensor(prob[:], prob[:], rank[:], ALU.mult))
            chain.ready()
            chain.then(dve.tensor_reduce(total[:], prob[:], AX.X, ALU.add))
            chain.ready()
            chain.then(dve.tensor_scalar(total[:], total[:], 1e-9, None, ALU.add))
            chain.ready()
            chain.then(dve.reciprocal(total[:], total[:]))
            chain.ready()
            chain.then(dve.tensor_tensor(weight[:], prob[:], bcast(total[:], 2, NE), ALU.mult))
            chain.ready()


def hidden_blocks():
    out = []
    for m in range(HM):
        rows = min(P, HIDDEN - m * P)
        out.append((rows, m * P // EHID, (m * P + rows - 1) // EHID + 1))
    return out


def experts(nc, d, H, X3, fT, weight, out):
    LAG = 2
    blocks = hidden_blocks()
    starts = np.cumsum([0] + [(e1 - e0) * C for _, e0, e1 in blocks])
    with ExitStack() as ctx:
        m = Scope(nc, ctx, "ex")
        raw = m.sb("raw", [P, HIDDEN])
        w1hi = m.sb("w1hi", [P, HIDDEN], F32R)
        w1lo = m.sb("w1lo", [P, HIDDEN], F32R)
        w3hi = m.sb("w3hi", [P, HIDDEN], F32R)
        w3lo = m.sb("w3lo", [P, HIDDEN], F32R)
        w2 = m.sb("w2", [P, int(starts[-1])])
        ln2 = m.sb("ln2", [P, 1])
        act1 = m.sb("act1", [P, 2, CH])
        hidden = m.sb("hidden", [P, HM, CH])
        scaled = m.sb("scaled", [P, 2, NE, C])
        mixed = m.sb("mixed", [P, CT, C])
        pA = m.ps("pA", [P, 2, 512])
        pB = m.ps("pB", [P, 2, 512])
        pY = m.ps("pY", [P, CT, 512])

        raw_in = [m.sem("raw_in0"), m.sem("raw_in1")]
        weights_in = m.sem("weights_in")
        first_split = m.sem("first_split")
        split_done = m.sem("split_done")
        x3_added = m.sem("x3_added")
        a_ready = m.sem("a_ready")
        b_ready = m.sem("b_ready")
        act1_made = m.sem("act1_made")
        hidden_made = m.sem("hidden_made")
        hidden_used = m.sem("hidden_used")
        y_ready = m.sem("y_ready")
        y_scaled = m.sem("y_scaled")
        out_made = m.sem("out_made")
        stored = m.sem("stored")
        dve_chain = m.sem("dve_chain")
        pe_gate, act_gate, dve_gate, sp_gate = (m.sem(f"{e}_gate") for e in ("pe", "act", "dve", "sp"))
        block = ctx.enter_context(nc.Block())
        N = BATCH * CHUNKS

        @block.sync
        def _(sp):
            for half in (0, C):
                sp.dma_start(raw[half:half + C, :], d["w1"]).then_inc(raw_in[0], 16)
                sp.dma_start(ln2[half:half + C, :], d["ln2_w"]).then_inc(raw_in[0], 16)
            sp.dma_start(w2[:], d["w2"]).then_inc(weights_in, 16)
            sp.wait_ge(first_split, 1)
            for half in (0, C):
                sp.dma_start(raw[half:half + C, :], d["w3"]).then_inc(raw_in[1], 16)
            rows = out.rearrange("b (t p) c -> p (b t) c", p=P)
            with sp.Fori(0, N) as n:
                sp.wait_ge(out_made, n + 1)
                sp.sem_inc(sp_gate, 1)
                sp.dma_start(rows[:, bass.ds(n * CT, CT), :], H[:, bass.ds(n * CT, CT), :]).then_inc(stored, 16)
            sp.wait_ge(stored, 16 * N)

        @block.gpsimd
        def _(pool):
            pool.tensor_tensor(H[:], H[:], X3[:], ALU.add).then_inc(x3_added, 1)

        @block.tensor
        def _(pe):
            def gated_wait(sem, value):
                pe.wait_ge(sem, value)
                pe.sem_inc(pe_gate, 1)

            pe.sem_inc(hidden_used, 1)
            pe.wait_ge(split_done, 1)
            pe.wait_ge(weights_in, 16)
            with pe.Fori(0, N) as n:
                rhs = fT[:, bass.ds(n * CH, CH)]

                def project(k):
                    rows = blocks[k][0]
                    cols = slice(k * P, k * P + rows)
                    gated_wait(act1_made, n * HM + (k + 1))
                    for w in (w1hi, w1lo):
                        last = pe.matmul(pA[0:rows, k % 2, :], w[:, cols], rhs, start=w is w1hi, stop=w is w1lo)
                    last.then_inc(a_ready, 1)
                    gated_wait(hidden_made, n * HM + (k + 1))
                    for w in (w3hi, w3lo):
                        last = pe.matmul(pB[0:rows, k % 2, :], w[:, cols], rhs, start=w is w3hi, stop=w is w3lo)
                    last.then_inc(b_ready, 1)

                def reduce(k):
                    rows, e0, e1 = blocks[k]
                    gated_wait(hidden_made, n * HM + (k + 3))
                    for t in range(CT):
                        if k == 0:
                            gated_wait(y_scaled, n * CT + (t + 1))
                        last = pe.matmul(pY[:, t, e0 * C:e1 * C], hidden[0:rows, k, t * P:(t + 1) * P],
                                         w2[0:rows, int(starts[k]):int(starts[k + 1])], start=k == 0,
                                         stop=k == HM - 1, skip_group_check=True)
                        if k == HM - 1:
                            last.then_inc(y_ready, 1)

                for k in range(HM + LAG):
                    if k < HM:
                        project(k)
                    if k >= LAG:
                        reduce(k - LAG)
                gated_wait(y_ready, n * CT + CT)
                pe.sem_inc(hidden_used, 1)

        @block.scalar
        def _(act):
            act.sem_inc(act1_made, 2)
            with act.Fori(0, N) as n:
                for k in range(HM):
                    rows = blocks[k][0]
                    act.wait_ge(a_ready, n * HM + (k + 1))
                    act.wait_ge(hidden_made, n * HM + (k + 1))
                    act.activation(act1[0:rows, k % 2, :], pA[0:rows, k % 2, :], ACT.Silu).then_inc(act1_made, 1)

        @block.vector
        def _(dve):
            chain = Chain(dve, dve_chain)
            dve.sem_inc(hidden_made, 2)
            dve.sem_inc(y_scaled, CT)
            for r, (hi, lo) in enumerate(((w1hi, w1lo), (w3hi, w3lo))):
                dve.wait_ge(raw_in[r], 64 if r == 0 else 32)
                chain.then(dve.tensor_scalar(raw[:], raw[:], ln2[:, 0:1], None, ALU.mult))
                chain.ready()
                split_weights(dve, chain, raw[:], hi[:], lo[:])
                chain.ready()
                dve.sem_inc(first_split if r == 0 else split_done, 1)
            dve.wait_ge(x3_added, 1)
            before = chain.n
            with dve.Fori(0, N) as n:
                chain.enter(n * CT + before)
                for k in range(HM):
                    rows = blocks[k][0]
                    dve.wait_ge(b_ready, n * HM + (k + 1))
                    dve.wait_ge(act1_made, n * HM + (k + 3))
                    if k == 0:
                        dve.wait_ge(hidden_used, n + 1)
                        dve.sem_inc(dve_gate, 1)
                    dve.tensor_tensor(hidden[0:rows, k, :], pB[0:rows, k % 2, :], act1[0:rows, k % 2, :],
                                      ALU.mult).then_inc(hidden_made, 1)
                for t in range(CT):
                    dve.wait_ge(y_ready, n * CT + (t + 1))
                    dve.sem_inc(dve_gate, 1)
                    by_expert = bcast(weight[:, bass.ds(n * CT + t, 1), :].rearrange("p a e -> p (a e)"), 2, C)
                    dve.tensor_tensor(scaled[:, t % 2, :, :], pY[:, t, :].rearrange("p (e c) -> p e c", c=C),
                                      by_expert, ALU.mult).then_inc(y_scaled, 1)
                    dve.wait_ge(y_scaled, n * CT + (t + 1 + CT))
                    chain.then(dve.tensor_reduce(mixed[:, t, :], scaled[:, t % 2, :, :].rearrange("p e c -> p c e"),
                                                 AX.X, ALU.add))
                chain.ready()
                dve.sem_inc(dve_gate, 1)
                tiles = bass.ds(n * CT, CT)
                dve.tensor_tensor(H[:, tiles, :], H[:, tiles, :], mixed[:], ALU.add).then_inc(out_made, 1)
                chain.leave(CT, N)


_OUT = ("out", (BATCH, SEQ, C))


def program(nc, d, out):
    with ExitStack() as ctx:
        m = Scope(nc, ctx, "all")
        H = m.sb("H", [P, TILES, C])
        XC = m.sb("XC", [P, TILES, C])
        scale = m.sb("scale", [P, TILES])
        ident = m.sb("ident", [P, P])
        identb = m.sb("identb", [P, P], BF16)
        rawmasks = m.sb("rawmasks", [P, 2, P])
        masks = m.sb("masks", [P, 2, P], BF16)
        consts_in = m.sem("consts_in")
        with nc.Block() as block:
            @block.sync
            def _(sp):
                sp.dma_start(ident[:], d["ident"]).then_inc(consts_in, 16)
                sp.dma_start(rawmasks[:], d["masks"]).then_inc(consts_in, 16)

            @block.vector
            def _(dve):
                dve.wait_ge(consts_in, 32)
                dve.tensor_copy(identb[:], ident[:])
                dve.tensor_copy(masks[:], rawmasks[:])
        token_embedding(nc, d, H, XC, scale)
        gated_attention(nc, d, H, XC, scale, ident)
        normed_input(nc, H, XC, XC, scale)
        causal_attention(nc, d, XC, scale, ident, identb, masks)
        with ExitStack() as late:
            r = Scope(nc, late, "moe")
            fT = r.sb("fT", [P, BATCH * SEQ], F32R)
            weight = r.sb("weight", [P, TILES, NE])
            routing(nc, d, XC, ident, fT, weight)
            experts(nc, d, H, XC, fT, weight, out)


def down_blocks(w2):
    rows = np.ascontiguousarray(w2.transpose(0, 2, 1)).reshape(HIDDEN, C)
    parts = []
    for k, (n, e0, e1) in enumerate(hidden_blocks()):
        for e in range(e0, e1):
            block = np.zeros((P, C), np.float32)
            a, b = max(k * P, e * EHID), min(k * P + n, (e + 1) * EHID)
            block[a - k * P:b - k * P] = rows[a:b]
            parts.append(block)
    return np.ascontiguousarray(np.concatenate(parts, axis=1))


def shape_constants():
    freq = 1.0 / 10000.0 ** (np.arange(0, HD, 2, dtype=np.float32) / HD)
    angle = np.outer(np.arange(SEQ, dtype=np.float32), freq)
    angle = np.concatenate([angle, angle], axis=-1)
    cos, sin = np.cos(angle).astype(np.float32), np.sin(angle).astype(np.float32)
    sin[:, :HD // 2] *= -1
    row, col = np.arange(P)[:, None], np.arange(P)[None, :]
    masks = np.stack([np.where(row > col, np.float32(-1e30), np.float32(0)),
                      np.where(col > row, np.float32(-1e30), np.float32(0))], axis=1)
    tiled = [np.ascontiguousarray(t.reshape(BT, P, HD).transpose(1, 0, 2)) for t in (cos, sin)]
    earlier = np.tril(np.ones((NE, NE), np.float32), -1)
    return {"earlier": np.ascontiguousarray(np.broadcast_to(earlier, (P, NE, NE))), "cos": tiled[0], "sin": tiled[1], "masks": np.ascontiguousarray(masks.astype(np.float32))}


def kernel(x, L0_tok_bases, L0_tok_W_spline, L0_tok_b_spline, L0_tok_W_base, L0_tok_b_base, L0_attn_g,
           L0_attn_W_uv, L0_attn_b_uv, L0_attn_gamma, L0_attn_beta, L0_attn_W_o, L0_attn_b_o, L0_ffn_ln1_w,
           L0_ffn_ln2_w, L0_ffn_wq, L0_ffn_wk, L0_ffn_wv, L0_ffn_wo, L0_ffn_router_w, L0_ffn_w1, L0_ffn_w2,
           L0_ffn_w3):
    import concourse.bacc as bacc
    from concourse.bass_utils import run_bass_kernel_spmd as run

    asc = np.ascontiguousarray
    bases, ws = np.asarray(L0_tok_bases), np.asarray(L0_tok_W_spline).reshape(C, C, 3)
    one = np.ones((C, 1), np.float32)
    wb = np.asarray(L0_tok_W_base)
    arrays = {
        "x": asc(np.asarray(x).reshape(BATCH, C, SEQ)),
        "wtok": asc(np.stack([np.concatenate([wb.T, ws[:, :, 0].T]),
                              np.concatenate([ws[:, :, 1].T, ws[:, :, 2].T])], axis=1)),
        "tok_factor": asc(np.concatenate([np.concatenate([one, bases[:, 0:1]]),
                                          np.concatenate([bases[:, 1:2], bases[:, 2:3]])], axis=1)),
        "b_base": asc(L0_tok_b_base), "b_spline": asc(L0_tok_b_spline),
        "g": asc(np.asarray(L0_attn_g).reshape(1)),
        "W_uv": asc(L0_attn_W_uv), "b_uv": asc(L0_attn_b_uv),
        "ga_cols": asc(np.concatenate([np.asarray(L0_attn_b_uv).reshape(3, GH), np.asarray(L0_attn_gamma),
                                       np.asarray(L0_attn_beta)]).T),
        "W_o": asc(L0_attn_W_o), "b_o": asc(L0_attn_b_o),
        "wqkv": asc(np.concatenate([np.asarray(L0_ffn_wq), np.asarray(L0_ffn_wk), np.asarray(L0_ffn_wv)]).T),
        "wo": asc(np.asarray(L0_ffn_wo).T), "ln1_w": asc(np.asarray(L0_ffn_ln1_w).reshape(C, 1)),
        "ident": np.eye(P, dtype=np.float32),
        "router": asc(np.asarray(L0_ffn_router_w).T), "ln2_w": asc(np.asarray(L0_ffn_ln2_w).reshape(C, 1)),
        "w1": asc(np.asarray(L0_ffn_w1).reshape(HIDDEN, C).T), "w3": asc(np.asarray(L0_ffn_w3).reshape(HIDDEN, C).T),
        "w2": down_blocks(np.asarray(L0_ffn_w2)),
        **shape_constants(),
    }
    nc = bacc.Bacc("TRN2", target_bir_lowering=False, num_devices=1)
    d = {name: nc.dram_tensor(name, a.shape, mybir.dt.from_np(a.dtype), kind="ExternalInput").ap()
         for name, a in arrays.items()}
    out = nc.dram_tensor(_OUT[0], _OUT[1], F32, kind="ExternalOutput").ap()
    program(nc, d, out)
    r = run(nc, [arrays], core_ids=[0])
    return r.results[0]["out"]
```

```python
from contextlib import ExitStack

import numpy as np

import concourse.bass as bass
from concourse import mybir

F32 = mybir.dt.float32
F32R = mybir.dt.float32r
BF16 = mybir.dt.bfloat16
ALU = mybir.AluOpType
ACT = mybir.ActivationFunctionType
AX = mybir.AxisListType

P = 128
BATCH, SEQ, C = 2, 4096, 64
TILES = BATCH * SEQ // P
BT = SEQ // P
CH = 512
CT = CH // P
CHUNKS = SEQ // CH
GH = 128
NH, NKV, HD = 4, 2, 16
QKV = (NH + 2 * NKV) * HD
ROPED = (NH + NKV) * HD
Q_PARTS = (0, 0, 1, 0, 2, 1)
K_PARTS = (0, 1, 0, 2, 0, 1)
STACK = len(Q_PARTS) * HD
SHIFT = 3
VW = 32
NE, TOPK, EHID = 8, 2, 170
HIDDEN = NE * EHID
HM = -(-HIDDEN // P)
LN_EPS, RMS_EPS, NORM_EPS = 1e-5, 1e-6, 1e-5


def bcast(ap, axis, n):
    a = ap.unsqueeze(axis)
    shape = list(a.shape)
    shape[axis] = n
    return a.broadcast_to(shape)


class Chain:

    def __init__(self, eng, sem):
        self.eng, self.sem, self.n, self.base = eng, sem, 0, None

    def then(self, ins):
        ins.then_inc(self.sem, 1)
        self.n += 1

    def ready(self):
        self.eng.wait_ge(self.sem, self.n if self.base is None else self.base + self.n)

    def enter(self, base):
        self.outer, self.base, self.n = self.n, base, 0

    def leave(self, per, times):
        assert self.n == per, self.n
        self.base, self.n = None, self.outer + per * times


class Scope:

    def __init__(self, nc, ctx, tag):
        self.nc, self.ctx, self.tag = nc, ctx, tag

    def sb(self, name, shape, dt=F32):
        return self.ctx.enter_context(self.nc.sbuf_tensor(f"{self.tag}.{name}", shape, dt))

    def ps(self, name, shape, dt=F32):
        return self.ctx.enter_context(self.nc.psum_tensor(f"{self.tag}.{name}", shape, dt))

    def sem(self, name):
        return self.ctx.enter_context(self.nc.semaphore(f"{self.tag}.{name}"))


def token_embedding(nc, d, H, XC, scale):
    W = 1024
    WT = W // P
    STEPS = SEQ // W
    with ExitStack() as ctx:
        m = Scope(nc, ctx, "tok")
        x2 = m.sb("x2", [P, BATCH, SEQ])
        wtok = m.sb("wtok", [P, 2, C])
        factor = m.sb("factor", [P, 2])
        biases = m.sb("biases", [P, 2, C])
        bias = m.sb("bias", [P, C])
        g = m.sb("g", [P, 1])
        feat = m.sb("feat", [P, 2, 2, W])
        square = m.sb("square", [P, TILES, C])
        sums = m.sb("sums", [P, TILES])
        mean = m.sb("mean", [P, TILES])
        var = m.sb("var", [P, TILES])
        shifted = m.sb("shifted", [P, TILES])
        root = m.sb("root", [P, 2, TILES])
        inv = m.sb("inv", [P, TILES])
        norm = m.sb("norm", [P, TILES])
        pH = m.ps("pH", [P, 2, 512])

        weights_in = m.sem("weights_in")
        x_in = [m.sem("x_in0"), m.sem("x_in1")]
        sigmoids_made = m.sem("sigmoids_made")
        silu_made = m.sem("silu_made")
        feat_free = m.sem("feat_free")
        h_ready = m.sem("h_ready")
        h_free = m.sem("h_free")
        var_made = m.sem("var_made")
        roots_made = m.sem("roots_made")
        dve_chain = m.sem("dve_chain")
        block = ctx.enter_context(nc.Block())

        @block.sync
        def _(sp):
            for b in range(BATCH):
                for half in (0, C):
                    sp.dma_start(x2[half:half + C, b, :], d["x"][b]).then_inc(x_in[b], 16)

        @block.scalar
        def _(act):
            act.dma_start(wtok[:], d["wtok"]).then_inc(weights_in, 16)
            act.dma_start(factor[:], d["tok_factor"]).then_inc(weights_in, 16)
            act.dma_start(biases[:, 0, :], d["b_base"].partition_broadcast(P)).then_inc(weights_in, 16)
            act.dma_start(biases[:, 1, :], d["b_spline"].partition_broadcast(P)).then_inc(weights_in, 16)
            act.dma_start(g[:], d["g"].partition_broadcast(P)).then_inc(weights_in, 16)
            act.wait_ge(weights_in, 80)
            for b in range(BATCH):
                act.wait_ge(x_in[b], 32)
                with act.Fori(0, STEPS // 2) as i:
                    for j in range(2):
                        act.wait_ge(feat_free, 2 * i + (STEPS * b + j + 1))
                        for f in range(2):
                            act.activation(feat[:, j, f, :], x2[:, b, bass.ds(i * (2 * W) + j * W, W)],
                                           ACT.Sigmoid, scale=factor[:, f:f + 1]).then_inc(sigmoids_made, 1)
            act.wait_ge(var_made, 1)
            act.activation(root[:, 0, :], shifted[:], ACT.Sqrt).then_inc(roots_made, 1)
            act.activation(root[:, 1, :], var[:], ACT.Sqrt).then_inc(roots_made, 1)

        @block.tensor
        def _(pe):
            pe.sem_inc(feat_free, 2)
            pe.wait_ge(weights_in, 80)
            with pe.Fori(0, BATCH * STEPS // 2) as i:
                for j in range(2):
                    pe.wait_ge(silu_made, 2 * i + (j + 1))
                    pe.wait_ge(sigmoids_made, 4 * i + (2 * j + 2))
                    pe.wait_ge(h_free, 2 * i + (j + 1))
                    for t in range(WT):
                        for f in range(2):
                            last = pe.matmul(pH[:, j, t * C:(t + 1) * C], feat[:, j, f, t * P:(t + 1) * P],
                                             wtok[:, f, :], start=f == 0, stop=f == 1)
                    last.then_inc(h_ready, 1)
                    pe.wait_ge(h_ready, 2 * i + (j + 1))
                    pe.sem_inc(feat_free, 1)

        @block.gpsimd
        def _(pool):
            for b in range(BATCH):
                with pool.Fori(0, STEPS // 2) as i:
                    for j in range(2):
                        pool.wait_ge(sigmoids_made, 4 * i + (2 * STEPS * b + 2 * j + 1))
                        pool.tensor_tensor(feat[0:C, j, 0, :], feat[0:C, j, 0, :],
                                           x2[0:C, b, bass.ds(i * (2 * W) + j * W, W)],
                                           ALU.mult).then_inc(silu_made, 1)

        @block.vector
        def _(dve):
            chain = Chain(dve, dve_chain)
            dve.sem_inc(h_free, 2)
            dve.wait_ge(weights_in, 80)
            chain.then(dve.tensor_tensor(bias[:], biases[:, 0, :], biases[:, 1, :], ALU.add))
            chain.ready()
            with dve.Fori(0, BATCH * STEPS // 2) as i:
                for j in range(2):
                    dve.wait_ge(h_ready, 2 * i + (j + 1))
                    dve.tensor_tensor(H[:, bass.ds(i * (2 * WT) + j * WT, WT), :],
                                      pH[:, j, :].rearrange("p (t c) -> p t c", c=C),
                                      bcast(bias[:], 1, WT), ALU.add).then_inc(h_free, 1)
            dve.wait_ge(h_free, BATCH * STEPS + 2)
            centre(dve, chain, H, XC, square, sums, mean, var)
            chain.ready()
            dve.tensor_scalar(shifted[:], var[:], LN_EPS, None, ALU.add).then_inc(var_made, 1)
            dve.wait_ge(roots_made, 2)
            chain.then(dve.reciprocal(inv[:], root[:, 0, :]))
            chain.ready()
            chain.then(dve.tensor_tensor(norm[:], root[:, 1, :], inv[:], ALU.mult))
            chain.ready()
            chain.then(dve.tensor_scalar(norm[:], norm[:], NORM_EPS, None, ALU.max))
            chain.ready()
            chain.then(dve.reciprocal(norm[:], norm[:]))
            chain.ready()
            chain.then(dve.scalar_tensor_tensor(out=scale[:], in0=norm[:], scalar=g[:, 0:1], in1=inv[:],
                                                op0=ALU.mult, op1=ALU.mult))
            chain.ready()


def centre(dve, chain, H, XC, square, sums, mean, var):
    chain.then(dve.tensor_reduce(sums[:], H[:], AX.X, ALU.add))
    chain.ready()
    chain.then(dve.tensor_scalar(mean[:], sums[:], 1.0 / C, None, ALU.mult))
    chain.ready()
    chain.then(dve.tensor_tensor(XC[:], H[:], bcast(mean[:], 2, C), ALU.subtract))
    chain.ready()
    chain.then(dve.tensor_tensor(square[:], XC[:], XC[:], ALU.mult))
    chain.ready()
    chain.then(dve.tensor_reduce(sums[:], square[:], AX.X, ALU.add))
    chain.ready()
    chain.then(dve.tensor_scalar(var[:], sums[:], 1.0 / C, None, ALU.mult))


def split_weights(dve, chain, raw, hi, lo):
    chain.then(dve.tensor_copy(hi, raw))
    chain.ready()
    chain.then(dve.tensor_tensor(lo, raw, hi.bitcast(F32), ALU.subtract))


def split_rows(dve, chain, src, pair):
    chain.then(dve.tensor_copy(pair[:, :, 0:C].bitcast(F32R), src))
    chain.ready()
    chain.then(dve.tensor_tensor(pair[:, :, C:2 * C], src, pair[:, :, 0:C], ALU.subtract))


def gated_attention(nc, d, H, XC, scale, ident):
    PAIRS = BT // 2
    AHEAD = 3
    SLOTS = 4
    LASTQ = CHUNKS - 1
    with ExitStack() as ctx:
        m = Scope(nc, ctx, "ga")
        wraw = m.sb("wraw", [P, 3 * GH])
        whi = m.sb("whi", [P, 3 * GH], F32R)
        wlo = m.sb("wlo", [P, 3 * GH], F32R)
        wo = m.sb("wo", [GH, C])
        cols = m.sb("cols", [P, 7])
        bcol, gb = cols[:, 0:3], cols[:, 3:7]
        warm = m.sb("warm", [P, 1])
        bv = m.sb("bv", [P, GH])
        bo = m.sb("bo", [P, C])
        xn = m.sb("xn", [P, CT, C])
        pair = m.sb("pair", [P, CT, 2 * C])
        qhi = m.sb("qhi", [P, SEQ], F32R)
        qlo = m.sb("qlo", [P, SEQ], F32R)
        khi = m.sb("khi", [P, SEQ], F32R)
        klo = m.sb("klo", [P, SEQ], F32R)
        Vhi = m.sb("Vhi", [P, BT, GH], F32R)
        Vlo = m.sb("Vlo", [P, BT, GH], F32R)
        uT = m.sb("uT", [P, SEQ])
        attn = m.sb("attn", [P, 2, 2 * CH])
        attn_hi = m.sb("attn_hi", [P, SLOTS, 2 * CH], F32R)
        attn_lo = m.sb("attn_lo", [P, 2, 2 * CH], F32R)
        gated = m.sb("gated", [P, CH])
        xT = attn_hi[:, 0, 0:CH]
        base, vb = attn[:, 0, 0:CH], attn[:, 0, CH:2 * CH].rearrange("p (t c) -> p t c", c=GH)
        q, k = attn[:, 1, 0:CH], attn[:, 1, CH:2 * CH]
        vs = gated[:].rearrange("p (t c) -> p t c", c=GH)
        pS = m.ps("pS", [P, 4, 512])
        pO = m.ps("pO", [P, 512])
        pY = m.ps("pY", [P, 512])
        pBase, pU, pV, pT = pS[:, 0, :], pS[:, 1, :], pS[:, 2, :], pS[:, 3, :]

        weights_in = m.sem("weights_in")
        split_done = m.sem("split_done")
        pair_made = m.sem("pair_made")
        xT_ready = m.sem("xT_ready")
        xT_made = m.sem("xT_made")
        base_ready = m.sem("base_ready")
        u_ready = m.sem("u_ready")
        v_ready = m.sem("v_ready")
        vb_made = m.sem("vb_made")
        vs_made = m.sem("vs_made")
        vhi_made = m.sem("vhi_made")
        vlo_made = m.sem("vlo_made")
        base_made = m.sem("base_made")
        u_made = m.sem("u_made")
        q_made = m.sem("q_made")
        qhi_made = m.sem("qhi_made")
        qlo_made = m.sem("qlo_made")
        k_made = m.sem("k_made")
        scores_ready = m.sem("scores_ready")
        squared = m.sem("squared")
        relu_made = m.sem("relu_made")
        hi_made = m.sem("hi_made")
        lo_made = m.sem("lo_made")
        pairs_summed = m.sem("pairs_summed")
        gated_made = m.sem("gated_made")
        y_ready = m.sem("y_ready")
        h_made = m.sem("h_made")
        bo_added = m.sem("bo_added")
        dve_chain = m.sem("dve_chain")
        pool_chain = m.sem("pool_chain")
        pe_gate, act_gate, dve_gate, pool_gate = (m.sem(f"{e}_gate") for e in ("pe", "act", "dve", "pool"))
        block = ctx.enter_context(nc.Block())

        @block.sync
        def _(sp):
            for half in (0, C):
                sp.dma_start(wraw[half:half + C, :], d["W_uv"]).then_inc(weights_in, 16)
            sp.dma_start(wo[:], d["W_o"]).then_inc(weights_in, 16)
            sp.dma_start(cols[:], d["ga_cols"]).then_inc(weights_in, 16)
            sp.dma_start(bv[:], d["b_uv"][GH:2 * GH].partition_broadcast(P)).then_inc(weights_in, 16)
            sp.dma_start(bo[:], d["b_o"].partition_broadcast(P)).then_inc(weights_in, 16)

        @block.tensor
        def _(pe):
            def gated_wait(sem, value):
                pe.wait_ge(sem, value)
                pe.sem_inc(pe_gate, 1)

            pe.wait_ge(weights_in, 96)
            pe.wait_ge(split_done, 1)
            with pe.Fori(0, BATCH) as b:
                n0 = b * CHUNKS

                def turn(c):
                    gated_wait(pair_made, n0 + c + 1)
                    gated_wait(xT_made, n0 + c + 1)
                    for t in range(CT):
                        last = pe.transpose(pT[:, t * P:(t + 1) * P], pair[:, t, :], ident[:])
                    last.then_inc(xT_ready, 1)

                def project_rows(out, col, ready):
                    for w in (whi, wlo):
                        last = pe.matmul(out, w[:, col:col + GH], xT, start=w is whi, stop=w is wlo)
                    last.then_inc(ready, 1)

                def project_base_u(c):
                    gated_wait(xT_made, n0 + c + 2)
                    gated_wait(u_made, n0 + c + 1)
                    project_rows(pBase, 2 * GH, base_ready)
                    project_rows(pU, 0, u_ready)

                def project_v(c):
                    gated_wait(vb_made, n0 + c + 1)
                    for t in range(CT):
                        for w in (whi, wlo):
                            last = pe.matmul(pV[:, t * P:(t + 1) * P], xT[:, t * P:(t + 1) * P],
                                             w[:, GH:2 * GH], start=w is whi, stop=w is wlo)
                    last.then_inc(v_ready, 1)

                turn(0)
                with pe.Fori(0, LASTQ) as c:
                    project_base_u(c)
                    turn(c + 1)
                    project_v(c)
                project_base_u(LASTQ)
                project_v(LASTQ)

                gated_wait(qlo_made, n0 + (CHUNKS + 1))
                gated_wait(k_made, n0 + (CHUNKS + 1))
                gated_wait(vlo_made, n0 + (CHUNKS + 1))
                gated_wait(u_made, n0 + (CHUNKS + 1))

                def scores(qb, p):
                    gated_wait(relu_made, (n0 + qb) * PAIRS + (p + 1))
                    qs = slice(qb * CH, (qb + 1) * CH) if isinstance(qb, int) else bass.ds(qb * CH, CH)
                    for j in range(2):
                        kt = slice((2 * p + j) * P, (2 * p + j + 1) * P)
                        out = pS[:, 2 * (p % 2) + j, :]
                        pe.matmul(out, khi[:, kt], qhi[:, qs], start=True, stop=False)
                        pe.matmul(out, khi[:, kt], qlo[:, qs], start=False, stop=False)
                        last = pe.matmul(out, klo[:, kt], qhi[:, qs], start=False, stop=True)
                    last.then_inc(scores_ready, 1)

                def weigh_values(qb, p):
                    if p == 0:
                        gated_wait(gated_made, n0 + qb + 1)
                    for j in range(2):
                        gated_wait(lo_made, 2 * ((n0 + qb) * PAIRS) + (2 * p + j + 5))
                        hi = attn_hi[:, p % SLOTS, j * CH:(j + 1) * CH]
                        lo = attn_lo[:, p % 2, j * CH:(j + 1) * CH]
                        pe.matmul(pO[:], Vhi[:, 2 * p + j, :], hi, start=p == 0 and j == 0, stop=False)
                        pe.matmul(pO[:], Vlo[:, 2 * p + j, :], hi, start=False, stop=False)
                        last = pe.matmul(pO[:], Vhi[:, 2 * p + j, :], lo, start=False,
                                         stop=p == PAIRS - 1 and j == 1)
                    last.then_inc(pairs_summed, 1)

                def project_out(qb):
                    gated_wait(gated_made, n0 + qb + 2)
                    gated_wait(h_made, n0 + qb + 1)
                    for t in range(CT):
                        last = pe.matmul(pY[:, t * C:(t + 1) * C], gated[:, t * P:(t + 1) * P], wo[:],
                                         start=True, stop=True)
                    last.then_inc(y_ready, 1)

                def query_block(qb, last):
                    for p in range(PAIRS):
                        weigh_values(qb, p)
                        if p + AHEAD < PAIRS:
                            scores(qb, p + AHEAD)
                        elif not last:
                            scores(qb + 1, p + AHEAD - PAIRS)
                    project_out(qb)

                for p in range(AHEAD):
                    scores(0, p)
                with pe.Fori(0, LASTQ) as qb:
                    query_block(qb, False)
                query_block(LASTQ, True)

        @block.scalar
        def _(act):
            def gated_wait(sem, value):
                act.wait_ge(sem, value)
                act.sem_inc(act_gate, 1)

            act.sem_inc(u_made, 1)
            act.sem_inc(vs_made, 1)
            act.sem_inc(relu_made, 2)
            act.wait_ge(weights_in, 96)
            with act.Fori(0, BATCH) as b:
                act.activation(warm[:], cols[:, 0:1], ACT.Silu)
                with act.Fori(0, CHUNKS) as c:
                    n = b * CHUNKS + c
                    gated_wait(base_ready, n + 1)
                    gated_wait(q_made, n + 1)
                    gated_wait(k_made, n + 1)
                    act.activation(base, pBase, ACT.Silu, bias=bcol[:, 2:3]).then_inc(base_made, 1)
                    gated_wait(u_ready, n + 1)
                    act.activation(uT[:, bass.ds(c * CH, CH)], pU, ACT.Silu, bias=bcol[:, 0:1]).then_inc(u_made, 1)
                    gated_wait(q_made, n + 2)
                    act.activation(qhi[:, bass.ds(c * CH, CH)], q, ACT.Copy).then_inc(qhi_made, 1)
                    gated_wait(vb_made, n + 2)
                    gated_wait(vlo_made, n + 1)
                    act.activation(vs, vb, ACT.Silu).then_inc(vs_made, 1)
                    gated_wait(vs_made, n + 2)
                    act.activation(Vhi[:, bass.ds(c * CT, CT), :], vs, ACT.Copy).then_inc(vhi_made, 1)
                with act.Fori(0, CHUNKS * PAIRS // SLOTS) as i:
                    for slot in range(SLOTS):
                        g = (b * (CHUNKS * PAIRS // SLOTS) + i) * SLOTS + slot
                        gated_wait(scores_ready, g + 1)
                        gated_wait(lo_made, 2 * g + 2)
                        banks = pS[:, 2 * (slot % 2):2 * (slot % 2) + 2, :].rearrange("p j q -> p (j q)")
                        act.activation(attn[:, slot % 2, :], banks, ACT.Relu).then_inc(relu_made, 1)
                        gated_wait(relu_made, g + 3)
                        gated_wait(pairs_summed, g + 1)
                        act.activation(attn_hi[:, slot, :], attn[:, slot % 2, :], ACT.Square).then_inc(hi_made, 1)

        @block.gpsimd
        def _(pool):
            chain = Chain(pool, pool_chain)
            pool.sem_inc(k_made, 1)
            pool.sem_inc(pairs_summed, SLOTS)
            pool.wait_ge(weights_in, 96)
            pool.tensor_tensor(H[:], H[:], bcast(bo[:], 1, TILES), ALU.add).then_inc(bo_added, 1)
            with pool.Fori(0, BATCH) as b:
                with pool.Fori(0, CHUNKS) as c:
                    chain.enter((b * CHUNKS + c) * 2)
                    pool.wait_ge(base_made, b * CHUNKS + c + 1)
                    pool.sem_inc(pool_gate, 1)
                    chain.then(pool.tensor_scalar(k, base, gb[:, 1:2], gb[:, 3:4], ALU.mult, ALU.add))
                    chain.ready()
                    hi = khi[:, bass.ds(c * CH, CH)]
                    chain.then(pool.tensor_copy(hi, k))
                    chain.ready()
                    pool.tensor_tensor(klo[:, bass.ds(c * CH, CH)], k, hi.bitcast(F32),
                                       ALU.subtract).then_inc(k_made, 1)
                    chain.leave(2, 0)

        @block.vector
        def _(dve):
            chain = Chain(dve, dve_chain)

            def gated_wait(sem, value):
                dve.wait_ge(sem, value)
                dve.sem_inc(dve_gate, 1)

            for credit, many in ((vb_made, 1), (q_made, 1), (vlo_made, 1), (xT_made, 1), (lo_made, 4), (gated_made, 1), (h_made, 1)):
                dve.sem_inc(credit, many)
            dve.sem_inc(xT_ready, 1)
            dve.sem_inc(qlo_made, 1)
            dve.wait_ge(weights_in, 96)
            split_weights(dve, chain, wraw[:], whi[:], wlo[:])
            chain.ready()
            dve.sem_inc(split_done, 1)
            SPLITS = chain.n
            dve.wait_ge(bo_added, 1)
            with dve.Fori(0, BATCH) as b:
                n0 = b * CHUNKS

                def split(c):
                    chain.enter((n0 + c) * 2 + SPLITS)
                    tiles = bass.ds(b * BT + c * CT, CT)
                    chain.then(dve.tensor_tensor(xn[:], XC[:, tiles, :], bcast(scale[:, tiles], 2, C), ALU.mult))
                    gated_wait(xT_ready, n0 + c + 1)
                    chain.ready()
                    chain.then(dve.tensor_copy(pair[:, :, 0:C].bitcast(F32R), xn[:]))
                    chain.ready()
                    dve.tensor_tensor(pair[:, :, C:2 * C], xn[:], pair[:, :, 0:C],
                                      ALU.subtract).then_inc(pair_made, 1)
                    chain.leave(2, 0)

                def take_rows(c):
                    gated_wait(xT_ready, n0 + c + 2)
                    gated_wait(v_ready, n0 + c)
                    dve.tensor_copy(xT, pT).then_inc(xT_made, 1)

                def operands(c):
                    gated_wait(base_made, n0 + c + 1)
                    gated_wait(qlo_made, n0 + c + 1)
                    dve.tensor_scalar(q, base, gb[:, 0:1], gb[:, 2:3], ALU.mult, ALU.add).then_inc(q_made, 1)
                    gated_wait(v_ready, n0 + c + 1)
                    gated_wait(vs_made, n0 + c + 1)
                    dve.tensor_tensor(vb, pV.rearrange("p (t c) -> p t c", c=GH), bcast(bv[:], 1, CT),
                                      ALU.add).then_inc(vb_made, 1)

                def remainders(c):
                    gated_wait(qhi_made, n0 + c + 1)
                    own = bass.ds(c * CH, CH) if not isinstance(c, int) else slice(c * CH, (c + 1) * CH)
                    dve.tensor_tensor(qlo[:, own], q, qhi[:, own].bitcast(F32), ALU.subtract).then_inc(qlo_made, 1)
                    gated_wait(vhi_made, n0 + c + 1)
                    own = bass.ds(c * CT, CT) if not isinstance(c, int) else slice(c * CT, (c + 1) * CT)
                    dve.tensor_tensor(Vlo[:, own, :], vs, Vhi[:, own, :].bitcast(F32),
                                      ALU.subtract).then_inc(vlo_made, 1)

                split(0)
                take_rows(0)
                split(1)
                operands(0)
                with dve.Fori(1, LASTQ) as c:
                    take_rows(c)
                    split(c + 1)
                    remainders(c - 1)
                    operands(c)
                take_rows(LASTQ)
                remainders(LASTQ - 1)
                operands(LASTQ)
                remainders(LASTQ)

                def remainder(qb, p):
                    g = (n0 + qb) * PAIRS + p
                    gated_wait(hi_made, g + 1)
                    for j in range(2):
                        half = attn[:, p % 2, j * CH:(j + 1) * CH]
                        dve.tensor_tensor(half, half, half, ALU.mult).then_inc(squared, 1)
                    gated_wait(pairs_summed, g + (1 + SLOTS - 2))
                    for j in range(2):
                        own = slice(j * CH, (j + 1) * CH)
                        gated_wait(squared, 2 * g + (j + 1))
                        dve.tensor_tensor(attn_lo[:, p % 2, own], attn[:, p % 2, own],
                                          attn_hi[:, p % SLOTS, own].bitcast(F32), ALU.subtract).then_inc(lo_made, 1)

                def gate(qb):
                    gated_wait(pairs_summed, (n0 + qb) * PAIRS + (PAIRS + SLOTS))
                    own = bass.ds(qb * CH, CH) if not isinstance(qb, int) else slice(qb * CH, (qb + 1) * CH)
                    dve.scalar_tensor_tensor(out=gated[:], in0=pO[:], scalar=1.0 / GH, in1=uT[:, own],
                                             op0=ALU.mult, op1=ALU.mult).then_inc(gated_made, 1)

                def add_y(qb):
                    gated_wait(y_ready, n0 + qb + 1)
                    tiles = bass.ds(b * BT + qb * CT, CT)
                    dve.tensor_tensor(H[:, tiles, :], pY[:, 0:CT * C].rearrange("p (t c) -> p t c", c=C),
                                      H[:, tiles, :], ALU.add).then_inc(h_made, 1)

                def query_block(qb, last):
                    for p in range(2, PAIRS):
                        remainder(qb, p)
                    if not last:
                        remainder(qb + 1, 0)
                    gate(qb)
                    if not last:
                        remainder(qb + 1, 1)
                    add_y(qb)

                remainder(0, 0)
                remainder(0, 1)
                with dve.Fori(0, LASTQ) as qb:
                    query_block(qb, False)
                query_block(LASTQ, True)


def normed_input(nc, H, XC, X2, inv_rms):
    with ExitStack() as ctx:
        m = Scope(nc, ctx, "ln")
        square = m.sb("square", [P, TILES, C])
        sums = m.sb("sums", [P, TILES])
        mean = m.sb("mean", [P, TILES])
        var = m.sb("var", [P, TILES])
        shifted = m.sb("shifted", [P, TILES])
        root = m.sb("root", [P, TILES])
        inv = m.sb("inv", [P, TILES])
        ms = m.sb("ms", [P, TILES])
        shifted_made = m.sem("shifted_made")
        root_made = m.sem("root_made")
        dve_chain = m.sem("dve_chain")
        block = ctx.enter_context(nc.Block())

        @block.scalar
        def _(act):
            for n in range(2):
                act.wait_ge(shifted_made, n + 1)
                act.activation(root[:], shifted[:], ACT.Sqrt).then_inc(root_made, 1)

        @block.vector
        def _(dve):
            chain = Chain(dve, dve_chain)
            centre(dve, chain, H, XC, square, sums, mean, var)
            chain.ready()
            dve.tensor_scalar(shifted[:], var[:], LN_EPS, None, ALU.add).then_inc(shifted_made, 1)
            dve.wait_ge(root_made, 1)
            chain.then(dve.reciprocal(inv[:], root[:]))
            chain.ready()
            chain.then(dve.tensor_tensor(X2[:], XC[:], bcast(inv[:], 2, C), ALU.mult))
            chain.then(dve.tensor_tensor(ms[:], var[:], inv[:], ALU.mult))
            chain.ready()
            chain.then(dve.tensor_tensor(ms[:], ms[:], inv[:], ALU.mult))
            chain.ready()
            dve.tensor_scalar(shifted[:], ms[:], RMS_EPS, None, ALU.add).then_inc(shifted_made, 1)
            dve.wait_ge(root_made, 2)
            chain.then(dve.reciprocal(inv_rms[:], root[:]))
            chain.ready()


def stack(eng, chain, chained, src, out, res, parts, signal):
    def block_of(i):
        return out[:, :, :, i * HD:(i + 1) * HD]

    first = [parts.index(k) for k in range(3)]
    chain.then(eng.tensor_copy(block_of(first[0]), src))
    chained()
    chain.then(eng.tensor_tensor(res, src, block_of(first[0]), ALU.subtract))
    chained()
    chain.then(eng.tensor_copy(block_of(first[1]), res))
    chained()
    chain.then(eng.tensor_tensor(res, res, block_of(first[1]), ALU.subtract))
    chained()
    chain.then(eng.tensor_copy(block_of(first[2]), res))
    for i, k in enumerate(parts):
        if i not in first:
            chain.then(eng.tensor_copy(block_of(i), block_of(first[k])))
    chained()
    eng.sem_inc(signal, 1)


def causal_attention(nc, d, X2, inv_rms, ident, identb, masks):
    LASTQ = CHUNKS - 1
    PER = 8
    FULL = CHUNKS * (CHUNKS + 1) // 2 * CT

    def before(qb):
        return 2 * qb * (qb + 1)

    with ExitStack() as ctx:
        m = Scope(nc, ctx, "ca")
        wraw = m.sb("wraw", [P, QKV])
        whi = m.sb("whi", [P, QKV], F32R)
        wlo = m.sb("wlo", [P, QKV], F32R)
        woraw = m.sb("woraw", [P, C])
        wohi = m.sb("wohi", [P, C], F32R)
        wolo = m.sb("wolo", [P, C], F32R)
        ln1 = m.sb("ln1", [P, 1])
        warm = m.sb("warm", [P, 1])
        cos = m.sb("cos", [P, BT, HD])
        sin = m.sb("sin", [P, BT, HD])
        hx = m.sb("hx", [P, CT, C])
        pair = m.sb("pair", [P, CT, 2 * C])
        xT = m.sb("xT", [P, CH], F32R)
        direct = m.sb("direct", [P, CT, NH + NKV, HD])
        turned = m.sb("turned", [P, CT, NH + NKV, HD])
        QK = m.sb("QK", [P, BT, ROPED])
        KS = m.sb("KS", [P, CT, NKV, STACK], BF16)
        QS = m.sb("QS", [P, 2, CT, NH, STACK], BF16)
        rest = m.sb("rest", [P, CT, NH, HD])
        first_rest = m.sb("first_rest", [P, CT, NH, HD])
        KT = m.sb("KT", [STACK + SHIFT, NKV, SEQ], BF16)
        QT = m.sb("QT", [STACK + SHIFT, 3, NH, CH], BF16)
        VA = m.sb("VA", [P, BT, NKV, VW])
        VS = m.sb("VS", [P, CT, NKV, VW])
        zeros = m.sb("zeros", [P, CH], BF16)
        probs = m.sb("probs", [P, 2, NH, CH])
        peaks = m.sb("peaks", [P, CT, NH, CHUNKS])
        peak = m.sb("peak", [P, CT, NH])
        left = m.sb("left", [P, CT, NH])
        shift = m.sb("shift", [P, CT, NH, SHIFT + 1], BF16)
        oT = m.sb("oT", [P, CH])
        inv = m.sb("inv", [P, CT, NH])
        y = m.sb("y", [P, CT, C])
        ypair = m.sb("ypair", [P, CT, 2 * C])
        yT = m.sb("yT", [P, CH], F32R)
        pS = m.ps("pS", [P, 2, 512])
        pM = m.ps("pM", [P, 4, 512])
        pO = m.ps("pO", [P, 512])
        pX = m.ps("pX", [P, 512])
        pK, pT, pQ = pM[:, 0, :].bitcast(BF16), pM[:, 2, :], pM[:, 3, :]

        weights_in = m.sem("weights_in")
        split_done = m.sem("split_done")
        fills_done = m.sem("fills_done")
        zeros_made = m.sem("zeros_made")
        pair_made = m.sem("pair_made")
        xT_ready = m.sem("xT_ready")
        xT_made = m.sem("xT_made")
        qkv_ready = m.sem("qkv_ready")
        roped = m.sem("roped")
        v_made = m.sem("v_made")
        parts_made = m.sem("parts_made")
        rests_made = m.sem("rests_made")
        ks_made = m.sem("ks_made")
        kT_ready = m.sem("kT_ready")
        kT_made = m.sem("kT_made")
        qs_made = m.sem("qs_made")
        qT_ready = m.sem("qT_ready")
        qT_made = m.sem("qT_made")
        raw_ready = m.sem("raw_ready")
        raw_free = m.sem("raw_free")
        shift_made = m.sem("shift_made")
        shiftT_ready = m.sem("shiftT_ready")
        shiftT_made = m.sem("shiftT_made")
        vs_made = m.sem("vs_made")
        scores_ready = m.sem("scores_ready")
        probs_made = m.sem("probs_made")
        weighed = m.sem("weighed")
        o_copied = m.sem("o_copied")
        oT_ready = m.sem("oT_ready")
        y_made = m.sem("y_made")
        yT_ready = m.sem("yT_ready")
        yT_made = m.sem("yT_made")
        wo_ready = m.sem("wo_ready")
        x3_made = m.sem("x3_made")
        dve_chain = m.sem("dve_chain")
        pool_chain = m.sem("pool_chain")
        pe_gate, act_gate, dve_gate, pool_gate = (m.sem(f"{e}_gate") for e in ("pe", "act", "dve", "pool"))
        block = ctx.enter_context(nc.Block())

        @block.sync
        def _(sp):
            for half in (0, C):
                sp.dma_start(wraw[half:half + C, :], d["wqkv"]).then_inc(weights_in, 16)
                sp.dma_start(woraw[half:half + C, :], d["wo"]).then_inc(weights_in, 16)
                sp.dma_start(ln1[half:half + C, :], d["ln1_w"]).then_inc(weights_in, 16)
            sp.dma_start(cos[:], d["cos"]).then_inc(weights_in, 16)
            sp.dma_start(sin[:], d["sin"]).then_inc(weights_in, 16)

        @block.tensor
        def _(pe):
            def gated_wait(sem, value):
                pe.wait_ge(sem, value)
                pe.sem_inc(pe_gate, 1)

            pe.sem_inc(qT_ready, 4)
            pe.sem_inc(weighed, CT)
            pe.sem_inc(xT_ready, 1)
            pe.sem_inc(qkv_ready, 1)
            pe.wait_ge(weights_in, 128)
            pe.wait_ge(split_done, 1)
            pe.wait_ge(fills_done, 3)
            with pe.Fori(0, BATCH) as b:
                s0 = b * FULL

                def turn_rows(n):
                    gated_wait(pair_made, n + 1)
                    gated_wait(xT_made, n + 1)
                    for t in range(CT):
                        last = pe.transpose(pT[:, t * P:(t + 1) * P], pair[:, t, :], ident[:])
                    last.then_inc(xT_ready, 1)

                def project(n):
                    gated_wait(xT_made, n + 2)
                    gated_wait(v_made, n + 1)
                    for t in range(CT):
                        for w in (whi, wlo):
                            last = pe.matmul(pQ[:, t * QKV:(t + 1) * QKV], xT[:, t * P:(t + 1) * P], w[:],
                                             start=w is whi, stop=w is wlo)
                    last.then_inc(qkv_ready, 1)

                def turn_keys(n):
                    gated_wait(ks_made, n + 1)
                    gated_wait(kT_made, n + 1)
                    for kv in range(NKV):
                        for t in range(CT):
                            col = (kv * CT + t) * P
                            last = pe.transpose(pK[0:STACK, col:col + P], KS[:, t, kv, :], identb[:])
                    last.then_inc(kT_ready, 1)

                n0 = b * CHUNKS
                turn_rows(n0)
                project(n0)
                turn_rows(n0 + 1)
                with pe.Fori(1, LASTQ) as c:
                    project(n0 + c)
                    turn_rows(n0 + c + 1)
                    turn_keys(n0 + c - 1)
                project(n0 + LASTQ)
                for c in (LASTQ - 1, LASTQ):
                    turn_keys(n0 + c)
                gated_wait(kT_made, (b + 1) * CHUNKS + 1)
                gated_wait(v_made, (b + 1) * CHUNKS + 1)

                def turn_queries(qb, half):
                    n = b * CHUNKS + qb
                    gated_wait(qs_made, n + 1)
                    gated_wait(qT_made, 2 * n + half + 1)
                    bank = pX[:].bitcast(BF16)
                    for h in range(2):
                        for t in range(CT):
                            col = (h * CT + t) * P
                            last = pe.transpose(bank[0:STACK, col:col + P], QS[:, qb % 2, t, 2 * half + h, :],
                                                identb[:])
                    last.then_inc(qT_ready, 1)

                def turn_shift(qb, half):
                    n = b * CHUNKS + qb
                    gated_wait(shift_made, n + 1)
                    gated_wait(shiftT_made, 2 * n + half + 1)
                    bank = pX[:].bitcast(BF16)
                    for h in range(2):
                        for t in range(CT):
                            col = (h * CT + t) * P
                            last = pe.transpose(bank[STACK:STACK + SHIFT, col:col + P],
                                                shift[:, t, 2 * half + h, 0:SHIFT], identb[:])
                    last.then_inc(shiftT_ready, 1)

                def raw_scores(qb, order, c, t, diag=False):
                    unit = s0 + before(qb) + order
                    keys = (t + 1) * P if diag else CH
                    for k in range(2):
                        pe.wait_ge(raw_free, 2 * unit + (k + 1))
                        for h in (2 * k, 2 * k + 1):
                            rhs = KT[0:STACK, h // 2, c * CH:c * CH + keys] if isinstance(c, int) else \
                                KT[0:STACK, h // 2, bass.ds(c * CH, CH)]
                            last = pe.matmul(pM[:, h, 0:keys], QT[0:STACK, qb % 3, h, t * P:(t + 1) * P], rhs,
                                             start=True, stop=not diag)
                            if diag:
                                last = pe.matmul(pM[:, h, t * P:keys], identb[:], masks[:, 1, :],
                                                 start=False, stop=True)
                        last.then_inc(raw_ready, 1)

                def scores(qb, order, c, t, heads, diag=False):
                    step = s0 + before(qb) + order
                    q0 = t * P if diag else 0
                    for h in heads:
                        gated_wait(probs_made, 4 * step + (h - 1 if qb == LASTQ else h + 1))
                        out = pM[:, h, :] if qb == LASTQ else pS[:, h % 2, :]
                        lhsT = KT[:, h // 2, (4 * c + t) * P:(4 * c + t + 1) * P] if isinstance(c, int) else \
                            KT[:, h // 2, bass.ds(c * CH + t * P, P)]
                        last = pe.matmul(out[:, q0:CH], lhsT, QT[:, qb % 3, h, q0:CH], start=True, stop=not diag)
                        if diag:
                            last = pe.matmul(out[:, q0:q0 + P], identb[:], masks[:, 0, :], start=False, stop=True)
                        last.then_inc(scores_ready, 1)

                def weigh(qb, order, slot, q0=0):
                    step = s0 + before(qb) + order
                    pe.wait_ge(probs_made, 4 * step + 6)
                    for h in range(NH):
                        last = pe.matmul(pO[VW * h:VW * h + VW, q0:CH], VS[:, slot, h // 2, :],
                                         probs[:, slot % 2, h, q0:CH], start=False, stop=False,
                                         skip_group_check=True)
                    last.then_inc(weighed, 1)

                def turn_output(qb):
                    gated_wait(o_copied, b * CHUNKS + qb + 2)
                    for t in range(CT):
                        last = pe.transpose(pX[:, t * P:(t + 1) * P], oT[:, t * P:(t + 1) * P], ident[:])
                    last.then_inc(oT_ready, 1)

                def turn_y(qb):
                    gated_wait(y_made, b * CHUNKS + qb + 1)
                    for t in range(CT):
                        last = pe.transpose(pX[:, t * P:(t + 1) * P], ypair[:, t, :], ident[:])
                    last.then_inc(yT_ready, 1)

                def project_y(qb):
                    gated_wait(yT_made, b * CHUNKS + qb + 1)
                    for t in range(CT):
                        for w in (wohi, wolo):
                            last = pe.matmul(pX[:, t * C:(t + 1) * C], yT[:, t * P:(t + 1) * P], w[:],
                                             start=w is wohi, stop=w is wolo)
                    last.then_inc(wo_ready, 1)

                def early_maxima(qb):
                    return [(qb, t, qb - 1, t) for t in range(CT)] + \
                        [(qb, CT + t, qb, t, True) for t in range(CT)] if qb < CHUNKS else []

                def take_maxima(side, units):
                    for args in side[:units]:
                        raw_scores(*args)
                    del side[:units]

                def step(qb, order, c, t, between=None, diag=False):
                    q0 = t * P if diag else 0
                    before_q0 = (t - 1) * P if diag and t else 0
                    now, later = ((0, 1, 2, 3), ()) if qb == LASTQ else ((0, 1), (2, 3))
                    scores(qb, order, c, t, now, diag)
                    if between is None:
                        weigh(qb, order - 1, (t - 1) % CT, before_q0)
                    else:
                        between()
                    scores(qb, order, c, t, later, diag)

                n0 = b * CHUNKS
                for half in range(2):
                    turn_queries(0, half)
                gated_wait(qT_made, 2 * n0 + 3)
                for t in range(CT):
                    raw_scores(0, t, 0, t, diag=True)
                for half in range(2):
                    turn_queries(1, half)
                gated_wait(qT_made, 2 * n0 + 5)
                side = early_maxima(1)
                for half in range(2):
                    take_maxima(side, 1)
                    turn_shift(0, half)
                take_maxima(side, 5)
                gated_wait(shiftT_made, 2 * n0 + 3)
                for half in range(2):
                    turn_queries(2, half)
                take_maxima(side, 1)
                gated_wait(qT_made, 2 * n0 + 7)
                for qb in range(CHUNKS):
                    n = n0 + qb
                    if qb == LASTQ:
                        gated_wait(raw_free, 2 * (s0 + FULL) + 2)
                    gated_wait(o_copied, n + 1)
                    pe.matmul(pO[:], zeros[:, 0:P], zeros[:], start=True, stop=False, skip_group_check=True)

                    def key_chunk(c, opens=False):
                        for t in range(CT):
                            order = 4 * c + t

                            def more_maxima():
                                if qb < LASTQ:
                                    raw_scores(qb + 1, order + 2 * CT, c, t)

                            def between():
                                if qb + 2 < CHUNKS:
                                    turn_queries(qb + 2, 1)
                                more_maxima()

                            if opens and t == 0:
                                step(qb, order, c, t, between)
                            else:
                                step(qb, order, c, t)
                                more_maxima()

                    if qb:
                        key_chunk(0, opens=True)
                    if qb > 1:
                        with pe.Fori(1, qb) as c:
                            key_chunk(c)
                    side = early_maxima(qb + 2)
                    if qb and qb + 2 < CHUNKS:
                        gated_wait(qT_made, 2 * n + 7)
                    for t in range(CT):
                        step(qb, CT * qb + t, qb, t, (lambda: None) if qb == 0 and t == 0 else None, diag=True)
                        take_maxima(side, 1)
                        if t < 2 and qb < LASTQ:
                            if t == 0:
                                gated_wait(x3_made, n if qb else n + 1)
                            turn_shift(qb + 1, t)
                        if t == 2:
                            take_maxima(side, 1)
                            if qb < LASTQ:
                                gated_wait(shiftT_made, 2 * n + 5)
                            else:
                                gated_wait(x3_made, n)
                            if qb:
                                turn_output(qb - 1)
                    if qb:
                        turn_y(qb - 1)
                    weigh(qb, CT * (qb + 1) - 1, CT - 1, (CT - 1) * P)
                    take_maxima(side, 1)
                    if qb:
                        project_y(qb - 1)
                    take_maxima(side, 1)
                    if qb + 3 < CHUNKS:
                        gated_wait(x3_made, n + 1)
                        turn_queries(qb + 3, 0)
                    take_maxima(side, 1)
                gated_wait(x3_made, (b + 1) * CHUNKS)
                turn_output(LASTQ)
                turn_y(LASTQ)
                project_y(LASTQ)
                gated_wait(x3_made, (b + 1) * CHUNKS + 1)

        @block.scalar
        def _(act):
            def gated_wait(sem, value):
                act.wait_ge(sem, value)
                act.sem_inc(act_gate, 1)

            for credit, many in ((v_made, 1), (kT_made, 1), (qT_made, 1), (shiftT_made, 1), (probs_made, 2),
                                 (o_copied, 1)):
                act.sem_inc(credit, many)
            act.wait_ge(fills_done, 3)
            act.wait_ge(zeros_made, 1)
            with act.Fori(0, BATCH) as b:
                s0 = b * FULL
                act.activation(warm[:], zeros[:, 0:1], ACT.Exp)

                def take_values(c):
                    gated_wait(roped, b * CHUNKS + c + 1)
                    own = bass.ds(c * CT, CT) if not isinstance(c, int) else slice(c * CT, (c + 1) * CT)
                    act.activation(VA[:, own, :, 0:HD],
                                   pQ.rearrange("p (t n) -> p t n", n=QKV)[:, :, ROPED:QKV]
                                   .rearrange("p t (k e) -> p t k e", e=HD), ACT.Copy).then_inc(v_made, 1)

                def take_keys(c):
                    gated_wait(kT_ready, b * CHUNKS + c + 1)
                    own = bass.ds(c * CH, CH) if not isinstance(c, int) else slice(c * CH, (c + 1) * CH)
                    act.activation(KT[0:STACK, :, own],
                                   pK[0:STACK, :].rearrange("p (k n) -> p k n", n=CH),
                                   ACT.Copy).then_inc(kT_made, 1)

                def stack_keys(c):
                    own = bass.ds(c * CT, CT) if not isinstance(c, int) else slice(c * CT, (c + 1) * CT)
                    src = QK[:, own, NH * HD:ROPED].rearrange("p t (h e) -> p t h e", e=HD)
                    for k in range(3):
                        if k:
                            gated_wait(rests_made, 2 * (b * CHUNKS + c) + k)
                        for i in (i for i in range(len(K_PARTS)) if K_PARTS[i] == k):
                            last = act.activation(KS[:, :, :, i * HD:(i + 1) * HD],
                                                  rest[:, :, 0:NKV, :] if k else src, ACT.Copy)
                        last.then_inc(ks_made if k == 2 else parts_made, 1)

                take_values(0)
                stack_keys(0)
                with act.Fori(1, CHUNKS) as c:
                    take_values(c)
                    take_keys(c - 1)
                    stack_keys(c)
                take_keys(LASTQ)

                def take(ready, value, made, rows, qb, half):
                    gated_wait(ready, value)
                    act.activation(QT[rows, qb % 3, 2 * half:2 * half + 2, :].rearrange("p h n -> p (h n)"),
                                   pX[rows, :].bitcast(BF16), ACT.Copy).then_inc(made, 1)

                def take_queries(qb, half):
                    take(qT_ready, 2 * (b * CHUNKS + qb) + half + 5, qT_made, slice(0, STACK), qb, half)

                def take_shift(qb, half):
                    take(shiftT_ready, 2 * (b * CHUNKS + qb) + half + 1, shiftT_made,
                         slice(STACK, STACK + SHIFT), qb, half)

                def exps(qb, order, slot, q0=0):
                    step = s0 + before(qb) + order
                    gated_wait(weighed, step + (CT - 1))
                    for h in range(NH):
                        act.wait_ge(scores_ready, 4 * step + (h + 1))
                        if h == NH - 1:
                            gated_wait(vs_made, step + 1)
                        src = pM[:, h, :] if qb == LASTQ else pS[:, h % 2, :]
                        act.activation(probs[:, slot % 2, h, q0:CH], src[:, q0:CH], ACT.Exp,
                                       scale=float(HD) ** -0.5).then_inc(probs_made, 1)

                for take_part, qb in ((take_queries, 0), (take_queries, 1), (take_shift, 0), (take_queries, 2)):
                    for half in range(2):
                        take_part(qb, half)
                for qb in range(CHUNKS):
                    if qb:
                        with act.Fori(0, qb) as c:
                            for t in range(CT):
                                exps(qb, 4 * c + t, t)
                    for t in range(CT):
                        exps(qb, CT * qb + t, t, t * P)
                        if t < 2 and qb < LASTQ:
                            take_shift(qb + 1, t)
                    gated_wait(weighed, s0 + before(qb + 1) + CT)
                    gated_wait(oT_ready, b * CHUNKS + qb + 1)
                    act.activation(oT[:], pO[:], ACT.Copy).then_inc(o_copied, 1)
                    for half in range(2 if qb + 3 < CHUNKS else 0):
                        take_queries(qb + 3, half)

        @block.gpsimd
        def _(pool):
            chain = Chain(pool, pool_chain)

            def gated_wait(sem, value):
                pool.wait_ge(sem, value)
                pool.sem_inc(pool_gate, 1)

            def chained():
                chain.ready()
                if chain.base is not None:
                    pool.sem_inc(pool_gate, 1)

            pool.memset(VA[:], 0.0).then_inc(fills_done, 1)
            pool.wait_ge(fills_done, 1)
            pool.memset(KT[STACK:STACK + SHIFT, :, :], 1.0).then_inc(fills_done, 1)
            pool.wait_ge(fills_done, 2)
            pool.memset(VA[:, :, :, HD:HD + 1], 1.0).then_inc(fills_done, 1)
            pool.sem_inc(oT_ready, 1)
            IMAGE = (CHUNKS - 2) * PER
            with pool.Fori(0, BATCH) as b:
                s0 = b * FULL
                def key_rests(c):
                    own = bass.ds(c * CT, CT)
                    src = QK[:, own, NH * HD:ROPED].rearrange("p t (h e) -> p t h e", e=HD)
                    res = rest[:, :, 0:NKV, :]
                    for k in range(2):
                        gated_wait(parts_made, 2 * (b * CHUNKS + c) + (k + 1))
                        if k:
                            gated_wait(rests_made, 2 * (b * CHUNKS + c) + 1)
                        i = K_PARTS.index(k)
                        pool.tensor_tensor(res, res if k else src, KS[:, :, :, i * HD:(i + 1) * HD],
                                           ALU.subtract).then_inc(rests_made, 1)

                with pool.Fori(0, CHUNKS) as c:
                    key_rests(c)
                def stack_queries(qb):
                    chain.enter(b * IMAGE + (qb - 2) * PER)
                    gated_wait(qT_ready, 2 * (b * CHUNKS + qb) + 2)
                    stack(pool, chain, chained, QK[:, qb * CT:(qb + 1) * CT, 0:NH * HD].rearrange("p t (h e) -> p t h e", e=HD),
                          QS[:, qb % 2, :, :, :], rest[:], Q_PARTS, qs_made)
                    chain.leave(PER, 0)

                def stage_values(qb, order, c, t, slot):
                    gated_wait(weighed, s0 + before(qb) + order + 1)
                    if isinstance(c, int):
                        pool.tensor_copy(VS[:, slot, :, :], VA[:, 4 * c + t, :, :]).then_inc(vs_made, 1)
                    else:
                        pool.tensor_copy(VS[:, slot:slot + 1, :, :],
                                         VA[:, bass.ds(c * CT + t, 1), :, :]).then_inc(vs_made, 1)

                stack_queries(2)
                for qb in range(CHUNKS):
                    if qb:
                        with pool.Fori(0, qb) as c:
                            for t in range(CT):
                                stage_values(qb, 4 * c + t, c, t, t)
                        if qb + 3 < CHUNKS:
                            stack_queries(qb + 3)
                    for t in range(CT):
                        stage_values(qb, CT * qb + t, qb, t, t)
                    if qb == 0:
                        stack_queries(3)

        @block.vector
        def _(dve):
            chain = Chain(dve, dve_chain)
            for credit, many in ((raw_free, 2), (x3_made, 1), (xT_made, 1)):
                dve.sem_inc(credit, many)
            dve.memset(zeros[:], 0.0).then_inc(zeros_made, 1)
            dve.wait_ge(weights_in, 128)
            chain.then(dve.tensor_scalar(wraw[:], wraw[:], ln1[:, 0:1], None, ALU.mult))
            chain.ready()
            split_weights(dve, chain, wraw[:], whi[:], wlo[:])
            split_weights(dve, chain, woraw[:], wohi[:], wolo[:])
            chain.ready()
            dve.sem_inc(split_done, 1)
            SPLITS = chain.n
            PREP = 6
            TAIL = 11

            def gated_wait(sem, value):
                dve.wait_ge(sem, value)
                dve.sem_inc(dve_gate, 1)

            def chained():
                chain.ready()
                dve.sem_inc(dve_gate, 1)

            with dve.Fori(0, BATCH) as b:
                s0 = b * FULL
                c0 = b * (CHUNKS * (PREP + TAIL) + 2 * PER) + SPLITS
                def split(c):
                    own = b * BT + c * CT
                    tiles = bass.ds(own, CT)
                    chain.then(dve.tensor_tensor(hx[:], X2[:, tiles, :], bcast(inv_rms[:, tiles], 2, C), ALU.mult))
                    gated_wait(xT_ready, b * CHUNKS + c + 1)
                    chained()
                    chain.then(dve.tensor_copy(pair[:, :, 0:C].bitcast(F32R), hx[:]))
                    chained()
                    dve.tensor_tensor(pair[:, :, C:2 * C], hx[:], pair[:, :, 0:C],
                                      ALU.subtract).then_inc(pair_made, 1)

                def take_rows(c):
                    gated_wait(xT_ready, b * CHUNKS + c + 2)
                    gated_wait(qkv_ready, b * CHUNKS + c + 1)
                    dve.tensor_copy(xT[:], pT).then_inc(xT_made, 1)

                def rope(c):
                    own = bass.ds(c * CT, CT) if not isinstance(c, int) else slice(c * CT, (c + 1) * CT)
                    gated_wait(qkv_ready, b * CHUNKS + c + 2)
                    qk = pQ.rearrange("p (t n) -> p t n", n=QKV)[:, :, 0:ROPED].rearrange(
                        "p t (h e) -> p t h e", e=HD)
                    chain.then(dve.tensor_tensor(direct[:], qk, bcast(cos[:, own, :], 2, NH + NKV), ALU.mult))
                    half = HD // 2
                    for lo, hi in ((0, half), (half, 0)):
                        chain.then(dve.tensor_tensor(turned[:, :, :, lo:lo + half], qk[:, :, :, hi:hi + half],
                                                     bcast(sin[:, own, lo:lo + half], 2, NH + NKV), ALU.mult))
                    chained()
                    chain.then(dve.tensor_tensor(QK[:, own, :].rearrange("p t (h e) -> p t h e", e=HD),
                                                 direct[:], turned[:], ALU.add))
                    chained()
                    dve.sem_inc(roped, 1)

                chain.enter(c0)
                split(0)
                take_rows(0)
                split(1)
                chain.leave(4, 0)
                with dve.Fori(0, CHUNKS - 2) as c:
                    chain.enter(c0 + 4 + c * PREP)
                    rope(c)
                    take_rows(c + 1)
                    split(c + 2)
                    chain.leave(PREP, 0)
                chain.enter(c0 + 4 + (CHUNKS - 2) * PREP)
                rope(LASTQ - 1)
                take_rows(LASTQ)
                rope(LASTQ)
                chain.leave(8, 0)

                def maxima(qb, order, c, t, diag=False):
                    unit = s0 + before(qb) + order
                    keys = (t + 1) * P if diag else CH
                    at = slice(c, c + 1) if isinstance(c, int) else bass.ds(c, 1)
                    for k in range(2):
                        gated_wait(raw_ready, 2 * unit + (k + 1))
                        dve.tensor_reduce(peaks[:, t, 2 * k:2 * k + 2, at].rearrange("p h c -> p (h c)"),
                                          pM[:, 2 * k:2 * k + 2, 0:keys], AX.X, ALU.max).then_inc(raw_free, 1)

                def make_shift(qb):
                    gated_wait(raw_free, 2 * (s0 + before(qb + 1)) + 2)
                    chain.then(dve.tensor_reduce(peak[:], peaks[:, :, :, 0:qb + 1], AX.X, ALU.max, negate=True))
                    chained()
                    chain.then(dve.tensor_copy(shift[:, :, :, 0], peak[:]))
                    chained()
                    chain.then(dve.tensor_tensor(left[:], peak[:], shift[:, :, :, 0], ALU.subtract))
                    chained()
                    chain.then(dve.tensor_copy(shift[:, :, :, 1], left[:]))
                    chained()
                    chain.then(dve.tensor_tensor(left[:], left[:], shift[:, :, :, 1], ALU.subtract))
                    chained()
                    chain.then(dve.tensor_copy(shift[:, :, :, 2], left[:]))
                    chained()
                    dve.sem_inc(shift_made, 1)

                def normalise(qb):
                    gated_wait(oT_ready, b * CHUNKS + qb + 2)
                    o = pX[:].rearrange("p (t h e) -> p t h e", h=NH, e=VW)
                    chain.then(dve.reciprocal(inv[:], o[:, :, :, HD]))
                    chained()
                    chain.then(dve.tensor_tensor(y[:].rearrange("p t (h e) -> p t h e", e=HD), o[:, :, :, 0:HD],
                                                 bcast(inv[:], 3, HD), ALU.mult))
                    chained()
                    chain.then(dve.tensor_copy(ypair[:, :, 0:C].bitcast(F32R), y[:]))
                    chained()
                    chain.then(dve.tensor_tensor(ypair[:, :, C:2 * C], y[:], ypair[:, :, 0:C], ALU.subtract))
                    chained()
                    dve.sem_inc(y_made, 1)

                def take_y(qb):
                    gated_wait(yT_ready, b * CHUNKS + qb + 1)
                    dve.tensor_copy(yT[:], pX[:]).then_inc(yT_made, 1)

                def add_y(qb):
                    gated_wait(wo_ready, b * CHUNKS + qb + 1)
                    tiles = bass.ds(b * BT + qb * CT, CT)
                    chain.then(dve.tensor_tensor(X2[:, tiles, :], pX[:, 0:CT * C].rearrange("p (t c) -> p t c", c=C),
                                                 X2[:, tiles, :], ALU.add))
                    chained()
                    dve.sem_inc(x3_made, 1)

                chain.enter(c0 + CHUNKS * PREP)
                for qb in range(2):
                    gated_wait(qT_ready, 2 * (b * CHUNKS + qb) + 2)
                    stack(dve, chain, chained, QK[:, qb * CT:(qb + 1) * CT, 0:NH * HD].rearrange(
                        "p t (h e) -> p t h e", e=HD), QS[:, qb, :, :, :], first_rest[:], Q_PARTS, qs_made)
                def early_maxima(qb):
                    return [(qb, t, qb - 1, t) for t in range(CT)] + \
                        [(qb, CT + t, qb, t, True) for t in range(CT)] if qb < CHUNKS else []

                def take_maxima(side, units):
                    for args in side[:units]:
                        maxima(*args)
                    del side[:units]

                for t in range(CT):
                    maxima(0, t, 0, t, diag=True)
                make_shift(0)
                take_maxima(early_maxima(1), 2 * CT)
                for qb in range(CHUNKS):
                    if qb and qb < LASTQ:
                        with dve.Fori(0, qb) as c:
                            for t in range(CT):
                                maxima(qb + 1, 4 * c + (2 * CT + t), c, t)
                    if qb < LASTQ:
                        make_shift(qb + 1)
                    side = early_maxima(qb + 2)
                    take_maxima(side, 4)
                    if qb:
                        normalise(qb - 1)
                    take_maxima(side, 1)
                    if qb:
                        take_y(qb - 1)
                    take_maxima(side, 1)
                    if qb:
                        add_y(qb - 1)
                    take_maxima(side, 2)
                normalise(LASTQ)
                take_y(LASTQ)
                add_y(LASTQ)
                chain.leave(CHUNKS * TAIL + 2 * PER, 0)


def routing(nc, d, X3, ident, fT, weight, expert_weights):
    w1hi, w1lo, w3hi, w3lo, w2 = expert_weights
    with ExitStack() as ctx:
        m = Scope(nc, ctx, "ro")
        square = m.sb("square", [P, TILES, C])
        ms = m.sb("ms", [P, TILES])
        root = m.sb("root", [P, TILES])
        inv = m.sb("inv", [P, TILES])
        rraw = m.sb("rraw", [P, NE])
        rhi = m.sb("rhi", [P, NE], F32R)
        rlo = m.sb("rlo", [P, NE], F32R)
        raw1 = m.sb("raw1", [P, HIDDEN])
        raw3 = m.sb("raw3", [P, HIDDEN])
        ln2 = m.sb("ln2", [P, 1])
        flat = m.sb("flat", [P, CT, C])
        pair = m.sb("pair", [P, CT, 2 * C])
        xT = m.sb("xT", [P, CH], F32R)
        logits = m.sb("logits", [P, TILES, NE])
        top = m.sb("top", [P, TILES])
        prob = m.sb("prob", [P, TILES, NE])
        total = m.sb("total", [P, TILES])
        above = m.sb("above", [P, TILES, NE, NE])
        level = m.sb("level", [P, TILES, NE, NE])
        earlier = m.sb("earlier", [P, NE, NE])
        rank = m.sb("rank", [P, TILES, NE])
        pT = m.ps("pT", [P, 512])
        pL = m.ps("pL", [P, 512])

        weights_in = m.sem("weights_in")
        ms_made = m.sem("ms_made")
        root_made = m.sem("root_made")
        split_done = m.sem("split_done")
        pair_made = m.sem("pair_made")
        xT_ready = m.sem("xT_ready")
        xT_made = m.sem("xT_made")
        fT_made = m.sem("fT_made")
        expert_weights_in = m.sem("expert_weights_in")
        pool_chain = m.sem("pool_chain")
        logits_ready = m.sem("logits_ready")
        logits_made = m.sem("logits_made")
        margin_made = m.sem("margin_made")
        exp_made = m.sem("exp_made")
        dve_chain = m.sem("dve_chain")
        pe_gate, act_gate, dve_gate = (m.sem(f"{e}_gate") for e in ("pe", "act", "dve"))
        block = ctx.enter_context(nc.Block())
        N = BATCH * CHUNKS

        @block.sync
        def _(sp):
            for half in (0, C):
                sp.dma_start(rraw[half:half + C, :], d["router"]).then_inc(weights_in, 16)
                sp.dma_start(ln2[half:half + C, :], d["ln2_w"]).then_inc(weights_in, 16)
            sp.dma_start(earlier[:], d["earlier"]).then_inc(weights_in, 16)
            for half in (0, C):
                sp.dma_start(raw1[half:half + C, :], d["w1"]).then_inc(expert_weights_in, 16)
                sp.dma_start(raw3[half:half + C, :], d["w3"]).then_inc(expert_weights_in, 16)
            sp.dma_start(w2[:], d["w2"]).then_inc(expert_weights_in, 16)

        @block.scalar
        def _(act):
            act.sem_inc(fT_made, 1)
            act.wait_ge(ms_made, 1)
            act.activation(root[:], ms[:], ACT.Sqrt).then_inc(root_made, 1)
            with act.Fori(0, N) as n:
                act.wait_ge(xT_made, n + 2)
                act.sem_inc(act_gate, 1)
                act.activation(fT[:, bass.ds(n * CH, CH)], xT[:].bitcast(F32), ACT.Copy).then_inc(fT_made, 1)
            act.wait_ge(margin_made, 1)
            act.activation(prob[:], prob[:], ACT.Exp).then_inc(exp_made, 1)

        @block.tensor
        def _(pe):
            def gated_wait(sem, value):
                pe.wait_ge(sem, value)
                pe.sem_inc(pe_gate, 1)

            pe.wait_ge(split_done, 1)

            def turn(n):
                gated_wait(pair_made, n + 1)
                gated_wait(xT_made, n + 1)
                for t in range(CT):
                    last = pe.transpose(pT[:, t * P:(t + 1) * P], pair[:, t, :], ident[:])
                last.then_inc(xT_ready, 1)

            def route(n):
                gated_wait(xT_made, n + 2)
                gated_wait(logits_made, n + 1)
                for t in range(CT):
                    for w in (rhi, rlo):
                        last = pe.matmul(pL[:, t * NE:(t + 1) * NE], xT[:, t * P:(t + 1) * P], w[:],
                                         start=w is rhi, stop=w is rlo)
                last.then_inc(logits_ready, 1)

            turn(0)
            with pe.Fori(0, N - 1) as n:
                route(n)
                turn(n + 1)
            route(N - 1)

        @block.gpsimd
        def _(pool):
            chain = Chain(pool, pool_chain)
            pool.wait_ge(expert_weights_in, 80)
            for raw, hi, lo in ((raw1, w1hi, w1lo), (raw3, w3hi, w3lo)):
                chain.then(pool.tensor_scalar(raw[:], raw[:], ln2[:, 0:1], None, ALU.mult))
                chain.ready()
                split_weights(pool, chain, raw[:], hi[:], lo[:])
            chain.ready()

        @block.vector
        def _(dve):
            chain = Chain(dve, dve_chain)

            def gated_wait(sem, value):
                dve.wait_ge(sem, value)
                dve.sem_inc(dve_gate, 1)

            for credit in (logits_made, logits_ready, xT_made, xT_ready):
                dve.sem_inc(credit, 1)
            dve.wait_ge(weights_in, 80)
            chain.then(dve.tensor_scalar(rraw[:], rraw[:], ln2[:, 0:1], None, ALU.mult))
            chain.ready()
            split_weights(dve, chain, rraw[:], rhi[:], rlo[:])
            chain.ready()
            dve.sem_inc(split_done, 1)
            chain.then(dve.tensor_tensor(square[:], X3[:], X3[:], ALU.mult))
            chain.ready()
            chain.then(dve.tensor_reduce(ms[:], square[:], AX.X, ALU.add))
            chain.ready()
            dve.tensor_scalar(ms[:], ms[:], 1.0 / C, RMS_EPS, ALU.mult, ALU.add).then_inc(ms_made, 1)
            dve.wait_ge(root_made, 1)
            chain.then(dve.reciprocal(inv[:], root[:]))
            chain.ready()
            before = chain.n

            def split(n):
                chain.enter(n * 2 + before)
                tiles = bass.ds(n * CT, CT)
                chain.then(dve.tensor_tensor(flat[:], X3[:, tiles, :], bcast(inv[:, tiles], 2, C), ALU.mult))
                gated_wait(xT_ready, n + 1)
                chain.ready()
                chain.then(dve.tensor_copy(pair[:, :, 0:C].bitcast(F32R), flat[:]))
                chain.ready()
                dve.tensor_tensor(pair[:, :, C:2 * C], flat[:], pair[:, :, 0:C], ALU.subtract).then_inc(pair_made, 1)
                chain.leave(2, 0)

            def take_rows(n):
                gated_wait(xT_ready, n + 2)
                gated_wait(logits_ready, n + 1)
                gated_wait(fT_made, n + 1)
                dve.tensor_copy(xT[:], pT[:]).then_inc(xT_made, 1)

            def take_logits(n):
                gated_wait(logits_ready, n + 2)
                tiles = bass.ds(n * CT, CT) if not isinstance(n, int) else slice(n * CT, (n + 1) * CT)
                dve.tensor_copy(logits[:, tiles, :], pL[:, 0:CT * NE].rearrange("p (t e) -> p t e", e=NE)) \
                    .then_inc(logits_made, 1)

            split(0)
            with dve.Fori(0, N - 1) as n:
                take_rows(n)
                split(n + 1)
                take_logits(n)
            take_rows(N - 1)
            take_logits(N - 1)
            chain.n = before + 2 * N
            dve.wait_ge(logits_made, N + 1)
            chain.then(dve.tensor_reduce(top[:], logits[:], AX.X, ALU.max))
            chain.ready()
            dve.tensor_tensor(prob[:], logits[:], bcast(top[:], 2, NE), ALU.subtract).then_inc(margin_made, 1)
            dve.wait_ge(exp_made, 1)
            chain.then(dve.tensor_reduce(total[:], prob[:], AX.X, ALU.add))
            chain.ready()
            chain.then(dve.reciprocal(total[:], total[:]))
            chain.ready()
            chain.then(dve.tensor_tensor(prob[:], prob[:], bcast(total[:], 2, NE), ALU.mult))
            chain.ready()
            chain.then(dve.tensor_tensor(above[:], bcast(prob[:], 2, NE), bcast(prob[:], 3, NE), ALU.is_gt))
            chain.then(dve.tensor_tensor(level[:], bcast(prob[:], 2, NE), bcast(prob[:], 3, NE), ALU.is_ge))
            chain.ready()
            chain.then(dve.tensor_tensor(level[:].rearrange("p t a b -> p t (a b)"),
                                         level[:].rearrange("p t a b -> p t (a b)"),
                                         bcast(earlier[:].rearrange("p a b -> p (a b)"), 1, TILES), ALU.mult))
            chain.ready()
            chain.then(dve.tensor_tensor(above[:], above[:], level[:], ALU.max))
            chain.ready()
            chain.then(dve.tensor_reduce(rank[:], above[:], AX.X, ALU.add))
            chain.ready()
            chain.then(dve.tensor_scalar(rank[:], rank[:], TOPK - 0.5, None, ALU.is_lt))
            chain.ready()
            chain.then(dve.tensor_tensor(prob[:], prob[:], rank[:], ALU.mult))
            chain.ready()
            chain.then(dve.tensor_reduce(total[:], prob[:], AX.X, ALU.add))
            chain.ready()
            chain.then(dve.tensor_scalar(total[:], total[:], 1e-9, None, ALU.add))
            chain.ready()
            chain.then(dve.reciprocal(total[:], total[:]))
            chain.ready()
            chain.then(dve.tensor_tensor(weight[:], prob[:], bcast(total[:], 2, NE), ALU.mult))
            chain.ready()


def hidden_blocks():
    out = []
    for m in range(HM):
        rows = min(P, HIDDEN - m * P)
        out.append((rows, m * P // EHID, (m * P + rows - 1) // EHID + 1))
    return out


class At:

    def __init__(self, k, i=None):
        self.k, self.i, self.odd = k, i, k % 2

    def plus(self, n):
        return At(self.k + n, self.i)

    def of(self, per):
        return self.k * per if self.i is None else self.i * (2 * per) + self.k * per

    def span(self, per, start=0, size=None):
        size = per if size is None else size
        first = self.of(per) + start
        return slice(first, first + size) if self.i is None else bass.ds(first, size)


def experts(nc, d, H, X3, fT, weight, weights, out):
    EARLY = 2
    FIRST = 5
    blocks = hidden_blocks()
    starts = np.cumsum([0] + [(e1 - e0) * C for _, e0, e1 in blocks])
    with ExitStack() as ctx:
        m = Scope(nc, ctx, "ex")
        w1hi, w1lo, w3hi, w3lo, w2 = weights
        act1 = m.sb("act1", [P, 2, CH])
        hidden = m.sb("hidden", [P, HM, CH])
        by_expert = m.sb("by_expert", [P, CT, NE * C])
        scaled = m.sb("scaled", [P, 2, NE, C])
        mixed = m.sb("mixed", [P, CT, C])
        pA = m.ps("pA", [P, 2, 512])
        pB = m.ps("pB", [P, 2, 512])
        pY = m.ps("pY", [P, CT, 512])

        x3_added = m.sem("x3_added")
        a_ready = m.sem("a_ready")
        b_ready = m.sem("b_ready")
        act1_made = m.sem("act1_made")
        hidden_made = m.sem("hidden_made")
        hidden_used = m.sem("hidden_used")
        y_ready = m.sem("y_ready")
        y_copied = m.sem("y_copied")
        y_scaled = m.sem("y_scaled")
        mixed_made = m.sem("mixed_made")
        out_made = m.sem("out_made")
        stored = m.sem("stored")
        pe_gate, act_gate, dve_gate, sp_gate = (m.sem(f"{e}_gate") for e in ("pe", "act", "dve", "sp"))
        block = ctx.enter_context(nc.Block())
        N = BATCH * CHUNKS

        @block.sync
        def _(sp):
            rows = out.rearrange("b (t p) c -> p (b t) c", p=P)
            with sp.Fori(0, N) as n:
                sp.wait_ge(out_made, n + 1)
                sp.sem_inc(sp_gate, 1)
                sp.dma_start(rows[:, bass.ds(n * CT, CT), :], H[:, bass.ds(n * CT, CT), :]).then_inc(stored, 16)
            sp.wait_ge(stored, 16 * N)

        @block.gpsimd
        def _(pool):
            pool.tensor_tensor(H[:], H[:], X3[:], ALU.add).then_inc(x3_added, 1)

        @block.tensor
        def _(pe):
            def gated_wait(sem, value):
                pe.wait_ge(sem, value)
                pe.sem_inc(pe_gate, 1)

            def project(n, k):
                rows = blocks[k][0]
                cols = slice(k * P, k * P + rows)
                rhs = fT[:, n.span(CH)]
                gated_wait(act1_made, n.of(HM) + (k + 1))
                for w in (w1hi, w1lo):
                    last = pe.matmul(pA[0:rows, (k + n.odd) % 2, :], w[:, cols], rhs, start=w is w1hi, stop=w is w1lo)
                last.then_inc(a_ready, 1)
                gated_wait(hidden_made, n.of(HM) + (k + 1))
                for w in (w3hi, w3lo):
                    last = pe.matmul(pB[0:rows, (k + n.odd) % 2, :], w[:, cols], rhs, start=w is w3hi, stop=w is w3lo)
                last.then_inc(b_ready, 1)

            def reduce(n, k):
                rows, e0, e1 = blocks[k]
                gated_wait(hidden_made, n.of(HM) + (k + 3))
                for t in range(CT):
                    if k == 0:
                        gated_wait(y_copied, n.of(CT) + (t + 1))
                    last = pe.matmul(pY[:, t, e0 * C:e1 * C], hidden[0:rows, k, t * P:(t + 1) * P],
                                     w2[0:rows, int(starts[k]):int(starts[k + 1])], start=k == 0,
                                     stop=k == HM - 1, skip_group_check=True)
                    if k == HM - 1:
                        last.then_inc(y_ready, 1)
                if k < HM - 1:
                    last.then_inc(hidden_used, 1)

            def chunk(n, last):
                for k in range(EARLY, HM):
                    project(n, k)
                    if k >= FIRST - 1:
                        reduce(n, k - (FIRST - 1))
                left = list(range(HM - FIRST + 1, HM))
                for k in left:
                    if not last and k >= HM - EARLY:
                        project(n.plus(1), k - (HM - EARLY))
                    reduce(n, k)

            for k in range(EARLY):
                project(At(0), k)
            with pe.Fori(0, N // 2 - 1) as i:
                chunk(At(0, i), False)
                chunk(At(1, i), False)
            chunk(At(N - 2), False)
            chunk(At(N - 1), True)

        @block.scalar
        def _(act):
            def gated_wait(sem, value):
                act.wait_ge(sem, value)
                act.sem_inc(act_gate, 1)

            act.sem_inc(act1_made, 2)
            act.sem_inc(y_copied, CT)

            def silu(n, k):
                rows = blocks[k][0]
                gated_wait(a_ready, n.of(HM) + (k + 1))
                gated_wait(hidden_made, n.of(HM) + (k + 1))
                act.activation(act1[0:rows, (k + n.odd) % 2, :], pA[0:rows, (k + n.odd) % 2, :], ACT.Silu).then_inc(act1_made, 1)

            def take_y(n, t):
                gated_wait(y_ready, n.of(CT) + (t + 1))
                gated_wait(y_scaled, n.of(CT) + (t + 1))
                act.activation(by_expert[:, t, :], pY[:, t, :], ACT.Copy).then_inc(y_copied, 1)

            def chunk(n):
                for k in range(EARLY):
                    silu(n, k)
                for t in range(CT):
                    take_y(n.plus(-1), t)
                    if t % 2:
                        silu(n, EARLY + t // 2)
                for k in range(EARLY + CT // 2, HM):
                    silu(n, k)

            for k in range(HM):
                silu(At(0), k)
            with act.Fori(0, N // 2 - 1) as i:
                chunk(At(1, i))
                chunk(At(2, i))
            chunk(At(N - 1))
            for t in range(CT):
                take_y(At(N - 1), t)

        @block.vector
        def _(dve):
            def gated_wait(sem, value):
                dve.wait_ge(sem, value)
                dve.sem_inc(dve_gate, 1)

            dve.sem_inc(hidden_made, 2)
            dve.sem_inc(y_scaled, CT)
            dve.sem_inc(hidden_used, HM - 1)
            dve.wait_ge(x3_added, 1)

            def multiply(n, k):
                rows = blocks[k][0]
                gated_wait(b_ready, n.of(HM) + (k + 1))
                gated_wait(act1_made, n.of(HM) + (k + 3))
                if k < HM - 1:
                    gated_wait(hidden_used, n.of((HM - 1)) + (k + 1))
                else:
                    gated_wait(y_copied, n.of(CT) + CT)
                dve.tensor_tensor(hidden[0:rows, k, :], pB[0:rows, (k + n.odd) % 2, :], act1[0:rows, (k + n.odd) % 2, :],
                                  ALU.mult).then_inc(hidden_made, 1)

            def scale(n, t):
                gated_wait(y_copied, n.of(CT) + (t + 1 + CT))
                gated_wait(mixed_made, n.of(CT) + (t + 1))
                dve.tensor_tensor(scaled[:, t % 2, :, :], by_expert[:, t, :].rearrange("p (e c) -> p e c", c=C),
                                  bcast(weight[:, n.span(CT, t, 1), :].rearrange("p a e -> p (a e)"), 2, C),
                                  ALU.mult).then_inc(y_scaled, 1)

            def mix(n, t):
                gated_wait(y_scaled, n.of(CT) + (t + 1 + CT))
                dve.tensor_reduce(mixed[:, t, :], scaled[:, t % 2, :, :].rearrange("p e c -> p c e"),
                                  AX.X, ALU.add).then_inc(mixed_made, 1)

            def finish(n):
                gated_wait(mixed_made, n.of(CT) + (CT + 2))
                tiles = n.span(CT)
                dve.tensor_tensor(H[:, tiles, :], H[:, tiles, :], mixed[:], ALU.add).then_inc(out_made, 1)

            dve.sem_inc(mixed_made, 2)
            def chunk(n):
                for k in range(HM):
                    multiply(n, k)
                    t = k - EARLY - 1
                    if 0 <= t < CT:
                        scale(n.plus(-1), t)
                    if 0 < t <= CT:
                        mix(n.plus(-1), t - 1)
                    if t == CT + 1:
                        finish(n.plus(-1))

            for k in range(HM):
                multiply(At(0), k)
            with dve.Fori(0, N // 2 - 1) as i:
                chunk(At(1, i))
                chunk(At(2, i))
            chunk(At(N - 1))
            for t in range(CT + 1):
                if t < CT:
                    scale(At(N - 1), t)
                if t:
                    mix(At(N - 1), t - 1)
            finish(At(N - 1))


_OUT = ("out", (BATCH, SEQ, C))


def program(nc, d, out):
    with ExitStack() as ctx:
        m = Scope(nc, ctx, "all")
        H = m.sb("H", [P, TILES, C])
        XC = m.sb("XC", [P, TILES, C])
        scale = m.sb("scale", [P, TILES])
        ident = m.sb("ident", [P, P])
        identb = m.sb("identb", [P, P], BF16)
        rawmasks = m.sb("rawmasks", [P, 2, P])
        masks = m.sb("masks", [P, 2, P], BF16)
        consts_in = m.sem("consts_in")
        with nc.Block() as block:
            @block.sync
            def _(sp):
                sp.dma_start(ident[:], d["ident"]).then_inc(consts_in, 16)
                sp.dma_start(rawmasks[:], d["masks"]).then_inc(consts_in, 16)

            @block.vector
            def _(dve):
                dve.wait_ge(consts_in, 32)
                dve.tensor_copy(identb[:], ident[:])
                dve.tensor_copy(masks[:], rawmasks[:])
        token_embedding(nc, d, H, XC, scale)
        gated_attention(nc, d, H, XC, scale, ident)
        normed_input(nc, H, XC, XC, scale)
        causal_attention(nc, d, XC, scale, ident, identb, masks)
        with ExitStack() as late:
            r = Scope(nc, late, "moe")
            fT = r.sb("fT", [P, BATCH * SEQ], F32R)
            weight = r.sb("weight", [P, TILES, NE])
            split = [r.sb(name, [P, HIDDEN], F32R) for name in ("w1hi", "w1lo", "w3hi", "w3lo")]
            w2 = r.sb("w2", [P, sum(e1 - e0 for _, e0, e1 in hidden_blocks()) * C])
            weights = (*split, w2)
            routing(nc, d, XC, ident, fT, weight, weights)
            experts(nc, d, H, XC, fT, weight, weights, out)


def down_blocks(w2):
    rows = np.ascontiguousarray(w2.transpose(0, 2, 1)).reshape(HIDDEN, C)
    parts = []
    for k, (n, e0, e1) in enumerate(hidden_blocks()):
        for e in range(e0, e1):
            block = np.zeros((P, C), np.float32)
            a, b = max(k * P, e * EHID), min(k * P + n, (e + 1) * EHID)
            block[a - k * P:b - k * P] = rows[a:b]
            parts.append(block)
    return np.ascontiguousarray(np.concatenate(parts, axis=1))


def shape_constants():
    freq = 1.0 / 10000.0 ** (np.arange(0, HD, 2, dtype=np.float32) / HD)
    angle = np.outer(np.arange(SEQ, dtype=np.float32), freq)
    angle = np.concatenate([angle, angle], axis=-1)
    cos, sin = np.cos(angle).astype(np.float32), np.sin(angle).astype(np.float32)
    sin[:, :HD // 2] *= -1
    row, col = np.arange(P)[:, None], np.arange(P)[None, :]
    masks = np.stack([np.where(row > col, np.float32(-1e30), np.float32(0)),
                      np.where(col > row, np.float32(-1e30), np.float32(0))], axis=1)
    tiled = [np.ascontiguousarray(t.reshape(BT, P, HD).transpose(1, 0, 2)) for t in (cos, sin)]
    earlier = np.tril(np.ones((NE, NE), np.float32), -1)
    return {"earlier": np.ascontiguousarray(np.broadcast_to(earlier, (P, NE, NE))), "cos": tiled[0], "sin": tiled[1], "masks": np.ascontiguousarray(masks.astype(np.float32))}


def kernel(x, L0_tok_bases, L0_tok_W_spline, L0_tok_b_spline, L0_tok_W_base, L0_tok_b_base, L0_attn_g,
           L0_attn_W_uv, L0_attn_b_uv, L0_attn_gamma, L0_attn_beta, L0_attn_W_o, L0_attn_b_o, L0_ffn_ln1_w,
           L0_ffn_ln2_w, L0_ffn_wq, L0_ffn_wk, L0_ffn_wv, L0_ffn_wo, L0_ffn_router_w, L0_ffn_w1, L0_ffn_w2,
           L0_ffn_w3):
    import concourse.bacc as bacc
    from concourse.bass_utils import run_bass_kernel_spmd as run

    asc = np.ascontiguousarray
    bases, ws = np.asarray(L0_tok_bases), np.asarray(L0_tok_W_spline).reshape(C, C, 3)
    one = np.ones((C, 1), np.float32)
    wb = np.asarray(L0_tok_W_base)
    arrays = {
        "x": asc(np.asarray(x).reshape(BATCH, C, SEQ)),
        "wtok": asc(np.stack([np.concatenate([wb.T, ws[:, :, 0].T]),
                              np.concatenate([ws[:, :, 1].T, ws[:, :, 2].T])], axis=1)),
        "tok_factor": asc(np.concatenate([np.concatenate([one, bases[:, 0:1]]),
                                          np.concatenate([bases[:, 1:2], bases[:, 2:3]])], axis=1)),
        "b_base": asc(L0_tok_b_base), "b_spline": asc(L0_tok_b_spline),
        "g": asc(np.asarray(L0_attn_g).reshape(1)),
        "W_uv": asc(L0_attn_W_uv), "b_uv": asc(L0_attn_b_uv),
        "ga_cols": asc(np.concatenate([np.asarray(L0_attn_b_uv).reshape(3, GH), np.asarray(L0_attn_gamma),
                                       np.asarray(L0_attn_beta)]).T),
        "W_o": asc(L0_attn_W_o), "b_o": asc(L0_attn_b_o),
        "wqkv": asc(np.concatenate([np.asarray(L0_ffn_wq), np.asarray(L0_ffn_wk), np.asarray(L0_ffn_wv)]).T),
        "wo": asc(np.asarray(L0_ffn_wo).T), "ln1_w": asc(np.asarray(L0_ffn_ln1_w).reshape(C, 1)),
        "ident": np.eye(P, dtype=np.float32),
        "router": asc(np.asarray(L0_ffn_router_w).T), "ln2_w": asc(np.asarray(L0_ffn_ln2_w).reshape(C, 1)),
        "w1": asc(np.asarray(L0_ffn_w1).reshape(HIDDEN, C).T), "w3": asc(np.asarray(L0_ffn_w3).reshape(HIDDEN, C).T),
        "w2": down_blocks(np.asarray(L0_ffn_w2)),
        **shape_constants(),
    }
    nc = bacc.Bacc("TRN2", target_bir_lowering=False, num_devices=1)
    d = {name: nc.dram_tensor(name, a.shape, mybir.dt.from_np(a.dtype), kind="ExternalInput").ap()
         for name, a in arrays.items()}
    out = nc.dram_tensor(_OUT[0], _OUT[1], F32, kind="ExternalOutput").ap()
    program(nc, d, out)
    r = run(nc, [arrays], core_ids=[0])
    return r.results[0]["out"]
```

```python
from contextlib import ExitStack

import numpy as np

import concourse.bass as bass
from concourse import mybir

F32 = mybir.dt.float32
F32R = mybir.dt.float32r
BF16 = mybir.dt.bfloat16
ALU = mybir.AluOpType
ACT = mybir.ActivationFunctionType
AX = mybir.AxisListType

P = 128
BATCH, SEQ, C = 2, 4096, 64
TILES = BATCH * SEQ // P
BT = SEQ // P
CH = 512
CT = CH // P
CHUNKS = SEQ // CH
GH = 128
NH, NKV, HD = 4, 2, 16
QKV = (NH + 2 * NKV) * HD
ROPED = (NH + NKV) * HD
Q_PARTS = (0, 0, 1, 0, 2, 1)
K_PARTS = (0, 1, 0, 2, 0, 1)
STACK = len(Q_PARTS) * HD
SHIFT = 3
VW = 32
NE, TOPK, EHID = 8, 2, 170
HIDDEN = NE * EHID
HM = -(-HIDDEN // P)
LN_EPS, RMS_EPS, NORM_EPS = 1e-5, 1e-6, 1e-5


def bcast(ap, axis, n):
    a = ap.unsqueeze(axis)
    shape = list(a.shape)
    shape[axis] = n
    return a.broadcast_to(shape)


class Chain:

    def __init__(self, eng, sem):
        self.eng, self.sem, self.n, self.base = eng, sem, 0, None

    def then(self, ins):
        ins.then_inc(self.sem, 1)
        self.n += 1

    def ready(self):
        self.eng.wait_ge(self.sem, self.n if self.base is None else self.base + self.n)

    def enter(self, base):
        self.outer, self.base, self.n = self.n, base, 0

    def leave(self, per, times):
        assert self.n == per, self.n
        self.base, self.n = None, self.outer + per * times


class At:

    def __init__(self, k, i=None):
        self.k, self.i, self.odd = k, i, k % 2

    def plus(self, n):
        return At(self.k + n, self.i)

    def of(self, per):
        return self.k * per if self.i is None else self.i * (2 * per) + self.k * per

    def span(self, per, start=0, size=None):
        size = per if size is None else size
        first = self.of(per) + start
        return slice(first, first + size) if self.i is None else bass.ds(first, size)


class Scope:

    def __init__(self, nc, ctx, tag):
        self.nc, self.ctx, self.tag = nc, ctx, tag

    def sb(self, name, shape, dt=F32):
        return self.ctx.enter_context(self.nc.sbuf_tensor(f"{self.tag}.{name}", shape, dt))

    def ps(self, name, shape, dt=F32):
        return self.ctx.enter_context(self.nc.psum_tensor(f"{self.tag}.{name}", shape, dt))

    def sem(self, name):
        return self.ctx.enter_context(self.nc.semaphore(f"{self.tag}.{name}"))


class Weights:

    def __init__(self, m, shapes, transfers):
        self.by_name = {name: m.sb(name, shape) for name, shape in shapes.items()}
        self.arrived = m.sem("arrived")
        self.transfers = transfers
        self.count = 16 * len(transfers)

    def __getitem__(self, name):
        return self.by_name[name]

    def load(self, eng):
        for name, half, source in self.transfers:
            target = self.by_name[name]
            eng.dma_start(target[:] if half is None else target[half:half + C, :], source).then_inc(self.arrived, 16)


def gated_weights(nc, ctx, d):
    return Weights(Scope(nc, ctx, "gw"),
                   {"wraw": [P, 3 * GH],
                    "wo": [GH, C],
                    "cols": [P, 7],
                    "bv": [P, GH], "bo": [P, C]},
                   [("wraw", half, d["W_uv"]) for half in (0, C)] +
                   [("wo", None, d["W_o"]), ("cols", None, d["ga_cols"]),
                    ("bv", None, d["b_uv"][GH:2 * GH].partition_broadcast(P)),
                    ("bo", None, d["b_o"].partition_broadcast(P))])


def causal_weights(nc, ctx, d):
    return Weights(Scope(nc, ctx, "cw"),
                   {"wraw": [P, QKV],
                    "woraw": [P, C], "ln1": [P, 1],
                    "cos": [P, BT, HD],
                    "sin": [P, BT, HD]},
                   [(name, half, d[source]) for half in (0, C)
                    for name, source in (("wraw", "wqkv"), ("woraw", "wo"), ("ln1", "ln1_w"))] +
                   [("cos", None, d["cos"]), ("sin", None, d["sin"])])


def token_embedding(nc, d, H, XC, scale, ident, next_weights):
    W = 1024
    WT = W // P
    STEPS = SEQ // W
    with ExitStack() as ctx:
        m = Scope(nc, ctx, "tok")
        x2 = m.sb("x2", [P, BATCH, SEQ])
        wtok = m.sb("wtok", [P, 2, C])
        factor = m.sb("factor", [P, 2])
        biases = m.sb("biases", [P, 2, C])
        bias = m.sb("bias", [P, C])
        g = m.sb("g", [P, 1])
        feat = m.sb("feat", [P, 2, 2, W])
        square = m.sb("square", [P, WT, C])
        sums = m.sb("sums", [P, WT])
        mean = m.sb("mean", [P, WT])
        var = m.sb("var", [P, TILES])
        shifted = m.sb("shifted", [P, TILES])
        root = m.sb("root", [P, 2, TILES])
        inv = m.sb("inv", [P, TILES])
        norm = m.sb("norm", [P, TILES])
        hT = m.sb("hT", [C, 2, W // 2])
        pH = m.ps("pH", [P, 2, 512])
        pC = m.ps("pC", [C, 2, 512])

        weights_in = m.sem("weights_in")
        x_in = [m.sem(f"x_in{n}") for n in range(BATCH * STEPS)]
        sigmoids_made = m.sem("sigmoids_made")
        silu_made = m.sem("silu_made")
        hT_ready = m.sem("hT_ready")
        hT_made = m.sem("hT_made")
        h_ready = m.sem("h_ready")
        h_free = m.sem("h_free")
        var_made = m.sem("var_made")
        roots_made = m.sem("roots_made")
        dve_chain = m.sem("dve_chain")
        pe_gate, dve_gate = m.sem("pe_gate"), m.sem("dve_gate")
        block = ctx.enter_context(nc.Block())

        @block.sync
        def _(sp):
            for n in range(BATCH * STEPS):
                b, own = n // STEPS, slice(n % STEPS * W, (n % STEPS + 1) * W)
                for half in (0, C):
                    sp.dma_start(x2[half:half + C, b, own], d["x"][b, :, own]).then_inc(x_in[n], 16)
            next_weights.load(sp)

        @block.scalar
        def _(act):
            act.dma_start(wtok[:], d["wtok"]).then_inc(weights_in, 16)
            act.dma_start(factor[:], d["tok_factor"]).then_inc(weights_in, 16)
            act.dma_start(biases[:, 0, :], d["b_base"].partition_broadcast(P)).then_inc(weights_in, 16)
            act.dma_start(biases[:, 1, :], d["b_spline"].partition_broadcast(P)).then_inc(weights_in, 16)
            act.dma_start(g[:], d["g"].partition_broadcast(P)).then_inc(weights_in, 16)
            act.wait_ge(weights_in, 80)

            def take_rows(n):
                for half in range(2):
                    act.wait_ge(hT_ready, 2 * n + half + 1)
                    if n:
                        act.wait_ge(h_ready, n)
                    act.activation(hT[:, half, :], pC[:, half, :], ACT.Copy).then_inc(hT_made, 1)

            act.sem_inc(hT_made, 2)
            for n in range(BATCH * STEPS):
                b, own = n // STEPS, slice(n % STEPS * W, (n % STEPS + 1) * W)
                act.wait_ge(x_in[n], 32)
                if n >= 2:
                    act.wait_ge(hT_ready, 2 * (n - 1))
                for f in range(2):
                    act.activation(feat[:, n % 2, f, :], x2[:, b, own], ACT.Sigmoid,
                                   scale=factor[:, f:f + 1]).then_inc(sigmoids_made, 1)
                if n:
                    take_rows(n - 1)
            take_rows(BATCH * STEPS - 1)
            act.wait_ge(var_made, 1)
            act.activation(root[:, 0, :], shifted[:], ACT.Sqrt).then_inc(roots_made, 1)
            act.activation(root[:, 1, :], var[:], ACT.Sqrt).then_inc(roots_made, 1)

        @block.tensor
        def _(pe):
            def embed(n):
                pe.wait_ge(silu_made, n.of(1) + 1)
                pe.wait_ge(sigmoids_made, n.of(2) + 2)
                for half in range(2):
                    pe.wait_ge(hT_made, n.of(2) + (half + 1))
                    for f in range(2):
                        last = pe.matmul(pC[:, half, :], wtok[:, f, :],
                                         feat[:, n.odd, f, half * (W // 2):(half + 1) * (W // 2)],
                                         start=f == 0, stop=f == 1)
                    last.then_inc(hT_ready, 1)

            def turn(n):
                pe.wait_ge(hT_made, n.of(2) + 4)
                pe.wait_ge(h_free, n.of(1) + 1)
                pe.sem_inc(pe_gate, 1)
                for t in range(WT):
                    half, col = divmod(t * P, W // 2)
                    last = pe.transpose(pH[:, n.odd, t * C:(t + 1) * C], hT[:, half, col:col + P], ident[0:C, 0:C])
                last.then_inc(h_ready, 1)

            pe.wait_ge(weights_in, 80)
            embed(At(0))
            with pe.Fori(0, BATCH * STEPS // 2 - 1) as i:
                for n in (At(1, i), At(2, i)):
                    embed(n)
                    turn(n.plus(-1))
            last_step = At(BATCH * STEPS - 1)
            embed(last_step)
            turn(last_step.plus(-1))
            turn(last_step)

        @block.gpsimd
        def _(pool):
            for b in range(BATCH):
                with pool.Fori(0, STEPS // 2) as i:
                    for j in range(2):
                        pool.wait_ge(sigmoids_made, 4 * i + (2 * STEPS * b + 2 * j + 1))
                        pool.tensor_tensor(feat[0:C, j, 0, :], feat[0:C, j, 0, :],
                                           x2[0:C, b, bass.ds(i * (2 * W) + j * W, W)],
                                           ALU.mult).then_inc(silu_made, 1)

        @block.vector
        def _(dve):
            chain = Chain(dve, dve_chain)
            dve.sem_inc(h_free, 2)
            dve.wait_ge(weights_in, 80)
            chain.then(dve.tensor_tensor(bias[:], biases[:, 0, :], biases[:, 1, :], ALU.add))
            chain.ready()
            STATS = 7

            def chained():
                chain.ready()
                dve.sem_inc(dve_gate, 1)

            with dve.Fori(0, BATCH * STEPS // 2) as i:
                for j in range(2):
                    chain.enter(i * (2 * STATS) + (j * STATS + 1))
                    dve.wait_ge(h_ready, 2 * i + (j + 1))
                    tiles = bass.ds(i * (2 * WT) + j * WT, WT)
                    dve.tensor_tensor(H[:, tiles, :], pH[:, j, :].rearrange("p (t c) -> p t c", c=C),
                                      bcast(bias[:], 1, WT), ALU.add).then_inc(h_free, 1)
                    dve.wait_ge(h_free, 2 * i + (j + 3))
                    dve.sem_inc(dve_gate, 1)
                    chain.then(dve.tensor_reduce(sums[:], H[:, tiles, :], AX.X, ALU.add))
                    chained()
                    chain.then(dve.tensor_scalar(mean[:], sums[:], 1.0 / C, None, ALU.mult))
                    chained()
                    chain.then(dve.tensor_tensor(XC[:, tiles, :], H[:, tiles, :], bcast(mean[:], 2, C), ALU.subtract))
                    chained()
                    chain.then(dve.tensor_tensor(square[:], XC[:, tiles, :], XC[:, tiles, :], ALU.mult))
                    chained()
                    chain.then(dve.tensor_reduce(sums[:], square[:], AX.X, ALU.add))
                    chained()
                    chain.then(dve.tensor_scalar(mean[:], sums[:], 1.0 / C, None, ALU.mult))
                    chained()
                    chain.then(dve.tensor_copy(var[:, tiles], mean[:]))
                    chain.leave(STATS, 0)
            chain.n = 1 + BATCH * STEPS * STATS
            chain.ready()
            dve.tensor_scalar(shifted[:], var[:], LN_EPS, None, ALU.add).then_inc(var_made, 1)
            dve.wait_ge(roots_made, 2)
            chain.then(dve.reciprocal(inv[:], root[:, 0, :]))
            chain.ready()
            chain.then(dve.tensor_tensor(norm[:], root[:, 1, :], inv[:], ALU.mult))
            chain.ready()
            chain.then(dve.tensor_scalar(norm[:], norm[:], NORM_EPS, None, ALU.max))
            chain.ready()
            chain.then(dve.reciprocal(norm[:], norm[:]))
            chain.ready()
            chain.then(dve.scalar_tensor_tensor(out=scale[:], in0=norm[:], scalar=g[:, 0:1], in1=inv[:],
                                                op0=ALU.mult, op1=ALU.mult))
            chain.ready()


def split_weights(dve, chain, raw, hi, lo):
    chain.then(dve.tensor_copy(hi, raw))
    chain.ready()
    chain.then(dve.tensor_tensor(lo, raw, hi.bitcast(F32), ALU.subtract))


def gated_attention(nc, H, XC, scale, ident, weights):
    PAIRS = BT // 2
    AHEAD = 3
    SLOTS = 4
    LASTQ = CHUNKS - 1
    with ExitStack() as ctx:
        m = Scope(nc, ctx, "ga")
        wraw, wo, cols, bv, bo = (weights[name] for name in ("wraw", "wo", "cols", "bv", "bo"))
        whi = m.sb("whi", [P, 3 * GH], F32R)
        wlo = m.sb("wlo", [P, 3 * GH], F32R)
        bcol, gb = cols[:, 0:3], cols[:, 3:7]
        warm = m.sb("warm", [P, 1])
        xn = m.sb("xn", [P, CT, C])
        pair = m.sb("pair", [P, CT, 2 * C])
        qhi = m.sb("qhi", [P, SEQ], F32R)
        qlo = m.sb("qlo", [P, SEQ], F32R)
        khi = m.sb("khi", [P, SEQ], F32R)
        klo = m.sb("klo", [P, SEQ], F32R)
        Vhi = m.sb("Vhi", [P, BT, GH], F32R)
        Vlo = m.sb("Vlo", [P, BT, GH], F32R)
        uT = m.sb("uT", [P, SEQ])
        attn = m.sb("attn", [P, 2, 2 * CH])
        attn_hi = m.sb("attn_hi", [P, SLOTS, 2 * CH], F32R)
        attn_lo = m.sb("attn_lo", [P, 2, 2 * CH], F32R)
        gated = m.sb("gated", [P, CH])
        rows = m.sb("rows", [P, CT, C])
        square = m.sb("square", [P, CT, C])
        folded = m.sb("folded", [P, CT, C // 2])
        sums = m.sb("sums", [P, CT])
        mean = m.sb("mean", [P, CT])
        xT = attn_hi[:, 0, 0:CH]
        base, vb = attn[:, 0, 0:CH], attn[:, 0, CH:2 * CH].rearrange("p (t c) -> p t c", c=GH)
        q, k = attn[:, 1, 0:CH], attn[:, 1, CH:2 * CH]
        vs = gated[:].rearrange("p (t c) -> p t c", c=GH)
        pS = m.ps("pS", [P, 4, 512])
        pO = m.ps("pO", [P, 512])
        pY = m.ps("pY", [P, 512])
        pBase, pU, pV, pT = pS[:, 0, :], pS[:, 1, :], pS[:, 2, :], pS[:, 3, :]

        split_done = m.sem("split_done")
        pair_made = m.sem("pair_made")
        xT_ready = m.sem("xT_ready")
        xT_made = m.sem("xT_made")
        base_ready = m.sem("base_ready")
        u_ready = m.sem("u_ready")
        v_ready = m.sem("v_ready")
        vb_made = m.sem("vb_made")
        vs_made = m.sem("vs_made")
        vhi_made = m.sem("vhi_made")
        vlo_made = m.sem("vlo_made")
        base_made = m.sem("base_made")
        u_made = m.sem("u_made")
        q_made = m.sem("q_made")
        qhi_made = m.sem("qhi_made")
        qlo_made = m.sem("qlo_made")
        k_made = m.sem("k_made")
        scores_ready = m.sem("scores_ready")
        squared = m.sem("squared")
        relu_made = m.sem("relu_made")
        hi_made = m.sem("hi_made")
        lo_made = m.sem("lo_made")
        pairs_summed = m.sem("pairs_summed")
        gated_made = m.sem("gated_made")
        y_ready = m.sem("y_ready")
        h_made = m.sem("h_made")
        bo_added = m.sem("bo_added")
        dve_chain = m.sem("dve_chain")
        pool_chain = m.sem("pool_chain")
        pe_gate, act_gate, dve_gate, pool_gate = (m.sem(f"{e}_gate") for e in ("pe", "act", "dve", "pool"))
        block = ctx.enter_context(nc.Block())

        @block.tensor
        def _(pe):
            def gated_wait(sem, value):
                pe.wait_ge(sem, value)
                pe.sem_inc(pe_gate, 1)

            pe.wait_ge(weights.arrived, weights.count)
            pe.wait_ge(split_done, 1)
            with pe.Fori(0, BATCH) as b:
                n0 = b * CHUNKS

                def turn(c):
                    gated_wait(pair_made, n0 + c + 1)
                    gated_wait(xT_made, n0 + c + 1)
                    for t in range(CT):
                        last = pe.transpose(pT[:, t * P:(t + 1) * P], pair[:, t, :], ident[:])
                    last.then_inc(xT_ready, 1)

                def project_rows(out, col, ready):
                    for w in (whi, wlo):
                        last = pe.matmul(out, w[:, col:col + GH], xT, start=w is whi, stop=w is wlo)
                    last.then_inc(ready, 1)

                def project_base_u(c):
                    gated_wait(xT_made, n0 + c + 2)
                    gated_wait(u_made, n0 + c + 1)
                    project_rows(pBase, 2 * GH, base_ready)
                    project_rows(pU, 0, u_ready)

                def project_v(c):
                    gated_wait(vb_made, n0 + c + 1)
                    for t in range(CT):
                        for w in (whi, wlo):
                            last = pe.matmul(pV[:, t * P:(t + 1) * P], xT[:, t * P:(t + 1) * P],
                                             w[:, GH:2 * GH], start=w is whi, stop=w is wlo)
                    last.then_inc(v_ready, 1)

                turn(0)
                with pe.Fori(0, LASTQ) as c:
                    project_base_u(c)
                    turn(c + 1)
                    project_v(c)
                project_base_u(LASTQ)
                project_v(LASTQ)

                gated_wait(qlo_made, n0 + (CHUNKS + 1))
                gated_wait(k_made, n0 + (CHUNKS + 1))
                gated_wait(vlo_made, n0 + (CHUNKS + 1))
                gated_wait(u_made, n0 + (CHUNKS + 1))

                def scores(qb, p):
                    gated_wait(relu_made, (n0 + qb) * PAIRS + (p + 1))
                    qs = slice(qb * CH, (qb + 1) * CH) if isinstance(qb, int) else bass.ds(qb * CH, CH)
                    for j in range(2):
                        kt = slice((2 * p + j) * P, (2 * p + j + 1) * P)
                        out = pS[:, 2 * (p % 2) + j, :]
                        pe.matmul(out, khi[:, kt], qhi[:, qs], start=True, stop=False)
                        pe.matmul(out, khi[:, kt], qlo[:, qs], start=False, stop=False)
                        last = pe.matmul(out, klo[:, kt], qhi[:, qs], start=False, stop=True)
                    last.then_inc(scores_ready, 1)

                def weigh_values(qb, p):
                    if p == 0:
                        gated_wait(gated_made, n0 + qb + 1)
                    for j in range(2):
                        gated_wait(lo_made, 2 * ((n0 + qb) * PAIRS) + (2 * p + j + 5))
                        hi = attn_hi[:, p % SLOTS, j * CH:(j + 1) * CH]
                        lo = attn_lo[:, p % 2, j * CH:(j + 1) * CH]
                        pe.matmul(pO[:], Vhi[:, 2 * p + j, :], hi, start=p == 0 and j == 0, stop=False)
                        pe.matmul(pO[:], Vlo[:, 2 * p + j, :], hi, start=False, stop=False)
                        last = pe.matmul(pO[:], Vhi[:, 2 * p + j, :], lo, start=False,
                                         stop=p == PAIRS - 1 and j == 1)
                    last.then_inc(pairs_summed, 1)

                def project_out(qb):
                    gated_wait(gated_made, n0 + qb + 2)
                    gated_wait(h_made, n0 + qb + 1)
                    for t in range(CT):
                        last = pe.matmul(pY[:, t * C:(t + 1) * C], gated[:, t * P:(t + 1) * P], wo[:],
                                         start=True, stop=True)
                    last.then_inc(y_ready, 1)

                def query_block(qb, last):
                    for p in range(PAIRS):
                        weigh_values(qb, p)
                        if p + AHEAD < PAIRS:
                            scores(qb, p + AHEAD)
                        elif not last:
                            scores(qb + 1, p + AHEAD - PAIRS)
                    project_out(qb)

                for p in range(AHEAD):
                    scores(0, p)
                with pe.Fori(0, LASTQ) as qb:
                    query_block(qb, False)
                query_block(LASTQ, True)

        @block.scalar
        def _(act):
            def gated_wait(sem, value):
                act.wait_ge(sem, value)
                act.sem_inc(act_gate, 1)

            act.sem_inc(u_made, 1)
            act.sem_inc(vs_made, 1)
            act.sem_inc(relu_made, 2)
            act.wait_ge(weights.arrived, weights.count)
            with act.Fori(0, BATCH) as b:
                act.activation(warm[:], cols[:, 0:1], ACT.Silu)
                with act.Fori(0, CHUNKS) as c:
                    n = b * CHUNKS + c
                    gated_wait(base_ready, n + 1)
                    gated_wait(q_made, n + 1)
                    gated_wait(k_made, n + 1)
                    act.activation(base, pBase, ACT.Silu, bias=bcol[:, 2:3]).then_inc(base_made, 1)
                    gated_wait(u_ready, n + 1)
                    act.activation(uT[:, bass.ds(c * CH, CH)], pU, ACT.Silu, bias=bcol[:, 0:1]).then_inc(u_made, 1)
                    gated_wait(q_made, n + 2)
                    act.activation(qhi[:, bass.ds(c * CH, CH)], q, ACT.Copy).then_inc(qhi_made, 1)
                    gated_wait(vb_made, n + 2)
                    gated_wait(vlo_made, n + 1)
                    act.activation(vs, vb, ACT.Silu).then_inc(vs_made, 1)
                    gated_wait(vs_made, n + 2)
                    act.activation(Vhi[:, bass.ds(c * CT, CT), :], vs, ACT.Copy).then_inc(vhi_made, 1)
                with act.Fori(0, CHUNKS * PAIRS // SLOTS) as i:
                    for slot in range(SLOTS):
                        g = (b * (CHUNKS * PAIRS // SLOTS) + i) * SLOTS + slot
                        gated_wait(scores_ready, g + 1)
                        gated_wait(lo_made, 2 * g + 2)
                        banks = pS[:, 2 * (slot % 2):2 * (slot % 2) + 2, :].rearrange("p j q -> p (j q)")
                        act.activation(attn[:, slot % 2, :], banks, ACT.Relu).then_inc(relu_made, 1)
                        gated_wait(relu_made, g + 3)
                        gated_wait(pairs_summed, g + 1)
                        act.activation(attn_hi[:, slot, :], attn[:, slot % 2, :], ACT.Square).then_inc(hi_made, 1)

        @block.gpsimd
        def _(pool):
            chain = Chain(pool, pool_chain)
            FOLDS = 6
            STATS = 7 + 2 * FOLDS

            def fold(src):
                width = C // 2
                for i in range(FOLDS):
                    out = sums[:].unsqueeze(2) if width == 1 else folded[:, :, 0:width]
                    chain.then(pool.tensor_tensor(out, src[:, :, 0:width], src[:, :, width:2 * width], ALU.add))
                    chained()
                    src, width = folded, width // 2

            def chained():
                chain.ready()
                pool.sem_inc(pool_gate, 1)

            pool.sem_inc(k_made, 1)
            pool.sem_inc(pairs_summed, SLOTS)
            pool.wait_ge(weights.arrived, weights.count)
            with pool.Fori(0, BATCH) as b:
                with pool.Fori(0, CHUNKS) as c:
                    chain.enter(b * (CHUNKS * (2 + STATS)) + c * 2)
                    pool.wait_ge(base_made, b * CHUNKS + c + 1)
                    pool.sem_inc(pool_gate, 1)
                    chain.then(pool.tensor_scalar(k, base, gb[:, 1:2], gb[:, 3:4], ALU.mult, ALU.add))
                    chain.ready()
                    hi = khi[:, bass.ds(c * CH, CH)]
                    chain.then(pool.tensor_copy(hi, k))
                    chain.ready()
                    pool.tensor_tensor(klo[:, bass.ds(c * CH, CH)], k, hi.bitcast(F32),
                                       ALU.subtract).then_inc(k_made, 1)
                    chain.leave(2, 0)
                image = bass.ds(b * BT, BT)
                pool.tensor_tensor(H[:, image, :], H[:, image, :], bcast(bo[:], 1, BT), ALU.add).then_inc(bo_added, 1)
                with pool.Fori(0, CHUNKS) as qb:
                    chain.enter(b * (CHUNKS * (2 + STATS)) + qb * STATS + 2 * CHUNKS)
                    pool.wait_ge(h_made, b * CHUNKS + qb + 2)
                    pool.sem_inc(pool_gate, 1)
                    tiles = bass.ds(b * BT + qb * CT, CT)
                    chain.then(pool.tensor_copy(rows[:], H[:, tiles, :]))
                    chained()
                    fold(rows)
                    chain.then(pool.tensor_scalar(mean[:], sums[:], 1.0 / C, None, ALU.mult))
                    chained()
                    chain.then(pool.tensor_tensor(rows[:], rows[:], bcast(mean[:], 2, C), ALU.subtract))
                    chained()
                    chain.then(pool.tensor_copy(XC[:, tiles, :], rows[:]))
                    chain.then(pool.tensor_tensor(square[:], rows[:], rows[:], ALU.mult))
                    chained()
                    fold(square)
                    chain.then(pool.tensor_scalar(mean[:], sums[:], 1.0 / C, None, ALU.mult))
                    chained()
                    chain.then(pool.tensor_copy(scale[:, tiles], mean[:]))
                    chained()
                    chain.leave(STATS, 0)

        @block.vector
        def _(dve):
            chain = Chain(dve, dve_chain)

            def gated_wait(sem, value):
                dve.wait_ge(sem, value)
                dve.sem_inc(dve_gate, 1)

            for credit, many in ((vb_made, 1), (q_made, 1), (vlo_made, 1), (xT_made, 1), (lo_made, 4), (gated_made, 1), (h_made, 1)):
                dve.sem_inc(credit, many)
            dve.sem_inc(xT_ready, 1)
            dve.sem_inc(qlo_made, 1)
            dve.wait_ge(weights.arrived, weights.count)
            split_weights(dve, chain, wraw[:], whi[:], wlo[:])
            chain.ready()
            dve.sem_inc(split_done, 1)
            SPLITS = chain.n
            with dve.Fori(0, BATCH) as b:
                n0 = b * CHUNKS

                def split(c):
                    chain.enter((n0 + c) * 2 + SPLITS)
                    tiles = bass.ds(b * BT + c * CT, CT)
                    chain.then(dve.tensor_tensor(xn[:], XC[:, tiles, :], bcast(scale[:, tiles], 2, C), ALU.mult))
                    gated_wait(xT_ready, n0 + c + 1)
                    chain.ready()
                    chain.then(dve.tensor_copy(pair[:, :, 0:C].bitcast(F32R), xn[:]))
                    chain.ready()
                    dve.tensor_tensor(pair[:, :, C:2 * C], xn[:], pair[:, :, 0:C],
                                      ALU.subtract).then_inc(pair_made, 1)
                    chain.leave(2, 0)

                def take_rows(c):
                    gated_wait(xT_ready, n0 + c + 2)
                    gated_wait(v_ready, n0 + c)
                    dve.tensor_copy(xT, pT).then_inc(xT_made, 1)

                def make_q(c):
                    gated_wait(base_made, n0 + c + 1)
                    gated_wait(qlo_made, n0 + c + 1)
                    dve.tensor_scalar(q, base, gb[:, 0:1], gb[:, 2:3], ALU.mult, ALU.add).then_inc(q_made, 1)

                def make_v(c):
                    gated_wait(v_ready, n0 + c + 1)
                    gated_wait(vs_made, n0 + c + 1)
                    dve.tensor_tensor(vb, pV.rearrange("p (t c) -> p t c", c=GH), bcast(bv[:], 1, CT),
                                      ALU.add).then_inc(vb_made, 1)

                def remainders(c):
                    gated_wait(qhi_made, n0 + c + 1)
                    own = bass.ds(c * CH, CH) if not isinstance(c, int) else slice(c * CH, (c + 1) * CH)
                    dve.tensor_tensor(qlo[:, own], q, qhi[:, own].bitcast(F32), ALU.subtract).then_inc(qlo_made, 1)
                    gated_wait(vhi_made, n0 + c + 1)
                    own = bass.ds(c * CT, CT) if not isinstance(c, int) else slice(c * CT, (c + 1) * CT)
                    dve.tensor_tensor(Vlo[:, own, :], vs, Vhi[:, own, :].bitcast(F32),
                                      ALU.subtract).then_inc(vlo_made, 1)

                split(0)
                take_rows(0)
                split(1)
                make_q(0)
                take_rows(1)
                make_v(0)
                with dve.Fori(1, LASTQ) as c:
                    split(c + 1)
                    remainders(c - 1)
                    make_q(c)
                    take_rows(c + 1)
                    make_v(c)
                remainders(LASTQ - 1)
                make_q(LASTQ)
                make_v(LASTQ)
                remainders(LASTQ)

                def remainder(qb, p, between=lambda: None):
                    g = (n0 + qb) * PAIRS + p
                    gated_wait(hi_made, g + 1)
                    for j in range(2):
                        half = attn[:, p % 2, j * CH:(j + 1) * CH]
                        dve.tensor_tensor(half, half, half, ALU.mult).then_inc(squared, 1)
                    between()
                    gated_wait(pairs_summed, g + (1 + SLOTS - 2))
                    for j in range(2):
                        own = slice(j * CH, (j + 1) * CH)
                        gated_wait(squared, 2 * g + (j + 1))
                        dve.tensor_tensor(attn_lo[:, p % 2, own], attn[:, p % 2, own],
                                          attn_hi[:, p % SLOTS, own].bitcast(F32), ALU.subtract).then_inc(lo_made, 1)

                def gate(qb):
                    gated_wait(pairs_summed, (n0 + qb) * PAIRS + (PAIRS + SLOTS))
                    own = bass.ds(qb * CH, CH) if not isinstance(qb, int) else slice(qb * CH, (qb + 1) * CH)
                    dve.scalar_tensor_tensor(out=gated[:], in0=pO[:], scalar=1.0 / GH, in1=uT[:, own],
                                             op0=ALU.mult, op1=ALU.mult).then_inc(gated_made, 1)

                def add_y(qb):
                    gated_wait(y_ready, n0 + qb + 1)
                    tiles = bass.ds(b * BT + qb * CT, CT)
                    dve.tensor_tensor(H[:, tiles, :], pY[:, 0:CT * C].rearrange("p (t c) -> p t c", c=C),
                                      H[:, tiles, :], ALU.add).then_inc(h_made, 1)

                def query_block(qb, last):
                    for p in range(2, PAIRS):
                        remainder(qb, p)
                    if last:
                        gate(qb)
                    else:
                        remainder(qb + 1, 0, lambda: gate(qb))
                        remainder(qb + 1, 1)
                    add_y(qb)

                gated_wait(bo_added, b + 1)
                remainder(0, 0)
                remainder(0, 1)
                with dve.Fori(0, LASTQ) as qb:
                    query_block(qb, False)
                query_block(LASTQ, True)


def normed_input(nc, XC, scale, next_weights):
    with ExitStack() as ctx:
        m = Scope(nc, ctx, "ln")
        shifted = m.sb("shifted", [P, TILES])
        root = m.sb("root", [P, TILES])
        inv = m.sb("inv", [P, TILES])
        ms = m.sb("ms", [P, TILES])
        shifted_made = m.sem("shifted_made")
        root_made = m.sem("root_made")
        dve_chain = m.sem("dve_chain")
        block = ctx.enter_context(nc.Block())

        @block.sync
        def _(sp):
            next_weights.load(sp)

        @block.scalar
        def _(act):
            for n in range(2):
                act.wait_ge(shifted_made, n + 1)
                act.activation(root[:], shifted[:], ACT.Sqrt).then_inc(root_made, 1)

        @block.vector
        def _(dve):
            chain = Chain(dve, dve_chain)
            dve.tensor_scalar(shifted[:], scale[:], LN_EPS, None, ALU.add).then_inc(shifted_made, 1)
            dve.wait_ge(root_made, 1)
            chain.then(dve.reciprocal(inv[:], root[:]))
            chain.ready()
            chain.then(dve.tensor_tensor(ms[:], scale[:], inv[:], ALU.mult))
            chain.ready()
            chain.then(dve.tensor_tensor(ms[:], ms[:], inv[:], ALU.mult))
            chain.ready()
            dve.tensor_scalar(shifted[:], ms[:], RMS_EPS, None, ALU.add).then_inc(shifted_made, 1)
            chain.then(dve.tensor_tensor(XC[:], XC[:], bcast(inv[:], 2, C), ALU.mult))
            dve.wait_ge(root_made, 2)
            chain.then(dve.reciprocal(scale[:], root[:]))
            chain.ready()


def stack(eng, chain, chained, src, out, res, parts, signal):
    def block_of(i):
        return out[:, :, :, i * HD:(i + 1) * HD]

    first = [parts.index(k) for k in range(3)]
    chain.then(eng.tensor_copy(block_of(first[0]), src))
    chained()
    chain.then(eng.tensor_tensor(res, src, block_of(first[0]), ALU.subtract))
    chained()
    chain.then(eng.tensor_copy(block_of(first[1]), res))
    chained()
    chain.then(eng.tensor_tensor(res, res, block_of(first[1]), ALU.subtract))
    chained()
    chain.then(eng.tensor_copy(block_of(first[2]), res))
    for i, k in enumerate(parts):
        if i not in first:
            chain.then(eng.tensor_copy(block_of(i), block_of(first[k])))
    chained()
    eng.sem_inc(signal, 1)


def causal_attention(nc, X2, inv_rms, ident, identb, masks, weights):
    LASTQ = CHUNKS - 1
    PER = 8
    FULL = CHUNKS * (CHUNKS + 1) // 2 * CT

    def before(qb):
        return 2 * qb * (qb + 1)

    with ExitStack() as ctx:
        m = Scope(nc, ctx, "ca")
        wraw, woraw, ln1, cos, sin = (weights[name] for name in ("wraw", "woraw", "ln1", "cos", "sin"))
        whi = m.sb("whi", [P, QKV], F32R)
        wlo = m.sb("wlo", [P, QKV], F32R)
        wohi = m.sb("wohi", [P, C], F32R)
        wolo = m.sb("wolo", [P, C], F32R)
        warm = m.sb("warm", [P, 1])
        hx = m.sb("hx", [P, CT, C])
        pair = m.sb("pair", [P, CT, 2 * C])
        xT = m.sb("xT", [P, CH], F32R)
        direct = m.sb("direct", [P, CT, NH + NKV, HD])
        turned = m.sb("turned", [P, CT, NH + NKV, HD])
        QK = m.sb("QK", [P, BT, ROPED])
        KS = m.sb("KS", [P, CT, NKV, STACK], BF16)
        QS = m.sb("QS", [P, 2, CT, NH, STACK], BF16)
        rest = m.sb("rest", [P, CT, NH, HD])
        square = m.sb("square", [P, (LASTQ - 1) * CT, C])
        first_rest = m.sb("first_rest", [P, CT, NH, HD])
        KT = m.sb("KT", [STACK + SHIFT, NKV, SEQ], BF16)
        QT = m.sb("QT", [STACK + SHIFT, 3, NH, CH], BF16)
        VA = m.sb("VA", [P, BT, NKV, VW])
        VS = m.sb("VS", [P, CT, NKV, VW])
        zeros = m.sb("zeros", [P, CH], BF16)
        probs = m.sb("probs", [P, 2, NH, CH])
        peaks = m.sb("peaks", [P, CT, NH, CHUNKS])
        peak = m.sb("peak", [P, CT, NH])
        left = m.sb("left", [P, CT, NH])
        shift = m.sb("shift", [P, CT, NH, SHIFT + 1], BF16)
        oT = m.sb("oT", [P, CH])
        inv = m.sb("inv", [P, CT, NH])
        y = m.sb("y", [P, CT, C])
        ypair = m.sb("ypair", [P, CT, 2 * C])
        yT = m.sb("yT", [P, CH], F32R)
        pS = m.ps("pS", [P, 2, 512])
        pM = m.ps("pM", [P, 4, 512])
        pO = m.ps("pO", [P, 512])
        pX = m.ps("pX", [P, 512])
        pK, pT, pQ = pM[:, 0, :].bitcast(BF16), pM[:, 2, :], pM[:, 3, :]

        split_done = m.sem("split_done")
        fills_done = m.sem("fills_done")
        zeros_made = m.sem("zeros_made")
        pair_made = m.sem("pair_made")
        xT_ready = m.sem("xT_ready")
        xT_made = m.sem("xT_made")
        qkv_ready = m.sem("qkv_ready")
        roped = m.sem("roped")
        v_made = m.sem("v_made")
        parts_made = m.sem("parts_made")
        rests_made = m.sem("rests_made")
        ks_made = m.sem("ks_made")
        kT_ready = m.sem("kT_ready")
        kT_made = m.sem("kT_made")
        qs_made = m.sem("qs_made")
        qT_ready = m.sem("qT_ready")
        qT_made = m.sem("qT_made")
        raw_ready = m.sem("raw_ready")
        raw_free = m.sem("raw_free")
        shift_made = m.sem("shift_made")
        shiftT_ready = m.sem("shiftT_ready")
        shiftT_made = m.sem("shiftT_made")
        vs_made = m.sem("vs_made")
        scores_ready = m.sem("scores_ready")
        probs_made = m.sem("probs_made")
        weighed = m.sem("weighed")
        o_copied = m.sem("o_copied")
        oT_ready = m.sem("oT_ready")
        y_made = m.sem("y_made")
        yT_ready = m.sem("yT_ready")
        yT_made = m.sem("yT_made")
        wo_ready = m.sem("wo_ready")
        x3_made = m.sem("x3_made")
        dve_chain = m.sem("dve_chain")
        pool_chain = m.sem("pool_chain")
        pe_gate, act_gate, dve_gate, pool_gate = (m.sem(f"{e}_gate") for e in ("pe", "act", "dve", "pool"))
        block = ctx.enter_context(nc.Block())

        @block.tensor
        def _(pe):
            def gated_wait(sem, value):
                pe.wait_ge(sem, value)
                pe.sem_inc(pe_gate, 1)

            pe.sem_inc(qT_ready, 4)
            pe.sem_inc(weighed, CT)
            pe.sem_inc(xT_ready, 1)
            pe.sem_inc(qkv_ready, 1)
            pe.wait_ge(weights.arrived, weights.count)
            pe.wait_ge(split_done, 1)
            with pe.Fori(0, BATCH) as b:
                s0 = b * FULL

                def turn_rows(n):
                    gated_wait(pair_made, n + 1)
                    gated_wait(xT_made, n + 1)
                    for t in range(CT):
                        last = pe.transpose(pT[:, t * P:(t + 1) * P], pair[:, t, :], ident[:])
                    last.then_inc(xT_ready, 1)

                def project(n):
                    gated_wait(xT_made, n + 2)
                    gated_wait(v_made, n + 1)
                    for t in range(CT):
                        for w in (whi, wlo):
                            last = pe.matmul(pQ[:, t * QKV:(t + 1) * QKV], xT[:, t * P:(t + 1) * P], w[:],
                                             start=w is whi, stop=w is wlo)
                    last.then_inc(qkv_ready, 1)

                def turn_keys(n):
                    gated_wait(ks_made, n + 1)
                    gated_wait(kT_made, n + 1)
                    for kv in range(NKV):
                        for t in range(CT):
                            col = (kv * CT + t) * P
                            last = pe.transpose(pK[0:STACK, col:col + P], KS[:, t, kv, :], identb[:])
                    last.then_inc(kT_ready, 1)

                n0 = b * CHUNKS
                turn_rows(n0)
                project(n0)
                turn_rows(n0 + 1)
                with pe.Fori(1, LASTQ) as c:
                    project(n0 + c)
                    turn_rows(n0 + c + 1)
                    turn_keys(n0 + c - 1)
                project(n0 + LASTQ)
                for c in (LASTQ - 1, LASTQ):
                    turn_keys(n0 + c)
                gated_wait(kT_made, (b + 1) * CHUNKS + 1)
                gated_wait(v_made, (b + 1) * CHUNKS + 1)
                pe.wait_ge(fills_done, 3)

                def turn_queries(qb, half):
                    n = b * CHUNKS + qb
                    gated_wait(qs_made, n + 1)
                    gated_wait(qT_made, 2 * n + half + 1)
                    bank = pX[:].bitcast(BF16)
                    for h in range(2):
                        for t in range(CT):
                            col = (h * CT + t) * P
                            last = pe.transpose(bank[0:STACK, col:col + P], QS[:, qb % 2, t, 2 * half + h, :],
                                                identb[:])
                    last.then_inc(qT_ready, 1)

                def turn_shift(qb, half):
                    n = b * CHUNKS + qb
                    gated_wait(shift_made, n + 1)
                    gated_wait(shiftT_made, 2 * n + half + 1)
                    bank = pX[:].bitcast(BF16)
                    for h in range(2):
                        for t in range(CT):
                            col = (h * CT + t) * P
                            last = pe.transpose(bank[STACK:STACK + SHIFT, col:col + P],
                                                shift[:, t, 2 * half + h, 0:SHIFT], identb[:])
                    last.then_inc(shiftT_ready, 1)

                def raw_scores(qb, order, c, t, diag=False):
                    unit = s0 + before(qb) + order
                    keys = (t + 1) * P if diag else CH
                    for k in range(2):
                        pe.wait_ge(raw_free, 2 * unit + (k + 1))
                        for h in (2 * k, 2 * k + 1):
                            rhs = KT[0:STACK, h // 2, c * CH:c * CH + keys] if isinstance(c, int) else \
                                KT[0:STACK, h // 2, bass.ds(c * CH, CH)]
                            last = pe.matmul(pM[:, h, 0:keys], QT[0:STACK, qb % 3, h, t * P:(t + 1) * P], rhs,
                                             start=True, stop=not diag)
                            if diag:
                                last = pe.matmul(pM[:, h, t * P:keys], identb[:], masks[:, 1, :],
                                                 start=False, stop=True)
                        last.then_inc(raw_ready, 1)

                def scores(qb, order, c, t, heads, diag=False):
                    step = s0 + before(qb) + order
                    q0 = t * P if diag else 0
                    for h in heads:
                        gated_wait(probs_made, 4 * step + (h - 1 if qb == LASTQ else h + 1))
                        out = pM[:, h, :] if qb == LASTQ else pS[:, h % 2, :]
                        lhsT = KT[:, h // 2, (4 * c + t) * P:(4 * c + t + 1) * P] if isinstance(c, int) else \
                            KT[:, h // 2, bass.ds(c * CH + t * P, P)]
                        last = pe.matmul(out[:, q0:CH], lhsT, QT[:, qb % 3, h, q0:CH], start=True, stop=not diag)
                        if diag:
                            last = pe.matmul(out[:, q0:q0 + P], identb[:], masks[:, 0, :], start=False, stop=True)
                        last.then_inc(scores_ready, 1)

                def weigh(qb, order, slot, q0=0):
                    step = s0 + before(qb) + order
                    pe.wait_ge(probs_made, 4 * step + 6)
                    for h in range(NH):
                        last = pe.matmul(pO[VW * h:VW * h + VW, q0:CH], VS[:, slot, h // 2, :],
                                         probs[:, slot % 2, h, q0:CH], start=False, stop=False,
                                         skip_group_check=True)
                    last.then_inc(weighed, 1)

                def turn_output(qb):
                    gated_wait(o_copied, b * CHUNKS + qb + 2)
                    for t in range(CT):
                        last = pe.transpose(pX[:, t * P:(t + 1) * P], oT[:, t * P:(t + 1) * P], ident[:])
                    last.then_inc(oT_ready, 1)

                def turn_y(qb):
                    gated_wait(y_made, b * CHUNKS + qb + 1)
                    for t in range(CT):
                        last = pe.transpose(pX[:, t * P:(t + 1) * P], ypair[:, t, :], ident[:])
                    last.then_inc(yT_ready, 1)

                def project_y(qb):
                    gated_wait(yT_made, b * CHUNKS + qb + 1)
                    for t in range(CT):
                        for w in (wohi, wolo):
                            last = pe.matmul(pX[:, t * C:(t + 1) * C], yT[:, t * P:(t + 1) * P], w[:],
                                             start=w is wohi, stop=w is wolo)
                    last.then_inc(wo_ready, 1)

                def early_maxima(qb):
                    return [(qb, t, qb - 1, t) for t in range(CT)] + \
                        [(qb, CT + t, qb, t, True) for t in range(CT)] if qb < CHUNKS else []

                def take_maxima(side, units):
                    for args in side[:units]:
                        raw_scores(*args)
                    del side[:units]

                def step(qb, order, c, t, between=None, diag=False):
                    q0 = t * P if diag else 0
                    before_q0 = (t - 1) * P if diag and t else 0
                    now, later = ((0, 1, 2, 3), ()) if qb == LASTQ else ((0, 1), (2, 3))
                    scores(qb, order, c, t, now, diag)
                    if between is None:
                        weigh(qb, order - 1, (t - 1) % CT, before_q0)
                    else:
                        between()
                    scores(qb, order, c, t, later, diag)

                n0 = b * CHUNKS
                for half in range(2):
                    turn_queries(0, half)
                gated_wait(qT_made, 2 * n0 + 3)
                for t in range(CT):
                    raw_scores(0, t, 0, t, diag=True)
                for half in range(2):
                    turn_queries(1, half)
                gated_wait(qT_made, 2 * n0 + 5)
                side = early_maxima(1)
                for half in range(2):
                    take_maxima(side, 1)
                    turn_shift(0, half)
                take_maxima(side, 5)
                gated_wait(shiftT_made, 2 * n0 + 3)
                for half in range(2):
                    turn_queries(2, half)
                take_maxima(side, 1)
                gated_wait(qT_made, 2 * n0 + 7)
                for qb in range(CHUNKS):
                    n = n0 + qb
                    if qb == LASTQ:
                        gated_wait(raw_free, 2 * (s0 + FULL) + 2)
                    gated_wait(o_copied, n + 1)
                    pe.matmul(pO[:], zeros[:, 0:P], zeros[:], start=True, stop=False, skip_group_check=True)

                    def key_chunk(c, opens=False):
                        for t in range(CT):
                            order = 4 * c + t

                            def more_maxima():
                                if qb < LASTQ:
                                    raw_scores(qb + 1, order + 2 * CT, c, t)

                            def between():
                                if qb + 2 < CHUNKS:
                                    turn_queries(qb + 2, 1)
                                more_maxima()

                            if opens and t == 0:
                                step(qb, order, c, t, between)
                            else:
                                step(qb, order, c, t)
                                more_maxima()

                    if qb:
                        key_chunk(0, opens=True)
                    if qb > 1:
                        with pe.Fori(1, qb) as c:
                            key_chunk(c)
                    side = early_maxima(qb + 2)
                    if qb and qb + 2 < CHUNKS:
                        gated_wait(qT_made, 2 * n + 7)
                    for t in range(CT):
                        step(qb, CT * qb + t, qb, t, (lambda: None) if qb == 0 and t == 0 else None, diag=True)
                        take_maxima(side, 1)
                        if t < 2 and qb < LASTQ:
                            if t == 0:
                                gated_wait(x3_made, n if qb else n + 1)
                            turn_shift(qb + 1, t)
                        if t == 2:
                            take_maxima(side, 1)
                            if qb < LASTQ:
                                gated_wait(shiftT_made, 2 * n + 5)
                            else:
                                gated_wait(x3_made, n)
                            if qb:
                                turn_output(qb - 1)
                    if qb:
                        turn_y(qb - 1)
                    weigh(qb, CT * (qb + 1) - 1, CT - 1, (CT - 1) * P)
                    take_maxima(side, 1)
                    if qb:
                        project_y(qb - 1)
                    take_maxima(side, 1)
                    if qb + 3 < CHUNKS:
                        gated_wait(x3_made, n + 1)
                        turn_queries(qb + 3, 0)
                    take_maxima(side, 1)
                gated_wait(x3_made, (b + 1) * CHUNKS)
                turn_output(LASTQ)
                turn_y(LASTQ)
                project_y(LASTQ)
                gated_wait(x3_made, (b + 1) * CHUNKS + 1)

        @block.scalar
        def _(act):
            def gated_wait(sem, value):
                act.wait_ge(sem, value)
                act.sem_inc(act_gate, 1)

            for credit, many in ((v_made, 1), (kT_made, 1), (qT_made, 1), (shiftT_made, 1), (probs_made, 2),
                                 (o_copied, 1)):
                act.sem_inc(credit, many)
            act.wait_ge(fills_done, 1)
            act.wait_ge(zeros_made, 1)
            with act.Fori(0, BATCH) as b:
                s0 = b * FULL
                act.activation(warm[:], zeros[:, 0:1], ACT.Exp)

                def take_values(c):
                    gated_wait(roped, b * CHUNKS + c + 1)
                    own = bass.ds(c * CT, CT) if not isinstance(c, int) else slice(c * CT, (c + 1) * CT)
                    act.activation(VA[:, own, :, 0:HD],
                                   pQ.rearrange("p (t n) -> p t n", n=QKV)[:, :, ROPED:QKV]
                                   .rearrange("p t (k e) -> p t k e", e=HD), ACT.Copy).then_inc(v_made, 1)

                def take_keys(c):
                    gated_wait(kT_ready, b * CHUNKS + c + 1)
                    own = bass.ds(c * CH, CH) if not isinstance(c, int) else slice(c * CH, (c + 1) * CH)
                    act.activation(KT[0:STACK, :, own],
                                   pK[0:STACK, :].rearrange("p (k n) -> p k n", n=CH),
                                   ACT.Copy).then_inc(kT_made, 1)

                def stack_keys(c):
                    own = bass.ds(c * CT, CT) if not isinstance(c, int) else slice(c * CT, (c + 1) * CT)
                    src = QK[:, own, NH * HD:ROPED].rearrange("p t (h e) -> p t h e", e=HD)
                    for k in range(3):
                        if k:
                            gated_wait(rests_made, 2 * (b * CHUNKS + c) + k)
                        for i in (i for i in range(len(K_PARTS)) if K_PARTS[i] == k):
                            last = act.activation(KS[:, :, :, i * HD:(i + 1) * HD],
                                                  rest[:, :, 0:NKV, :] if k else src, ACT.Copy)
                        last.then_inc(ks_made if k == 2 else parts_made, 1)

                take_values(0)
                stack_keys(0)
                with act.Fori(1, CHUNKS) as c:
                    take_values(c)
                    take_keys(c - 1)
                    stack_keys(c)
                take_keys(LASTQ)

                def take(ready, value, made, rows, qb, half):
                    gated_wait(ready, value)
                    act.activation(QT[rows, qb % 3, 2 * half:2 * half + 2, :].rearrange("p h n -> p (h n)"),
                                   pX[rows, :].bitcast(BF16), ACT.Copy).then_inc(made, 1)

                def take_queries(qb, half):
                    take(qT_ready, 2 * (b * CHUNKS + qb) + half + 5, qT_made, slice(0, STACK), qb, half)

                def take_shift(qb, half):
                    take(shiftT_ready, 2 * (b * CHUNKS + qb) + half + 1, shiftT_made,
                         slice(STACK, STACK + SHIFT), qb, half)

                def exps(qb, order, slot, q0=0):
                    step = s0 + before(qb) + order
                    gated_wait(weighed, step + (CT - 1))
                    for h in range(NH):
                        act.wait_ge(scores_ready, 4 * step + (h + 1))
                        if h == NH - 1:
                            gated_wait(vs_made, step + 1)
                        src = pM[:, h, :] if qb == LASTQ else pS[:, h % 2, :]
                        act.activation(probs[:, slot % 2, h, q0:CH], src[:, q0:CH], ACT.Exp,
                                       scale=float(HD) ** -0.5).then_inc(probs_made, 1)

                for take_part, qb in ((take_queries, 0), (take_queries, 1), (take_shift, 0), (take_queries, 2)):
                    for half in range(2):
                        take_part(qb, half)
                for qb in range(CHUNKS):
                    if qb:
                        with act.Fori(0, qb) as c:
                            for t in range(CT):
                                exps(qb, 4 * c + t, t)
                    for t in range(CT):
                        exps(qb, CT * qb + t, t, t * P)
                        if t < 2 and qb < LASTQ:
                            take_shift(qb + 1, t)
                    gated_wait(weighed, s0 + before(qb + 1) + CT)
                    gated_wait(oT_ready, b * CHUNKS + qb + 1)
                    act.activation(oT[:], pO[:], ACT.Copy).then_inc(o_copied, 1)
                    for half in range(2 if qb + 3 < CHUNKS else 0):
                        take_queries(qb + 3, half)

        @block.gpsimd
        def _(pool):
            chain = Chain(pool, pool_chain)

            def gated_wait(sem, value):
                pool.wait_ge(sem, value)
                pool.sem_inc(pool_gate, 1)

            def chained():
                chain.ready()
                if chain.base is not None:
                    pool.sem_inc(pool_gate, 1)

            pool.memset(VA[:], 0.0).then_inc(fills_done, 1)
            pool.wait_ge(fills_done, 1)
            pool.memset(VA[:, :, :, HD:HD + 1], 1.0).then_inc(fills_done, 1)
            pool.wait_ge(fills_done, 2)
            pool.memset(KT[STACK:STACK + SHIFT, :, :], 1.0).then_inc(fills_done, 1)
            pool.wait_ge(fills_done, 3)
            pool.sem_inc(oT_ready, 1)
            IMAGE = (CHUNKS - 2) * PER
            with pool.Fori(0, BATCH) as b:
                s0 = b * FULL
                def key_rests(c):
                    own = bass.ds(c * CT, CT)
                    src = QK[:, own, NH * HD:ROPED].rearrange("p t (h e) -> p t h e", e=HD)
                    res = rest[:, :, 0:NKV, :]
                    for k in range(2):
                        gated_wait(parts_made, 2 * (b * CHUNKS + c) + (k + 1))
                        if k:
                            gated_wait(rests_made, 2 * (b * CHUNKS + c) + 1)
                        i = K_PARTS.index(k)
                        pool.tensor_tensor(res, res if k else src, KS[:, :, :, i * HD:(i + 1) * HD],
                                           ALU.subtract).then_inc(rests_made, 1)

                with pool.Fori(0, CHUNKS) as c:
                    key_rests(c)
                def stack_queries(qb):
                    chain.enter(b * IMAGE + (qb - 2) * PER)
                    gated_wait(qT_ready, 2 * (b * CHUNKS + qb) + 2)
                    stack(pool, chain, chained, QK[:, qb * CT:(qb + 1) * CT, 0:NH * HD].rearrange("p t (h e) -> p t h e", e=HD),
                          QS[:, qb % 2, :, :, :], rest[:], Q_PARTS, qs_made)
                    chain.leave(PER, 0)

                def stage_values(qb, order, c, t, slot):
                    gated_wait(weighed, s0 + before(qb) + order + 1)
                    if isinstance(c, int):
                        pool.tensor_copy(VS[:, slot, :, :], VA[:, 4 * c + t, :, :]).then_inc(vs_made, 1)
                    else:
                        pool.tensor_copy(VS[:, slot:slot + 1, :, :],
                                         VA[:, bass.ds(c * CT + t, 1), :, :]).then_inc(vs_made, 1)

                stack_queries(2)
                for qb in range(CHUNKS):
                    if qb:
                        with pool.Fori(0, qb) as c:
                            for t in range(CT):
                                stage_values(qb, 4 * c + t, c, t, t)
                        if qb + 3 < CHUNKS:
                            stack_queries(qb + 3)
                    for t in range(CT):
                        stage_values(qb, CT * qb + t, qb, t, t)
                    if qb == 0:
                        stack_queries(3)

        @block.vector
        def _(dve):
            chain = Chain(dve, dve_chain)
            for credit, many in ((raw_free, 2), (x3_made, 1), (xT_made, 1)):
                dve.sem_inc(credit, many)
            dve.memset(zeros[:], 0.0).then_inc(zeros_made, 1)
            dve.wait_ge(weights.arrived, weights.count)
            chain.then(dve.tensor_scalar(wraw[:], wraw[:], ln1[:, 0:1], None, ALU.mult))
            chain.ready()
            split_weights(dve, chain, wraw[:], whi[:], wlo[:])
            split_weights(dve, chain, woraw[:], wohi[:], wolo[:])
            chain.ready()
            dve.sem_inc(split_done, 1)
            SPLITS = chain.n
            PREP = 6
            TAIL = 11

            def gated_wait(sem, value):
                dve.wait_ge(sem, value)
                dve.sem_inc(dve_gate, 1)

            def chained():
                chain.ready()
                dve.sem_inc(dve_gate, 1)

            with dve.Fori(0, BATCH) as b:
                s0 = b * FULL
                c0 = b * (CHUNKS * (PREP + TAIL) + 2 * PER + 4) + SPLITS
                def split(c):
                    own = b * BT + c * CT
                    tiles = bass.ds(own, CT)
                    chain.then(dve.tensor_tensor(hx[:], X2[:, tiles, :], bcast(inv_rms[:, tiles], 2, C), ALU.mult))
                    gated_wait(xT_ready, b * CHUNKS + c + 1)
                    chained()
                    chain.then(dve.tensor_copy(pair[:, :, 0:C].bitcast(F32R), hx[:]))
                    chained()
                    dve.tensor_tensor(pair[:, :, C:2 * C], hx[:], pair[:, :, 0:C],
                                      ALU.subtract).then_inc(pair_made, 1)

                def take_rows(c):
                    gated_wait(xT_ready, b * CHUNKS + c + 2)
                    gated_wait(qkv_ready, b * CHUNKS + c + 1)
                    dve.tensor_copy(xT[:], pT).then_inc(xT_made, 1)

                def rope(c):
                    own = bass.ds(c * CT, CT) if not isinstance(c, int) else slice(c * CT, (c + 1) * CT)
                    gated_wait(qkv_ready, b * CHUNKS + c + 2)
                    qk = pQ.rearrange("p (t n) -> p t n", n=QKV)[:, :, 0:ROPED].rearrange(
                        "p t (h e) -> p t h e", e=HD)
                    chain.then(dve.tensor_tensor(direct[:], qk, bcast(cos[:, own, :], 2, NH + NKV), ALU.mult))
                    half = HD // 2
                    for lo, hi in ((0, half), (half, 0)):
                        chain.then(dve.tensor_tensor(turned[:, :, :, lo:lo + half], qk[:, :, :, hi:hi + half],
                                                     bcast(sin[:, own, lo:lo + half], 2, NH + NKV), ALU.mult))
                    chained()
                    chain.then(dve.tensor_tensor(QK[:, own, :].rearrange("p t (h e) -> p t h e", e=HD),
                                                 direct[:], turned[:], ALU.add))
                    chained()
                    dve.sem_inc(roped, 1)

                chain.enter(c0)
                split(0)
                take_rows(0)
                split(1)
                chain.leave(4, 0)
                with dve.Fori(0, CHUNKS - 2) as c:
                    chain.enter(c0 + 4 + c * PREP)
                    rope(c)
                    take_rows(c + 1)
                    split(c + 2)
                    chain.leave(PREP, 0)
                chain.enter(c0 + 4 + (CHUNKS - 2) * PREP)
                rope(LASTQ - 1)
                take_rows(LASTQ)
                rope(LASTQ)
                chain.leave(8, 0)

                def maxima(qb, order, c, t, diag=False):
                    unit = s0 + before(qb) + order
                    keys = (t + 1) * P if diag else CH
                    at = slice(c, c + 1) if isinstance(c, int) else bass.ds(c, 1)
                    for k in range(2):
                        gated_wait(raw_ready, 2 * unit + (k + 1))
                        dve.tensor_reduce(peaks[:, t, 2 * k:2 * k + 2, at].rearrange("p h c -> p (h c)"),
                                          pM[:, 2 * k:2 * k + 2, 0:keys], AX.X, ALU.max).then_inc(raw_free, 1)

                def make_shift(qb):
                    gated_wait(raw_free, 2 * (s0 + before(qb + 1)) + 2)
                    chain.then(dve.tensor_reduce(peak[:], peaks[:, :, :, 0:qb + 1], AX.X, ALU.max, negate=True))
                    chained()
                    chain.then(dve.tensor_copy(shift[:, :, :, 0], peak[:]))
                    chained()
                    chain.then(dve.tensor_tensor(left[:], peak[:], shift[:, :, :, 0], ALU.subtract))
                    chained()
                    chain.then(dve.tensor_copy(shift[:, :, :, 1], left[:]))
                    chained()
                    chain.then(dve.tensor_tensor(left[:], left[:], shift[:, :, :, 1], ALU.subtract))
                    chained()
                    chain.then(dve.tensor_copy(shift[:, :, :, 2], left[:]))
                    chained()
                    dve.sem_inc(shift_made, 1)

                def normalise(qb):
                    gated_wait(oT_ready, b * CHUNKS + qb + 2)
                    o = pX[:].rearrange("p (t h e) -> p t h e", h=NH, e=VW)
                    chain.then(dve.reciprocal(inv[:], o[:, :, :, HD]))
                    chained()
                    chain.then(dve.tensor_tensor(y[:].rearrange("p t (h e) -> p t h e", e=HD), o[:, :, :, 0:HD],
                                                 bcast(inv[:], 3, HD), ALU.mult))
                    chained()
                    chain.then(dve.tensor_copy(ypair[:, :, 0:C].bitcast(F32R), y[:]))
                    chained()
                    chain.then(dve.tensor_tensor(ypair[:, :, C:2 * C], y[:], ypair[:, :, 0:C], ALU.subtract))
                    chained()
                    dve.sem_inc(y_made, 1)

                def take_y(qb):
                    gated_wait(yT_ready, b * CHUNKS + qb + 1)
                    dve.tensor_copy(yT[:], pX[:]).then_inc(yT_made, 1)

                def add_y(qb):
                    gated_wait(wo_ready, b * CHUNKS + qb + 1)
                    tiles = bass.ds(b * BT + qb * CT, CT)
                    chain.then(dve.tensor_tensor(X2[:, tiles, :], pX[:, 0:CT * C].rearrange("p (t c) -> p t c", c=C),
                                                 X2[:, tiles, :], ALU.add))
                    chained()
                    dve.sem_inc(x3_made, 1)

                def square_sums(first, end):
                    tiles = bass.ds(b * BT + first * CT, (end - first) * CT)
                    chain.then(dve.tensor_tensor(square[:, 0:(end - first) * CT, :], X2[:, tiles, :], X2[:, tiles, :],
                                                 ALU.mult))
                    chained()
                    chain.then(dve.tensor_reduce(inv_rms[:, tiles], square[:, 0:(end - first) * CT, :], AX.X, ALU.add))
                    chained()

                chain.enter(c0 + CHUNKS * PREP)
                for qb in range(2):
                    gated_wait(qT_ready, 2 * (b * CHUNKS + qb) + 2)
                    stack(dve, chain, chained, QK[:, qb * CT:(qb + 1) * CT, 0:NH * HD].rearrange(
                        "p t (h e) -> p t h e", e=HD), QS[:, qb, :, :, :], first_rest[:], Q_PARTS, qs_made)
                def early_maxima(qb):
                    return [(qb, t, qb - 1, t) for t in range(CT)] + \
                        [(qb, CT + t, qb, t, True) for t in range(CT)] if qb < CHUNKS else []

                def take_maxima(side, units):
                    for args in side[:units]:
                        maxima(*args)
                    del side[:units]

                for t in range(CT):
                    maxima(0, t, 0, t, diag=True)
                make_shift(0)
                take_maxima(early_maxima(1), 2 * CT)
                for qb in range(CHUNKS):
                    if qb and qb < LASTQ:
                        with dve.Fori(0, qb) as c:
                            for t in range(CT):
                                maxima(qb + 1, 4 * c + (2 * CT + t), c, t)
                    if qb < LASTQ:
                        make_shift(qb + 1)
                    else:
                        square_sums(0, LASTQ - 1)
                    side = early_maxima(qb + 2)
                    take_maxima(side, 4)
                    if qb:
                        normalise(qb - 1)
                    take_maxima(side, 1)
                    if qb:
                        take_y(qb - 1)
                    take_maxima(side, 1)
                    if qb:
                        add_y(qb - 1)
                    take_maxima(side, 2)
                normalise(LASTQ)
                take_y(LASTQ)
                add_y(LASTQ)
                square_sums(LASTQ - 1, CHUNKS)
                chain.leave(CHUNKS * TAIL + 2 * PER + 4, 0)


def routing(nc, d, X3, squares, ident, fT, weight, expert_weights):
    w1hi, w1lo, w3hi, w3lo, w2 = expert_weights
    with ExitStack() as ctx:
        m = Scope(nc, ctx, "ro")
        ms = m.sb("ms", [P, TILES])
        root = m.sb("root", [P, TILES])
        inv = m.sb("inv", [P, TILES])
        rraw = m.sb("rraw", [P, NE])
        rhi = m.sb("rhi", [P, NE], F32R)
        rlo = m.sb("rlo", [P, NE], F32R)
        raw1 = m.sb("raw1", [P, HIDDEN])
        raw3 = m.sb("raw3", [P, HIDDEN])
        ln2 = m.sb("ln2", [P, 1])
        flat = m.sb("flat", [P, CT, C])
        pair = m.sb("pair", [P, 2, CT, 2 * C])
        xT = m.sb("xT", [P, 2, CH], F32R)
        logits = m.sb("logits", [P, TILES, NE])
        top = m.sb("top", [P, TILES])
        prob = m.sb("prob", [P, TILES, NE])
        total = m.sb("total", [P, TILES])
        no_less = m.sb("no_less", [P, NE - 1, TILES, NE])
        ahead = m.sb("ahead", [P, TILES, NE])
        behind = m.sb("behind", [P, TILES, NE])
        limit = m.sb("limit", [P, NE])
        rank = m.sb("rank", [P, TILES, NE])
        pT = m.ps("pT", [P, 2, 512])
        pL = m.ps("pL", [P, 2, 512])

        weights_in = m.sem("weights_in")
        ms_made = m.sem("ms_made")
        root_made = m.sem("root_made")
        split_done = m.sem("split_done")
        pair_made = m.sem("pair_made")
        xT_ready = m.sem("xT_ready")
        xT_made = m.sem("xT_made")
        fT_made = m.sem("fT_made")
        expert_weights_in = m.sem("expert_weights_in")
        pool_chain = m.sem("pool_chain")
        logits_ready = m.sem("logits_ready")
        logits_made = m.sem("logits_made")
        margin_made = m.sem("margin_made")
        exp_made = m.sem("exp_made")
        dve_chain = m.sem("dve_chain")
        pe_gate, act_gate, dve_gate = (m.sem(f"{e}_gate") for e in ("pe", "act", "dve"))
        block = ctx.enter_context(nc.Block())
        N = BATCH * CHUNKS

        @block.sync
        def _(sp):
            for half in (0, C):
                sp.dma_start(rraw[half:half + C, :], d["router"]).then_inc(weights_in, 16)
                sp.dma_start(ln2[half:half + C, :], d["ln2_w"]).then_inc(weights_in, 16)
            sp.dma_start(limit[:], d["limit"]).then_inc(weights_in, 16)
            for half in (0, C):
                sp.dma_start(raw1[half:half + C, :], d["w1"]).then_inc(expert_weights_in, 16)
                sp.dma_start(raw3[half:half + C, :], d["w3"]).then_inc(expert_weights_in, 16)
            sp.dma_start(w2[:], d["w2"]).then_inc(expert_weights_in, 16)

        @block.scalar
        def _(act):
            act.sem_inc(fT_made, 2)
            act.wait_ge(ms_made, 1)
            act.activation(root[:], ms[:], ACT.Sqrt).then_inc(root_made, 1)
            with act.Fori(0, N // 2) as i:
                for n in (At(0, i), At(1, i)):
                    act.wait_ge(xT_made, n.of(1) + 3)
                    act.sem_inc(act_gate, 1)
                    act.activation(fT[:, n.span(CH)], xT[:, n.odd, :].bitcast(F32), ACT.Copy).then_inc(fT_made, 1)
            act.wait_ge(margin_made, 1)
            act.activation(prob[:], prob[:], ACT.Exp).then_inc(exp_made, 1)

        @block.tensor
        def _(pe):
            def gated_wait(sem, value):
                pe.wait_ge(sem, value)
                pe.sem_inc(pe_gate, 1)

            pe.wait_ge(split_done, 1)

            def turn(n):
                gated_wait(pair_made, n.of(1) + 2)
                gated_wait(xT_made, n.of(1) + 1)
                for t in range(CT):
                    last = pe.transpose(pT[:, n.odd, t * P:(t + 1) * P], pair[:, n.odd, t, :], ident[:])
                last.then_inc(xT_ready, 1)

            def route(n):
                gated_wait(xT_made, n.of(1) + 3)
                gated_wait(logits_made, n.of(1) + 1)
                for t in range(CT):
                    for w in (rhi, rlo):
                        last = pe.matmul(pL[:, n.odd, t * NE:(t + 1) * NE], xT[:, n.odd, t * P:(t + 1) * P], w[:],
                                         start=w is rhi, stop=w is rlo)
                last.then_inc(logits_ready, 1)

            turn(At(0))
            turn(At(1))
            with pe.Fori(0, N // 2 - 1) as i:
                for n in (At(0, i), At(1, i)):
                    route(n)
                    turn(n.plus(2))
            route(At(N - 2))
            route(At(N - 1))

        @block.gpsimd
        def _(pool):
            chain = Chain(pool, pool_chain)
            pool.wait_ge(expert_weights_in, 80)
            for raw, hi, lo in ((raw1, w1hi, w1lo), (raw3, w3hi, w3lo)):
                chain.then(pool.tensor_scalar(raw[:], raw[:], ln2[:, 0:1], None, ALU.mult))
                chain.ready()
                split_weights(pool, chain, raw[:], hi[:], lo[:])
            chain.ready()

        @block.vector
        def _(dve):
            chain = Chain(dve, dve_chain)

            def gated_wait(sem, value):
                dve.wait_ge(sem, value)
                dve.sem_inc(dve_gate, 1)

            for credit in (logits_made, logits_ready, xT_made, xT_ready):
                dve.sem_inc(credit, 2)
            dve.sem_inc(pair_made, 1)
            dve.tensor_scalar(ms[:], squares[:], 1.0 / C, RMS_EPS, ALU.mult, ALU.add).then_inc(ms_made, 1)
            dve.wait_ge(weights_in, 80)
            chain.then(dve.tensor_scalar(rraw[:], rraw[:], ln2[:, 0:1], None, ALU.mult))
            chain.ready()
            split_weights(dve, chain, rraw[:], rhi[:], rlo[:])
            chain.ready()
            dve.sem_inc(split_done, 1)
            dve.wait_ge(root_made, 1)
            chain.then(dve.reciprocal(inv[:], root[:]))
            chain.ready()
            before = chain.n

            def split(n):
                chain.enter(n.of(2) + before)
                gated_wait(pair_made, n.of(1) + 1)
                chain.then(dve.tensor_tensor(flat[:], X3[:, n.span(CT), :], bcast(inv[:, n.span(CT)], 2, C), ALU.mult))
                gated_wait(xT_ready, n.of(1) + 1)
                chain.ready()
                dve.sem_inc(dve_gate, 1)
                hi = pair[:, n.odd, :, 0:C]
                chain.then(dve.tensor_copy(hi.bitcast(F32R), flat[:]))
                chain.ready()
                dve.tensor_tensor(pair[:, n.odd, :, C:2 * C], flat[:], hi, ALU.subtract).then_inc(pair_made, 1)
                chain.leave(2, 0)

            def take_rows(n):
                gated_wait(xT_ready, n.of(1) + 3)
                gated_wait(logits_ready, n.of(1) + 1)
                gated_wait(fT_made, n.of(1) + 1)
                dve.tensor_copy(xT[:, n.odd, :], pT[:, n.odd, :]).then_inc(xT_made, 1)

            def take_logits(n):
                gated_wait(logits_ready, n.of(1) + 3)
                dve.tensor_copy(logits[:, n.span(CT), :],
                                pL[:, n.odd, 0:CT * NE].rearrange("p (t e) -> p t e", e=NE)).then_inc(logits_made, 1)

            split(At(0))
            split(At(1))
            take_rows(At(0))
            split(At(2))
            take_rows(At(1))
            split(At(3))
            take_logits(At(0))
            with dve.Fori(0, N // 2 - 2) as i:
                for n in (At(2, i), At(3, i)):
                    take_rows(n)
                    split(n.plus(2))
                    take_logits(n.plus(-1))
            for n in (At(N - 2), At(N - 1)):
                take_rows(n)
                take_logits(n.plus(-1))
            take_logits(At(N - 1))
            chain.n = before + 2 * N
            dve.wait_ge(logits_made, N + 2)
            chain.then(dve.tensor_reduce(top[:], logits[:], AX.X, ALU.max))
            chain.ready()
            dve.tensor_tensor(prob[:], logits[:], bcast(top[:], 2, NE), ALU.subtract).then_inc(margin_made, 1)
            dve.wait_ge(exp_made, 1)
            chain.then(dve.tensor_reduce(total[:], prob[:], AX.X, ALU.add))
            chain.ready()
            chain.then(dve.reciprocal(total[:], total[:]))
            chain.ready()
            chain.then(dve.tensor_tensor(prob[:], prob[:], bcast(total[:], 2, NE), ALU.mult))
            chain.ready()
            for gap in range(1, NE):
                chain.then(dve.tensor_tensor(no_less[:, gap - 1, :, 0:NE - gap], prob[:, :, 0:NE - gap],
                                             prob[:, :, gap:NE], ALU.is_ge))
            chain.ready()
            for count in (ahead, behind):
                chain.then(dve.memset(count[:], 0.0))
            chain.ready()
            chain.then(dve.tensor_copy(ahead[:, :, 1:NE], no_less[:, 0, :, 0:NE - 1]))
            chain.then(dve.tensor_copy(behind[:, :, 0:NE - 1], no_less[:, 0, :, 0:NE - 1]))
            for gap in range(2, NE):
                chain.ready()
                for count, part in ((ahead, slice(gap, NE)), (behind, slice(0, NE - gap))):
                    chain.then(dve.tensor_tensor(count[:, :, part], count[:, :, part],
                                                 no_less[:, gap - 1, :, 0:NE - gap], ALU.add))
            chain.ready()
            chain.then(dve.tensor_tensor(rank[:], ahead[:], behind[:], ALU.subtract))
            chain.ready()
            chain.then(dve.tensor_tensor(rank[:], rank[:], bcast(limit[:], 1, TILES), ALU.is_lt))
            chain.ready()
            chain.then(dve.tensor_tensor(prob[:], prob[:], rank[:], ALU.mult))
            chain.ready()
            chain.then(dve.tensor_reduce(total[:], prob[:], AX.X, ALU.add))
            chain.ready()
            chain.then(dve.tensor_scalar(total[:], total[:], 1e-9, None, ALU.add))
            chain.ready()
            chain.then(dve.reciprocal(total[:], total[:]))
            chain.ready()
            chain.then(dve.tensor_tensor(weight[:], prob[:], bcast(total[:], 2, NE), ALU.mult))
            chain.ready()


def hidden_blocks():
    out = []
    for m in range(HM):
        rows = min(P, HIDDEN - m * P)
        out.append((rows, m * P // EHID, (m * P + rows - 1) // EHID + 1))
    return out


def experts(nc, d, H, X3, fT, weight, weights, out):
    EARLY = 2
    FIRST = 5
    blocks = hidden_blocks()
    starts = np.cumsum([0] + [(e1 - e0) * C for _, e0, e1 in blocks])
    with ExitStack() as ctx:
        m = Scope(nc, ctx, "ex")
        w1hi, w1lo, w3hi, w3lo, w2 = weights
        act1 = m.sb("act1", [P, 2, CH])
        hidden = m.sb("hidden", [P, HM, CH])
        by_expert = m.sb("by_expert", [P, CT, NE * C])
        scaled = m.sb("scaled", [P, 2, NE, C])
        mixed = m.sb("mixed", [P, CT, C])
        pA = m.ps("pA", [P, 2, 512])
        pB = m.ps("pB", [P, 2, 512])
        pY = m.ps("pY", [P, CT, 512])

        x3_added = m.sem("x3_added")
        a_ready = m.sem("a_ready")
        b_ready = m.sem("b_ready")
        act1_made = m.sem("act1_made")
        hidden_made = m.sem("hidden_made")
        hidden_used = m.sem("hidden_used")
        y_ready = m.sem("y_ready")
        y_copied = m.sem("y_copied")
        y_scaled = m.sem("y_scaled")
        mixed_made = m.sem("mixed_made")
        out_made = m.sem("out_made")
        stored = m.sem("stored")
        pe_gate, act_gate, dve_gate, sp_gate = (m.sem(f"{e}_gate") for e in ("pe", "act", "dve", "sp"))
        block = ctx.enter_context(nc.Block())
        N = BATCH * CHUNKS

        @block.sync
        def _(sp):
            rows = out.rearrange("b (t p) c -> p (b t) c", p=P)
            with sp.Fori(0, N) as n:
                sp.wait_ge(out_made, n + 1)
                sp.sem_inc(sp_gate, 1)
                sp.dma_start(rows[:, bass.ds(n * CT, CT), :], H[:, bass.ds(n * CT, CT), :]).then_inc(stored, 16)
            sp.wait_ge(stored, 16 * N)

        @block.gpsimd
        def _(pool):
            pool.tensor_tensor(H[:], H[:], X3[:], ALU.add).then_inc(x3_added, 1)

        @block.tensor
        def _(pe):
            def gated_wait(sem, value):
                pe.wait_ge(sem, value)
                pe.sem_inc(pe_gate, 1)

            def project(n, k):
                rows = blocks[k][0]
                cols = slice(k * P, k * P + rows)
                rhs = fT[:, n.span(CH)]
                gated_wait(act1_made, n.of(HM) + (k + 1))
                for w in (w1hi, w1lo):
                    last = pe.matmul(pA[0:rows, (k + n.odd) % 2, :], w[:, cols], rhs, start=w is w1hi, stop=w is w1lo)
                last.then_inc(a_ready, 1)
                gated_wait(hidden_made, n.of(HM) + (k + 1))
                for w in (w3hi, w3lo):
                    last = pe.matmul(pB[0:rows, (k + n.odd) % 2, :], w[:, cols], rhs, start=w is w3hi, stop=w is w3lo)
                last.then_inc(b_ready, 1)

            def reduce(n, k):
                rows, e0, e1 = blocks[k]
                gated_wait(hidden_made, n.of(HM) + (k + 3))
                for t in range(CT):
                    if k == 0:
                        gated_wait(y_copied, n.of(CT) + (t + 1))
                    last = pe.matmul(pY[:, t, e0 * C:e1 * C], hidden[0:rows, k, t * P:(t + 1) * P],
                                     w2[0:rows, int(starts[k]):int(starts[k + 1])], start=k == 0,
                                     stop=k == HM - 1, skip_group_check=True)
                    if k == HM - 1:
                        last.then_inc(y_ready, 1)
                if k < HM - 1:
                    last.then_inc(hidden_used, 1)

            def chunk(n, last):
                for k in range(EARLY, HM):
                    project(n, k)
                    if k >= FIRST - 1:
                        reduce(n, k - (FIRST - 1))
                left = list(range(HM - FIRST + 1, HM))
                for k in left:
                    if not last and k >= HM - EARLY:
                        project(n.plus(1), k - (HM - EARLY))
                    reduce(n, k)

            for k in range(EARLY):
                project(At(0), k)
            with pe.Fori(0, N // 2 - 1) as i:
                chunk(At(0, i), False)
                chunk(At(1, i), False)
            chunk(At(N - 2), False)
            chunk(At(N - 1), True)

        @block.scalar
        def _(act):
            def gated_wait(sem, value):
                act.wait_ge(sem, value)
                act.sem_inc(act_gate, 1)

            act.sem_inc(act1_made, 2)
            act.sem_inc(y_copied, CT)

            def silu(n, k):
                rows = blocks[k][0]
                gated_wait(a_ready, n.of(HM) + (k + 1))
                gated_wait(hidden_made, n.of(HM) + (k + 1))
                act.activation(act1[0:rows, (k + n.odd) % 2, :], pA[0:rows, (k + n.odd) % 2, :], ACT.Silu).then_inc(act1_made, 1)

            def take_y(n, t):
                gated_wait(y_ready, n.of(CT) + (t + 1))
                gated_wait(y_scaled, n.of(CT) + (t + 1))
                act.activation(by_expert[:, t, :], pY[:, t, :], ACT.Copy).then_inc(y_copied, 1)

            def chunk(n):
                for k in range(EARLY):
                    silu(n, k)
                for t in range(CT):
                    take_y(n.plus(-1), t)
                    if t % 2:
                        silu(n, EARLY + t // 2)
                for k in range(EARLY + CT // 2, HM):
                    silu(n, k)

            for k in range(HM):
                silu(At(0), k)
            with act.Fori(0, N // 2 - 1) as i:
                chunk(At(1, i))
                chunk(At(2, i))
            chunk(At(N - 1))
            for t in range(CT):
                take_y(At(N - 1), t)

        @block.vector
        def _(dve):
            def gated_wait(sem, value):
                dve.wait_ge(sem, value)
                dve.sem_inc(dve_gate, 1)

            dve.sem_inc(hidden_made, 2)
            dve.sem_inc(y_scaled, CT)
            dve.sem_inc(hidden_used, HM - 1)
            dve.wait_ge(x3_added, 1)

            def multiply(n, k):
                rows = blocks[k][0]
                gated_wait(b_ready, n.of(HM) + (k + 1))
                gated_wait(act1_made, n.of(HM) + (k + 3))
                if k < HM - 1:
                    gated_wait(hidden_used, n.of((HM - 1)) + (k + 1))
                else:
                    gated_wait(y_copied, n.of(CT) + CT)
                dve.tensor_tensor(hidden[0:rows, k, :], pB[0:rows, (k + n.odd) % 2, :], act1[0:rows, (k + n.odd) % 2, :],
                                  ALU.mult).then_inc(hidden_made, 1)

            def scale(n, t):
                gated_wait(y_copied, n.of(CT) + (t + 1 + CT))
                gated_wait(mixed_made, n.of(CT) + (t + 1))
                dve.tensor_tensor(scaled[:, t % 2, :, :], by_expert[:, t, :].rearrange("p (e c) -> p e c", c=C),
                                  bcast(weight[:, n.span(CT, t, 1), :].rearrange("p a e -> p (a e)"), 2, C),
                                  ALU.mult).then_inc(y_scaled, 1)

            def mix(n, t):
                gated_wait(y_scaled, n.of(CT) + (t + 1 + CT))
                dve.tensor_reduce(mixed[:, t, :], scaled[:, t % 2, :, :].rearrange("p e c -> p c e"),
                                  AX.X, ALU.add).then_inc(mixed_made, 1)

            def finish(n):
                gated_wait(mixed_made, n.of(CT) + (CT + 2))
                tiles = n.span(CT)
                dve.tensor_tensor(H[:, tiles, :], H[:, tiles, :], mixed[:], ALU.add).then_inc(out_made, 1)

            dve.sem_inc(mixed_made, 2)
            def chunk(n):
                for k in range(HM):
                    multiply(n, k)
                    t = k - EARLY - 1
                    if 0 <= t < CT:
                        scale(n.plus(-1), t)
                    if 0 < t <= CT:
                        mix(n.plus(-1), t - 1)
                    if t == CT + 1:
                        finish(n.plus(-1))

            for k in range(HM):
                multiply(At(0), k)
            with dve.Fori(0, N // 2 - 1) as i:
                chunk(At(1, i))
                chunk(At(2, i))
            chunk(At(N - 1))
            for t in range(CT + 1):
                if t < CT:
                    scale(At(N - 1), t)
                if t:
                    mix(At(N - 1), t - 1)
            finish(At(N - 1))


_OUT = ("out", (BATCH, SEQ, C))


def program(nc, d, out):
    with ExitStack() as ctx:
        m = Scope(nc, ctx, "all")
        H = m.sb("H", [P, TILES, C])
        XC = m.sb("XC", [P, TILES, C])
        scale = m.sb("scale", [P, TILES])
        ident = m.sb("ident", [P, P])
        identb = m.sb("identb", [P, P], BF16)
        rawmasks = m.sb("rawmasks", [P, 2, P])
        masks = m.sb("masks", [P, 2, P], BF16)
        consts_in = m.sem("consts_in")
        with nc.Block() as block:
            @block.sync
            def _(sp):
                sp.dma_start(ident[:], d["ident"]).then_inc(consts_in, 16)
                sp.dma_start(rawmasks[:], d["masks"]).then_inc(consts_in, 16)

            @block.vector
            def _(dve):
                dve.wait_ge(consts_in, 32)
                dve.tensor_copy(identb[:], ident[:])
                dve.tensor_copy(masks[:], rawmasks[:])
        with ExitStack() as early:
            weights = gated_weights(nc, early, d)
            token_embedding(nc, d, H, XC, scale, ident, weights)
            gated_attention(nc, H, XC, scale, ident, weights)
        with ExitStack() as middle:
            weights = causal_weights(nc, middle, d)
            normed_input(nc, XC, scale, weights)
            causal_attention(nc, XC, scale, ident, identb, masks, weights)
        with ExitStack() as late:
            r = Scope(nc, late, "moe")
            fT = r.sb("fT", [P, BATCH * SEQ], F32R)
            weight = r.sb("weight", [P, TILES, NE])
            split = [r.sb(name, [P, HIDDEN], F32R) for name in ("w1hi", "w1lo", "w3hi", "w3lo")]
            w2 = r.sb("w2", [P, sum(e1 - e0 for _, e0, e1 in hidden_blocks()) * C])
            weights = (*split, w2)
            routing(nc, d, XC, scale, ident, fT, weight, weights)
            experts(nc, d, H, XC, fT, weight, weights, out)


def down_blocks(w2):
    rows = np.ascontiguousarray(w2.transpose(0, 2, 1)).reshape(HIDDEN, C)
    parts = []
    for k, (n, e0, e1) in enumerate(hidden_blocks()):
        for e in range(e0, e1):
            block = np.zeros((P, C), np.float32)
            a, b = max(k * P, e * EHID), min(k * P + n, (e + 1) * EHID)
            block[a - k * P:b - k * P] = rows[a:b]
            parts.append(block)
    return np.ascontiguousarray(np.concatenate(parts, axis=1))


def shape_constants():
    freq = 1.0 / 10000.0 ** (np.arange(0, HD, 2, dtype=np.float32) / HD)
    angle = np.outer(np.arange(SEQ, dtype=np.float32), freq)
    angle = np.concatenate([angle, angle], axis=-1)
    cos, sin = np.cos(angle).astype(np.float32), np.sin(angle).astype(np.float32)
    sin[:, :HD // 2] *= -1
    row, col = np.arange(P)[:, None], np.arange(P)[None, :]
    masks = np.stack([np.where(row > col, np.float32(-1e30), np.float32(0)),
                      np.where(col > row, np.float32(-1e30), np.float32(0))], axis=1)
    tiled = [np.ascontiguousarray(t.reshape(BT, P, HD).transpose(1, 0, 2)) for t in (cos, sin)]
    limit = (np.arange(NE) + (TOPK - 0.5 - (NE - 1))).astype(np.float32)
    return {"limit": np.ascontiguousarray(np.broadcast_to(limit, (P, NE))), "cos": tiled[0], "sin": tiled[1],
            "masks": np.ascontiguousarray(masks.astype(np.float32))}


def kernel(x, L0_tok_bases, L0_tok_W_spline, L0_tok_b_spline, L0_tok_W_base, L0_tok_b_base, L0_attn_g,
           L0_attn_W_uv, L0_attn_b_uv, L0_attn_gamma, L0_attn_beta, L0_attn_W_o, L0_attn_b_o, L0_ffn_ln1_w,
           L0_ffn_ln2_w, L0_ffn_wq, L0_ffn_wk, L0_ffn_wv, L0_ffn_wo, L0_ffn_router_w, L0_ffn_w1, L0_ffn_w2,
           L0_ffn_w3):
    import concourse.bacc as bacc
    from concourse.bass_utils import run_bass_kernel_spmd as run

    asc = np.ascontiguousarray
    bases, ws = np.asarray(L0_tok_bases), np.asarray(L0_tok_W_spline).reshape(C, C, 3)
    one = np.ones((C, 1), np.float32)
    wb = np.asarray(L0_tok_W_base)
    arrays = {
        "x": asc(np.asarray(x).reshape(BATCH, C, SEQ)),
        "wtok": asc(np.stack([np.concatenate([wb.T, ws[:, :, 0].T]),
                              np.concatenate([ws[:, :, 1].T, ws[:, :, 2].T])], axis=1)),
        "tok_factor": asc(np.concatenate([np.concatenate([one, bases[:, 0:1]]),
                                          np.concatenate([bases[:, 1:2], bases[:, 2:3]])], axis=1)),
        "b_base": asc(L0_tok_b_base), "b_spline": asc(L0_tok_b_spline),
        "g": asc(np.asarray(L0_attn_g).reshape(1)),
        "W_uv": asc(L0_attn_W_uv), "b_uv": asc(L0_attn_b_uv),
        "ga_cols": asc(np.concatenate([np.asarray(L0_attn_b_uv).reshape(3, GH), np.asarray(L0_attn_gamma),
                                       np.asarray(L0_attn_beta)]).T),
        "W_o": asc(L0_attn_W_o), "b_o": asc(L0_attn_b_o),
        "wqkv": asc(np.concatenate([np.asarray(L0_ffn_wq), np.asarray(L0_ffn_wk), np.asarray(L0_ffn_wv)]).T),
        "wo": asc(np.asarray(L0_ffn_wo).T), "ln1_w": asc(np.asarray(L0_ffn_ln1_w).reshape(C, 1)),
        "ident": np.eye(P, dtype=np.float32),
        "router": asc(np.asarray(L0_ffn_router_w).T), "ln2_w": asc(np.asarray(L0_ffn_ln2_w).reshape(C, 1)),
        "w1": asc(np.asarray(L0_ffn_w1).reshape(HIDDEN, C).T), "w3": asc(np.asarray(L0_ffn_w3).reshape(HIDDEN, C).T),
        "w2": down_blocks(np.asarray(L0_ffn_w2)),
        **shape_constants(),
    }
    nc = bacc.Bacc("TRN2", target_bir_lowering=False, num_devices=1)
    d = {name: nc.dram_tensor(name, a.shape, mybir.dt.from_np(a.dtype), kind="ExternalInput").ap()
         for name, a in arrays.items()}
    out = nc.dram_tensor(_OUT[0], _OUT[1], F32, kind="ExternalOutput").ap()
    program(nc, d, out)
    r = run(nc, [arrays], core_ids=[0])
    return r.results[0]["out"]
```
